# Optimizing a Trainium2 kernel written in Bass

```python
import numpy as np
import jax
import jax.numpy as jnp

def _softmax(x, axis=-1):
    return jax.nn.softmax(x, axis=axis)

def _gelu(x):
    return jax.nn.gelu(x, approximate=True)

def _silu(x):
    return jax.nn.silu(x)

def _sigmoid(x):
    return jax.nn.sigmoid(x)

def _layernorm(x, axis=-1, eps=1e-05):
    m = jnp.mean(x, axis=axis, keepdims=True)
    v = jnp.var(x, axis=axis, keepdims=True)
    return (x - m) / jnp.sqrt(v + eps)

def _scatter_add(tgt, idx, src, axis=0):
    return tgt.at[idx].add(src)

def _segment_sum(src, seg, n):
    return jax.ops.segment_sum(src, seg, n)
kernel_name = 'mk_decoder_preln_d2_seqx_r8_5a0f66'

def setup_inputs(seed: int=0):
    np.random.seed(seed)
    _w = jnp.asarray

    def _rec_inputs():
        import jax
        import jax.numpy as jnp
        _rk = jax.random.key(seed)
        x = -0.0002928 + 1 * jax.random.normal(jax.random.fold_in(_rk, 1), (32, 128, 128), jnp.float32)
        _lenS = 128 - jax.random.randint(jax.random.fold_in(_rk, 7), (32,), 0, max(1, 128 // 4) + 1, jnp.int32)
        _lenS2 = 128 - jax.random.randint(jax.random.fold_in(_rk, 8), (32,), 0, max(1, 128 // 4) + 1, jnp.int32)
        _ctx_1024P = jax.random.normal(jax.random.fold_in(_rk, 11), (32, 16, 128), jnp.float32)
        _ctx_1024c = jax.random.dirichlet(jax.random.fold_in(_rk, 511), 0.3 * jnp.ones((16,), jnp.float32), (32, 128))
        _ctx_1024t = jnp.einsum('bsk,bkd->bsd', _ctx_1024c, _ctx_1024P)
        _ctx_1024t = _ctx_1024t * jax.lax.rsqrt(jnp.mean(jnp.square(_ctx_1024t)) + 1e-12) * 0.953939
        ctx_1024 = -1.39393e-06 + 0.999914 * (_ctx_1024t + 0.3 * jax.random.normal(jax.random.fold_in(_rk, 611), (32, 128, 128), jnp.float32))
        _validS = jnp.arange(128)[None, :] < _lenS[:, None]
        _validS2 = jnp.arange(128)[None, :] < _lenS2[:, None]
        _causal = jnp.tril(jnp.ones((128, 128), dtype=bool))
        mask_BxS2_ik0 = jnp.where(jnp.broadcast_to(_validS2[:, :], (32, 128)), 0, 1).astype(jnp.int32)
        return (x, ctx_1024, mask_BxS2_ik0)
    x, ctx_1024, mask_BxS2_ik0 = _rec_inputs()

    def _L0_attn_setup():
        import jax, jax.numpy as jnp
        import numpy as np
        EPS = float(np.finfo(np.float32).eps)
        SEQ_LEN = 256
        NUM_HEADS = 16
        DIM_EMB = 128
        DIM_HEAD = DIM_EMB // NUM_HEADS
        DIM_K = DIM_EMB
        BATCH = 2

        def cosine_positional_encoding(seq_len, dim):
            idx = jnp.arange(seq_len, dtype=jnp.float32)
            scale = 1.0 / (10000.0 ** (jnp.arange(0, dim, 2, dtype=jnp.float32) / dim) + EPS)
            ang = idx[:, None] * scale[None, :]
            return jnp.stack([jnp.sin(ang), jnp.cos(ang)], axis=-1).reshape(seq_len, dim)
        key = jax.random.key(seed)
        ks = jax.random.split(key, 5)
        s = DIM_EMB ** (-0.5)
        return {'x': jax.random.normal(ks[0], (BATCH, SEQ_LEN, DIM_EMB), dtype=jnp.float32), 'Wq': jax.random.normal(ks[1], (DIM_EMB, DIM_EMB), dtype=jnp.float32) * s, 'Wk': jax.random.normal(ks[2], (DIM_EMB, DIM_EMB), dtype=jnp.float32) * s, 'Wv': jax.random.normal(ks[3], (DIM_EMB, DIM_EMB), dtype=jnp.float32) * s, 'Wo': jax.random.normal(ks[4], (DIM_EMB, DIM_EMB), dtype=jnp.float32) * s}
    _L0_attn_all = _L0_attn_setup()
    _L0_attn_in = {k: v for k, v in _L0_attn_all.items() if k in ('Wq', 'Wk', 'Wv', 'Wo')}
    del _L0_attn_all

    def _L0_xattn_setup():
        import jax, jax.numpy as jnp
        import numpy as np
        import math
        N_HEAD = 16
        key = jax.random.key(seed)
        ks = jax.random.split(key, 9)
        B, T, D = (2, 256, 128)
        s = 1.0 / math.sqrt(D)
        return {'queries': jax.random.normal(ks[0], (B, T, D), jnp.float32), 'keys': jax.random.normal(ks[1], (B, T, D), jnp.float32), 'key_mask': jax.random.randint(ks[2], (B, T), 0, 2, jnp.int32), 'Wq': jax.random.normal(ks[3], (D, D), jnp.float32) * s, 'bq': jax.random.normal(ks[4], (D,), jnp.float32) * 0.01, 'Wk': jax.random.normal(ks[5], (D, D), jnp.float32) * s, 'bk': jax.random.normal(ks[6], (D,), jnp.float32) * 0.01, 'Wv': jax.random.normal(ks[7], (D, D), jnp.float32) * s, 'bv': jax.random.normal(ks[8], (D,), jnp.float32) * 0.01}
    _L0_xattn_all = _L0_xattn_setup()
    _L0_xattn_in = {k: v for k, v in _L0_xattn_all.items() if k in ('Wq', 'bq', 'Wk', 'bk', 'Wv', 'bv')}
    del _L0_xattn_all

    def _L0_ffn_setup():
        import jax, jax.numpy as jnp
        import numpy as np
        E = 8
        K = 2
        CAPACITY_FACTOR = 1.25
        key = jax.random.key(seed)
        ks = jax.random.split(key, 4)
        B, T, C, H = (8, 256, 128, 512)
        x = jax.random.normal(ks[0], (B, T, C), jnp.float32)
        Wr = jax.random.normal(ks[1], (C, E), jnp.float32) * 0.02
        br = jnp.zeros((E,), jnp.float32)
        W1 = jax.random.normal(ks[2], (E, C, H), jnp.float32) * 0.02
        b1 = jnp.zeros((E, H), jnp.float32)
        W2 = jax.random.normal(ks[3], (E, H, C), jnp.float32) * 0.02
        b2 = jnp.zeros((E, C), jnp.float32)
        return {'x': x, 'Wr': Wr, 'br': br, 'W1': W1, 'b1': b1, 'W2': W2, 'b2': b2}
    _L0_ffn_all = _L0_ffn_setup()
    _L0_ffn_in = {k: v for k, v in _L0_ffn_all.items() if k in ('Wr', 'br', 'W1', 'b1', 'W2', 'b2')}
    del _L0_ffn_all

    def _L1_attn_setup():
        import jax, jax.numpy as jnp
        import numpy as np
        SEQ, BATCH, DIM = (256, 8, 128)
        key = jax.random.key(seed)
        k1, k2, k3 = jax.random.split(key, 3)
        x = jax.random.normal(k1, (SEQ, BATCH, DIM), dtype=jnp.float32)
        Wq = jax.random.normal(k2, (DIM, DIM), dtype=jnp.float32) * DIM ** (-0.5)
        Wk = jax.random.normal(k3, (DIM, DIM), dtype=jnp.float32) * DIM ** (-0.5)
        return {'x': x, 'Wq': Wq, 'Wk': Wk}
    _L1_attn_all = _L1_attn_setup()
    _L1_attn_in = {k: v for k, v in _L1_attn_all.items() if k in ('Wq', 'Wk')}
    del _L1_attn_all

    def _L1_xattn_setup():
        import jax, jax.numpy as jnp
        import numpy as np
        EMB = 128
        key = jax.random.key(seed)
        k1, k2, k3, k4, k5 = jax.random.split(key, 5)
        batch = jax.random.normal(k1, (8, 512, EMB), dtype=jnp.float32)
        latent = jax.random.normal(k2, (8, 128, EMB), dtype=jnp.float32)
        s = 1.0 / np.sqrt(EMB)
        Wk = jax.random.normal(k3, (EMB, EMB), dtype=jnp.float32) * s
        Wq = jax.random.normal(k4, (EMB, EMB), dtype=jnp.float32) * s
        Wv = jax.random.normal(k5, (EMB, EMB), dtype=jnp.float32) * s
        return {'batch': batch, 'latent': latent, 'Wk': Wk, 'Wq': Wq, 'Wv': Wv}
    _L1_xattn_all = _L1_xattn_setup()
    _L1_xattn_in = {k: v for k, v in _L1_xattn_all.items() if k in ('Wk', 'Wq', 'Wv')}
    del _L1_xattn_all

    def _L1_ffn_setup():
        import jax, jax.numpy as jnp
        import numpy as np
        S, B, D, E, C, FF = (256, 4, 128, 8, 256, 512)
        N = S * B
        key = jax.random.key(seed)
        ks = jax.random.split(key, 7)
        return {'hidden_states': jax.random.normal(ks[0], (S, B, D), dtype=jnp.float32), 'combine_weights': jax.random.uniform(ks[1], (N, E), dtype=jnp.float32), 'top_idx': jax.random.randint(ks[2], (C, E), 0, N, dtype=jnp.int64), 'W1': jax.random.normal(ks[3], (E, D, FF), dtype=jnp.float32) * (1.0 / np.sqrt(D)), 'b1': jnp.zeros((E, FF), dtype=jnp.float32), 'W2': jax.random.normal(ks[4], (E, FF, D), dtype=jnp.float32) * (1.0 / np.sqrt(FF)), 'b2': jnp.zeros((E, D), dtype=jnp.float32)}
    _L1_ffn_all = _L1_ffn_setup()
    _L1_ffn_in = {k: v for k, v in _L1_ffn_all.items() if k in ('combine_weights', 'top_idx', 'W1', 'b1', 'W2', 'b2')}
    del _L1_ffn_all
    return {'x': x, 'ctx_1024': ctx_1024, 'mask_BxS2_ik0': mask_BxS2_ik0, 'L0_attn_Wq': _L0_attn_in['Wq'], 'L0_attn_Wk': _L0_attn_in['Wk'], 'L0_attn_Wv': _L0_attn_in['Wv'], 'L0_attn_Wo': _L0_attn_in['Wo'], 'L0_xattn_Wq': _L0_xattn_in['Wq'], 'L0_xattn_bq': _L0_xattn_in['bq'], 'L0_xattn_Wk': _L0_xattn_in['Wk'], 'L0_xattn_bk': _L0_xattn_in['bk'], 'L0_xattn_Wv': _L0_xattn_in['Wv'], 'L0_xattn_bv': _L0_xattn_in['bv'], 'L0_ffn_Wr': _L0_ffn_in['Wr'], 'L0_ffn_br': _L0_ffn_in['br'], 'L0_ffn_W1': _L0_ffn_in['W1'], 'L0_ffn_b1': _L0_ffn_in['b1'], 'L0_ffn_W2': _L0_ffn_in['W2'], 'L0_ffn_b2': _L0_ffn_in['b2'], 'L1_attn_Wq': _L1_attn_in['Wq'], 'L1_attn_Wk': _L1_attn_in['Wk'], 'L1_xattn_Wk': _L1_xattn_in['Wk'], 'L1_xattn_Wq': _L1_xattn_in['Wq'], 'L1_xattn_Wv': _L1_xattn_in['Wv'], 'L1_ffn_combine_weights': _L1_ffn_in['combine_weights'], 'L1_ffn_top_idx': _L1_ffn_in['top_idx'], 'L1_ffn_W1': _L1_ffn_in['W1'], 'L1_ffn_b1': _L1_ffn_in['b1'], 'L1_ffn_W2': _L1_ffn_in['W2'], 'L1_ffn_b2': _L1_ffn_in['b2']}

def reference(x, ctx_1024, mask_BxS2_ik0, L0_attn_Wq, L0_attn_Wk, L0_attn_Wv, L0_attn_Wo, L0_xattn_Wq, L0_xattn_bq, L0_xattn_Wk, L0_xattn_bk, L0_xattn_Wv, L0_xattn_bv, L0_ffn_Wr, L0_ffn_br, L0_ffn_W1, L0_ffn_b1, L0_ffn_W2, L0_ffn_b2, L1_attn_Wq, L1_attn_Wk, L1_xattn_Wk, L1_xattn_Wq, L1_xattn_Wv, L1_ffn_combine_weights, L1_ffn_top_idx, L1_ffn_W1, L1_ffn_b1, L1_ffn_W2, L1_ffn_b2):
    import jax
    import jax.numpy as jnp

    def _L0_attn_ref(x, Wq, Wk, Wv, Wo):
        import jax, jax.numpy as jnp
        import numpy as np
        EPS = float(np.finfo(np.float32).eps)
        SEQ_LEN = 256
        NUM_HEADS = 16
        DIM_EMB = 128
        DIM_HEAD = DIM_EMB // NUM_HEADS
        DIM_K = DIM_EMB
        BATCH = 2

        def cosine_positional_encoding(seq_len, dim):
            idx = jnp.arange(seq_len, dtype=jnp.float32)
            scale = 1.0 / (10000.0 ** (jnp.arange(0, dim, 2, dtype=jnp.float32) / dim) + EPS)
            ang = idx[:, None] * scale[None, :]
            return jnp.stack([jnp.sin(ang), jnp.cos(ang)], axis=-1).reshape(seq_len, dim)
        B, S, E = x.shape
        pos = cosine_positional_encoding(S, DIM_HEAD)

        def split_heads(t):
            return t.reshape(B, S, NUM_HEADS, DIM_HEAD).transpose(0, 2, 1, 3)
        q = split_heads(x @ Wq) + pos[None, None]
        k = split_heads(x @ Wk) + pos[None, None]
        v = split_heads(x @ Wv)
        scores = jnp.einsum('bhqd,bhkd->bhqk', q, k) * DIM_K ** (-0.5)
        causal_mask = jnp.triu(jnp.ones((S, S), dtype=bool), k=1)
        m_inf = -jnp.finfo(scores.dtype).max
        scores = jnp.where(causal_mask[None, None], m_inf, scores)
        attn = jax.nn.softmax(scores, axis=-1)
        out = jnp.einsum('bhqk,bhkd->bhqd', attn, v)
        out = out.transpose(0, 2, 1, 3).reshape(B, S, E)
        return out @ Wo

    def _L0_xattn_ref(queries, keys, key_mask, Wq, bq, Wk, bk, Wv, bv):
        import jax, jax.numpy as jnp
        import numpy as np
        import math
        N_HEAD = 16
        B, Tq, D = queries.shape
        Tk = keys.shape[1]
        H = N_HEAD
        dk = D // H
        scale = 1.0 / math.sqrt(dk)
        Q = (queries @ Wq.T + bq).reshape(B, Tq, H, dk)
        K = (keys @ Wk.T + bk).reshape(B, Tk, H, dk)
        V = (keys @ Wv.T + bv).reshape(B, Tk, H, dk)
        Qf = Q.transpose(0, 2, 1, 3).reshape(B * H, Tq, dk)
        Kf = K.transpose(0, 2, 1, 3).reshape(B * H, Tk, dk)
        Vf = V.transpose(0, 2, 1, 3).reshape(B * H, Tk, dk)
        scores = jnp.einsum('nqd,nkd->nqk', Qf, Kf) * scale
        km = jnp.tile(key_mask, (H, 1))
        scores = jnp.where(km[:, None, :] == 0, -1000000000.0, scores)
        attn = jax.nn.softmax(scores, axis=-1)
        qm = jnp.tile(key_mask, (H, 1))[:, :, None].astype(attn.dtype)
        attn = attn * qm
        out = jnp.einsum('nqk,nkd->nqd', attn, Vf)
        out = out.reshape(B, H, Tq, dk).transpose(0, 2, 1, 3).reshape(B, Tq, D)
        return out

    def _L0_ffn_ref(x, Wr, br, W1, b1, W2, b2):
        import jax, jax.numpy as jnp
        import numpy as np
        E = 8
        K = 2
        CAPACITY_FACTOR = 1.25
        B, T, C = x.shape
        cap = max(1, int(T / E * CAPACITY_FACTOR))
        probs = jax.nn.softmax(x @ Wr + br, axis=-1)
        topk_p, topk_e = jax.lax.top_k(probs, K)
        e_flat = topk_e.reshape(B, T * K)
        p_flat = topk_p.reshape(B, T * K)
        oh = jax.nn.one_hot(e_flat, E, dtype=jnp.int32)
        pos_all = jnp.cumsum(oh, axis=1) - oh
        pos = jnp.take_along_axis(pos_all, e_flat[:, :, None], axis=2)[:, :, 0]
        keep = pos < cap
        b_idx = jnp.arange(B)[:, None]
        flat_idx = (e_flat * B + b_idx) * cap + jnp.minimum(pos, cap - 1)
        x_rep = jnp.broadcast_to(x[:, :, None, :], (B, T, K, C)).reshape(B, T * K, C)
        buf = jnp.zeros((E * B * cap, C), x.dtype).at[flat_idx.reshape(-1)].add((x_rep * keep[:, :, None].astype(x.dtype)).reshape(-1, C))
        buf = buf.reshape(E, B * cap, C)
        h = jax.nn.relu(jnp.einsum('enc,ech->enh', buf, W1) + b1[:, None, :])
        y = jnp.einsum('enh,ehc->enc', h, W2) + b2[:, None, :]
        y_tok = y.reshape(E * B * cap, C)[flat_idx.reshape(-1)].reshape(B, T * K, C)
        y_tok = y_tok * (p_flat * keep.astype(x.dtype))[:, :, None]
        return y_tok.reshape(B, T, K, C).sum(axis=2)

    def _L1_attn_ref(x, Wq, Wk):
        import jax, jax.numpy as jnp
        import numpy as np
        SEQ, BATCH, DIM = (256, 8, 128)
        q = jnp.einsum('sbd,ed->sbe', x, Wq)
        k = jnp.einsum('sbd,ed->sbe', x, Wk)
        scale = jnp.asarray(x.shape[2], x.dtype) ** 0.5
        scores = jnp.einsum('sbd,tbd->bst', q, k) / scale
        align = jax.nn.softmax(jnp.tanh(scores), axis=2)
        out = jnp.einsum('bst,tbd->sbd', align, x)
        return out

    def _L1_xattn_ref(batch, latent, Wk, Wq, Wv):
        import jax, jax.numpy as jnp
        import numpy as np
        EMB = 128
        keys = jnp.einsum('bpe,fe->bpf', batch, Wk)
        queries = jnp.einsum('ble,fe->blf', latent, Wq)
        values = jnp.einsum('bpe,fe->bpf', batch, Wv)
        scale = 1.0 / jnp.sqrt(jnp.asarray(batch.shape[-1], dtype=batch.dtype))
        weights = jnp.einsum('ble,bpe->blp', queries, keys) * scale
        weights = jax.nn.softmax(weights, axis=-1)
        attention = jnp.einsum('blp,bpe->ble', weights, values)
        return attention

    def _L1_ffn_ref(hidden_states, combine_weights, top_idx, W1, b1, W2, b2):
        import jax, jax.numpy as jnp
        import numpy as np
        S, B, D, E, C, FF = (256, 4, 128, 8, 256, 512)
        N = S * B
        s, b, d = hidden_states.shape
        x = hidden_states.reshape(-1, d)
        tok = top_idx.T
        gathered = x[tok]
        h = jax.nn.gelu(jnp.einsum('ecd,edf->ecf', gathered, W1) + b1[:, None, :])
        out_e = jnp.einsum('ecf,efd->ecd', h, W2) + b2[:, None, :]
        e_ids = jnp.arange(tok.shape[0])[:, None]
        w = combine_weights[tok, e_ids]
        weighted = (out_e * w[..., None]).reshape(-1, d)
        out = jnp.zeros_like(x).at[tok.reshape(-1)].add(weighted)
        return out.reshape(s, b, d)
    x = x + _L0_attn_ref(_layernorm(x, axis=-1), L0_attn_Wq, L0_attn_Wk, L0_attn_Wv, L0_attn_Wo)
    x = x + _L0_xattn_ref(_layernorm(x, axis=-1), ctx_1024, mask_BxS2_ik0, L0_xattn_Wq, L0_xattn_bq, L0_xattn_Wk, L0_xattn_bk, L0_xattn_Wv, L0_xattn_bv)
    x = x + _L0_ffn_ref(_layernorm(x, axis=-1), L0_ffn_Wr, L0_ffn_br, L0_ffn_W1, L0_ffn_b1, L0_ffn_W2, L0_ffn_b2)
    x = x + _L1_attn_ref(_layernorm(x, axis=-1), L1_attn_Wq, L1_attn_Wk)
    x = x + _L1_xattn_ref(ctx_1024, _layernorm(x, axis=-1), L1_xattn_Wk, L1_xattn_Wq, L1_xattn_Wv)
    x = x + _L1_ffn_ref(_layernorm(x, axis=-1), L1_ffn_combine_weights, L1_ffn_top_idx, L1_ffn_W1, L1_ffn_b1, L1_ffn_W2, L1_ffn_b2)
    return x

_drawn_inputs = setup_inputs


def setup_inputs(seed=0):
    import zlib

    import numpy as np

    out = dict(_drawn_inputs(seed))
    spreads = {'L0_ffn_br': (0.0, 0.395),
     'L0_ffn_b1': (0.0, 0.8),
     'L0_ffn_b2': (0.0, 0.459),
     'L1_ffn_b1': (0.0, 0.324),
     'L1_ffn_b2': (0.0, 0.1)}
    factors = {'L0_xattn_bq': 31.259,
     'L0_xattn_bk': 64.0,
     'L0_xattn_bv': 8.0,
     'L0_ffn_Wr': 3.582,
     'L0_ffn_W1': 6.31,
     'L0_ffn_W2': 4.473}
    for name, (base, spread) in spreads.items():
        noise = np.random.default_rng([zlib.crc32(name.encode()), seed]).standard_normal(out[name].shape)
        drawn = base * np.exp(spread * noise) if base else spread * noise
        out[name] = jnp.asarray(drawn.astype(out[name].dtype))
    for name, factor in factors.items():
        out[name] = (out[name] * factor).astype(out[name].dtype)
    return out
```

```python
import numpy as np

import concourse.bass as bass
from concourse import mybir
from contextlib import ExitStack

F32 = mybir.dt.float32
BF16 = mybir.dt.bfloat16
I32 = mybir.dt.int32
U32 = mybir.dt.uint32
ACT = mybir.ActivationFunctionType
ALU = mybir.AluOpType
AX = mybir.AxisListType

B, T, C = 32, 128, 128
G = 4
NG = B // G
H, DH = 16, 8
HB = 4
NBLK = H // HB
GT = G * T
EPS = 1e-5
CAUSAL_BIG = -1e30
NEG = -1e9 * DH ** 0.5



class Lin:

    def __init__(self, i, k, c):
        self.i, self.k, self.c = i, k, c

    def __add__(self, n):
        return Lin(self.i, self.k, self.c + n)

    def __sub__(self, n):
        return self + -n

    def __mul__(self, n):
        return Lin(self.i, self.k * n, self.c * n)

    __rmul__, __radd__ = __mul__, __add__

    def value(self):
        return self.i * self.k + self.c


def at(n):
    return bass.ds(n.value(), 1) if isinstance(n, Lin) else n


class Signal:

    def __init__(self, sem, free=0):
        self.sem, self.free = sem, free

    def credit(self, eng):
        eng.sem_inc(self.sem, self.free)

    def at(self, n):
        if isinstance(n, Lin):
            n = n + self.free
            assert n.c >= 1, (n.k, n.c)
            return n.value()
        return n + self.free if n > 0 else 0


def clear(nc, used):
    def end(error, *_):
        if error is None:
            with nc.Block() as block:
                @block.gpsimd
                def _(pool):
                    first = None
                    for n in sorted(used):
                        first = n if first is None else first
                        if n + 1 not in used:
                            pool.sem_clear(range(first, n + 1))
                            first = None
    return end


class Tally:

    def __init__(self, sem):
        self.sem, self.n, self.i, self.per = sem, 0, None, 0

    def one(self):
        self.n += 1
        return 1

    def value(self):
        return self.n if self.i is None else self.i * self.per + self.n

    def enter(self, i, per):
        self.start, self.i, self.per = self.n, i, per

    def leave(self, times):
        assert self.n - self.start == self.per, (self.n - self.start, self.per)
        self.n, self.i = self.start + times * self.per, None


def head_attention(nc, kind, X, io, consts, first):
    own = kind == "self"
    p = "a_" if own else "c_"
    ROWS = 6 * DH
    KS = ROWS if own else ROWS + 1
    MROW = KS
    KT = KS + 1
    SCALE = C ** -0.5 if own else DH ** -0.5
    ident, identb, passed = consts["ident"], consts["identb"], consts["passed"]
    Q_PARTS = [0, 0, 0, 1, 1, 2]
    K_RUNS = [(0, 3), (3, 2), (5, 1)]

    used = []
    with ExitStack() as ctx:
        ctx.push(clear(nc, used))

        def sb(name, shape, dt):
            return ctx.enter_context(nc.sbuf_tensor(p + name, shape, dt))

        def ps(name, shape, dt=F32):
            return ctx.enter_context(nc.psum_tensor(p + name, shape, dt))

        def sem(name):
            s = ctx.enter_context(nc.semaphore(p + name))
            used.append(s.num)
            return s

        def signal(name, free=0):
            return Signal(sem(name), free)

        wq, wk, wv = (sb(n, [128, 128], F32) for n in ("wq", "wk", "wv"))
        wo = sb("wo", [128, 128], F32) if own else None
        pos = sb("pos", [128, GT], F32) if own else None
        causal = sb("causal", [128, 128], F32) if own else None
        cmask = sb("cmask", [128, HB, 128], BF16) if own else None
        if not own:
            bqk = sb("bqk", [128, 2], F32)
            bv = sb("bv", [128, 128], F32)
            kmi = sb("kmi", [128, 2, 128], I32)
            km = sb("km", [128, G, 128], F32)
            kmf = sb("kmf", [128, 2, 128], F32)
            negrow = sb("negrow", [H, 2, 128], BF16)
            qmi = sb("qmi", [128, 32], I32)
            qm = sb("qm", [128, 32], F32)
            ctxT = sb("ctxT", [128, 2, GT], F32)
        ones = sb("ones", [H, GT], BF16)
        stats = sb("stats", [128, G, 6], F32)
        mv = sb("mv", [128, G, 2], F32)
        veps = sb("veps", [128, G], F32)
        half_neg = sb("half_neg", [128, G], F32)
        rstd = sb("rstd", [128, G], F32)
        hn = sb("hn", [128, G, 128], F32)
        hT = sb("hT", [128, GT], F32)
        full = [sb(n, [128, GT], F32) for n in ("qf", "kf")]
        parts = [sb(n, [128, 3, GT], BF16) for n in ("qp", "kp")]
        stack = [sb(n, [64, 2, H, GT], BF16) for n in ("qs", "ks")]
        Qs, Ks = stack
        vaug = sb("vaug", [128, 2, G, H, DH + 1], F32)
        mx = sb("mx", [128, 2, H], F32)
        negm = sb("negm", [H, 2, 128], BF16)
        PT = sb("PT", [128, NBLK, HB, 128], F32)
        rden = sb("rden", [128, 2, H], F32)
        O = sb("O", [128, H, DH], F32)
        oT = sb("oT", [128, 128], F32) if own else None

        psS = [ps(f"psS{n}", [128, HB, 128]) for n in range(2)]
        psT = [ps(f"psT{n}", [128, HB, 128]) for n in range(2)]
        psO = ps("psO", [128, 512])
        psH = ps("psH", [128, 512])
        psP = ps("psP", [128, 512])
        psM = ps("psM", [128, 512])
        outs = psO[:, 0:H * (DH + 1)].rearrange("p (h d) -> p h d", d=DH + 1)

        s_w = sem("weights")
        s_x = [sem(f"x{n}") for n in range(2)]
        s_ctx = [signal(f"ctx{n}") for n in range(2)]
        s_cst = sem("constants")
        s_ones = sem("ones")
        s_neg = sem("masked_rows")
        s_rows = sem("fixed_rows")
        ln_done = signal("ln_done")
        stats_ready = signal("stats_ready")
        rstd_ready = signal("rstd_ready")
        transposed = signal("transposed")
        hT_ready = signal("hT_ready")
        q_done = signal("q_projected")
        k_done = signal("k_projected")
        v_done = signal("v_projected")
        v_ready = signal("v_ready")
        taken = signal("taken")
        hi_ready = signal("hi_ready")
        rest_ready = signal("rest_ready")
        mid_ready = signal("mid_ready")
        lo_ready = signal("lo_ready")
        hi_spilled = [signal(f"hi_spilled{n}") for n in range(2)]
        lo_spilled = [signal(f"lo_spilled{n}") for n in range(2)]
        stacked = [signal(f"stacked{n}") for n in range(2)]
        scored = signal("scored")
        maxed = signal("maxed")
        max_turned = signal("max_turned")
        minus_ready = signal("minus_ready")
        row_placed = [signal(f"row_placed{n}") for n in range(2)]
        scored_t = signal("scored_t", 1)
        exp_done = signal("exp_done", 2)
        selected = signal("selected")
        weighed = signal("weighed", 4)
        normed = signal("normed", 1)
        out_turned = signal("out_turned", 1)
        out_copied = signal("out_copied", 1)
        out_projected = signal("out_projected", 1)
        added = signal("added", 1)
        probs_ready = selected if own else exp_done
        own_pool = signal("own_pool")
        own_dve = Tally(sem("own_dve"))

        NW = 5
        NSTACK = (len(Q_PARTS) + len(K_RUNS)) * 16

        def body(step, i):
            last = isinstance(i, int)
            for gp in range(2):
                g = 2 * i + gp if last else Lin(i, 2, gp)
                for r in range(G):
                    left = B - 1 - (G * g + r) if last else B
                    step(g, gp, r, left)

        def pairs(eng, step, tally=None, per=0):
            with eng.Fori(0, NG // 2 - 1) as i:
                if tally:
                    tally.enter(i, per)
                body(step, i)
            if tally:
                tally.leave(NG // 2 - 1)
            body(step, NG // 2 - 1)

        def pair(g, gp, more):
            n = (gp + more) // 2
            return Lin(g.i, 1, n) if isinstance(g, Lin) else (g - gp) // 2 + n

        def half(g, gp, r, more=0):
            n = 2 * gp + (r + more) // 2
            return Lin(g.i, 4, n) if isinstance(g, Lin) else 4 * ((g - gp) // 2) + n

        block = ctx.enter_context(nc.Block())

        @block.sync
        def _(sp):
            if first:
                xt = io["x"].rearrange("b t c -> t b c")
                sp.dma_start(X[:, 0:2 * G, :], xt[:, 0:2 * G, :]).then_inc(s_x[0], 16)
            sp.dma_start(wq[:, :], io[p + "wq"]).then_inc(s_w, 16)
            sp.dma_start(wk[:, :], io[p + "wk"]).then_inc(s_w, 16)
            sp.dma_start(wv[:, :], io[p + "wv"]).then_inc(s_w, 16)
            if own:
                sp.dma_start(pos[:, :], io["pos"]).then_inc(s_w, 16)
                sp.dma_start(wo[:, :], io[p + "wo"]).then_inc(s_w, 16)
                sp.dma_start(causal[:, :], io["causal"]).then_inc(s_cst, 16)
            else:
                for n in range(2):
                    sp.dma_start(ctxT[:, n, :], io["ctxT"][:, n * GT:(n + 1) * GT]).then_inc(s_ctx[n].sem, 16)
                sp.dma_start(bqk[:, :], io["bqk"]).then_inc(s_w, 16)
                sp.dma_start(bv[:, :], io["bv"].partition_broadcast(128)).then_inc(s_w, 16)
                for d in range(DH):
                    sp.dma_start(kmi[H * d:H * d + H, :, :],
                                 io["mask"].rearrange("(a h) t -> h a t", h=H)).then_inc(s_cst, 16)
                sp.dma_start(qmi[:, :], io["maskT"]).then_inc(s_cst, 16)
            if first:
                sp.dma_start(X[:, 2 * G:B, :], xt[:, 2 * G:B, :]).then_inc(s_x[1], 16)
            sp.wait_ge(s_ones, 1)
            for n in range(2):
                sp.dma_start(Ks[MROW:MROW + 1, n, :, :], ones[:, :]).then_inc(s_rows, 16)
                if not own:
                    sp.dma_start(Qs[ROWS:ROWS + 1, n, :, :], ones[:, :]).then_inc(s_rows, 16)
            if not own:
                sp.wait_ge(s_neg, 1)
                for n in range(2):
                    for r in range(G):
                        sp.dma_start(Ks[ROWS:ROWS + 1, n, :, r * T:(r + 1) * T],
                                     negrow[:, r % 2, :]).then_inc(s_rows, 16)

            def spill_hi(g, gp):
                for n in range(2):
                    sp.wait_ge(hi_ready.sem, hi_ready.at(2 * g + n + 1))
                    sp.sem_inc(passed, 1)
                    sp.dma_start(io["spill"][gp, n, 0], parts[n][:, 0, :]).then_inc(hi_spilled[gp].sem, 16)

            def spill_rest(g, gp):
                for n in range(2):
                    sp.wait_ge(lo_ready.sem, lo_ready.at(2 * g + n + 1))
                    sp.sem_inc(passed, 1)
                    sp.dma_start(io["spill"][gp, n, 1:3].rearrange("a p t -> p a t"),
                                 parts[n][:, 1:3, :]).then_inc(lo_spilled[gp].sem, 16)

            def fill(g, gp, nth):
                sp.wait_ge(hi_spilled[gp].sem, hi_spilled[gp].at(32 * nth + 32))
                sp.sem_inc(passed, 1)
                sp.wait_ge(lo_spilled[gp].sem, lo_spilled[gp].at(32 * nth + 32))
                sp.sem_inc(passed, 1)
                sp.wait_ge(scored_t.sem, scored_t.at(NBLK * G * (g - 1)))
                sp.sem_inc(passed, 1)
                for row, part in enumerate(Q_PARTS):
                    src = io["spill"][gp, 0, part].rearrange("(d h) t -> d (h t)", h=H)
                    sp.dma_start(Qs[DH * row:DH * row + DH, gp, :, :], src).then_inc(stacked[gp].sem, 16)
                for row, count in K_RUNS:
                    src = io["spill"][gp, 1, 0:count].rearrange("a (d h) t -> (a d) (h t)", h=H)
                    sp.dma_start(Ks[DH * row:DH * (row + count), gp, :, :], src).then_inc(stacked[gp].sem, 16)

            def place_row(b, gp, r):
                sp.wait_ge(minus_ready.sem, minus_ready.at(b + 1))
                sp.sem_inc(passed, 1)
                sp.dma_start(Qs[MROW:MROW + 1, gp, :, r * T:(r + 1) * T],
                             negm[:, r % 2, :]).then_inc(row_placed[r % 2].sem, 16)

            def step(g, gp, r, left):
                b = G * g + r
                if r == 0 and left >= G:
                    spill_rest(g + 1, 1 - gp)
                    fill(g + 1, 1 - gp, pair(g, gp, 1))
                if left >= 2:
                    if r < 2:
                        place_row(b + 2, gp, r + 2)
                    else:
                        place_row(b + 2, 1 - gp, r - 2)
                if r == 3 and left >= 2 * G - r:
                    spill_hi(g + 2, gp)
                if not own and r == 0 and left >= 2 * G:
                    sp.wait_ge(v_done.sem, v_done.at(g + 1))
                    sp.sem_inc(passed, 1)
                    lo = (g + 2) * GT
                    src = io["ctxT"][:, bass.ds(lo.value(), GT)] if isinstance(lo, Lin) else io["ctxT"][:, lo:lo + GT]
                    sp.dma_start(ctxT[:, gp, :], src).then_inc(s_ctx[gp].sem, 16)

            spill_hi(0, 0)
            spill_rest(0, 0)
            fill(0, 0, 0)
            spill_hi(1, 1)
            place_row(0, 0, 0)
            place_row(1, 0, 1)
            pairs(nc.sync, step)

        @block.tensor
        def _(pe):
            def prep_transpose(g):
                pe.wait_ge(ln_done.sem, ln_done.at(g + 1))
                pe.wait_ge(v_ready.sem, v_ready.at(g))
                for r in range(G):
                    ins = nc.tensor.transpose(psH[:, r * 128:(r + 1) * 128], hn[:, r, :], ident[:, :])
                ins.then_inc(transposed.sem, 1)

            def prep_q(g):
                pe.wait_ge(hT_ready.sem, hT_ready.at(g + 1))
                pe.wait_ge(taken.sem, taken.at(2 * g))
                nc.tensor.matmul(psP[:, :], wq[:, :], hT[:, :], start=True, stop=True).then_inc(q_done.sem, 1)

            def prep_k(g, gp, nth):
                if not own:
                    pe.wait_ge(s_ctx[gp].sem, s_ctx[gp].at(16 * nth + 16))
                pe.wait_ge(taken.sem, taken.at(2 * g + 1))
                nc.tensor.matmul(psP[:, :], wk[:, :], hT[:, :] if own else ctxT[:, gp, :],
                                 start=True, stop=True).then_inc(k_done.sem, 1)

            def prep_v(g, gp):
                for r in range(G):
                    src = hT[:, r * T:(r + 1) * T] if own else ctxT[:, gp, r * T:(r + 1) * T]
                    ins = nc.tensor.matmul(psH[:, r * 128:(r + 1) * 128], src, wv[:, :], start=True, stop=True)
                ins.then_inc(v_done.sem, 1)

            def scores(b, gp, r, j):
                pe.wait_ge(maxed.sem, maxed.at(NBLK * b + j - 1))
                out = psS[j % 2]
                if own:
                    nc.tensor.matmul(out[:, :, :], identb[:, :], cmask[:, :, :], start=True, stop=False,
                                     skip_group_check=True)
                for k in range(HB):
                    h = HB * j + k
                    ins = nc.tensor.matmul(out[:, k, :], Qs[0:KS, gp, h, r * T:(r + 1) * T],
                                           Ks[0:KS, gp, h, r * T:(r + 1) * T],
                                           start=not own, stop=True, skip_group_check=True)
                ins.then_inc(scored.sem, 1)

            def scores_t(b, gp, r, j):
                pe.wait_ge(exp_done.sem, exp_done.at(NBLK * b + j - 1))
                for k in range(HB):
                    h = HB * j + k
                    ins = nc.tensor.matmul(psT[j % 2][:, k, :], Ks[0:KT, gp, h, r * T:(r + 1) * T],
                                           Qs[0:KT, gp, h, r * T:(r + 1) * T],
                                           start=True, stop=True, skip_group_check=True)
                ins.then_inc(scored_t.sem, 1)

            def weigh(b, gp, r, j):
                pe.wait_ge(probs_ready.sem, probs_ready.at(NBLK * b + j + 1))
                for k in range(HB):
                    h = HB * j + k
                    ins = nc.tensor.matmul(outs[:, h, :], PT[:, j, k, :], vaug[:, gp, r, h, :],
                                           start=True, stop=True, skip_group_check=True)
                ins.then_inc(weighed.sem, 1)

            def turn_max(b, r):
                pe.wait_ge(maxed.sem, maxed.at(NBLK * (b + 1)))
                pe.wait_ge(minus_ready.sem, minus_ready.at(b))
                if own:
                    pe.wait_ge(added.sem, added.at(b - 2))
                nc.tensor.transpose(psM[0:H, 0:128], mx[:, r % 2, :], ident[:, :]).then_inc(max_turned.sem, 1)

            pe.wait_ge(s_w, 16 * NW)
            if own:
                pe.wait_ge(s_neg, 1)
            else:
                pe.wait_ge(s_cst, 16 * 9)
            prep_transpose(0)
            prep_q(0)
            prep_k(0, 0, 0)
            prep_v(0, 0)
            prep_transpose(1)
            prep_q(1)
            prep_k(1, 1, 0)
            pe.wait_ge(s_rows, 16 * (2 if own else 12))
            pe.wait_ge(s_ones, 2)
            pe.wait_ge(stacked[0].sem, stacked[0].at(NSTACK))
            for b in range(2):
                for j in range(NBLK):
                    scores(b, 0, b, j)
                turn_max(b, b)
            for s in (scored_t, weighed) + ((out_turned, out_projected) if own else ()):
                s.credit(nc.tensor)

            def step(g, gp, r, left):
                b = G * g + r
                ahead = left >= 2
                agp, ar = (gp, r + 2) if r < 2 else (1 - gp, r - 2)
                pe.wait_ge(row_placed[r % 2].sem, row_placed[r % 2].at(16 * half(g, gp, r) + 16))
                scores_t(b, gp, r, 0)
                scores_t(b, gp, r, 1)
                if ahead and r == 2:
                    pe.wait_ge(stacked[agp].sem, stacked[agp].at(NSTACK * pair(g, gp, 1) + NSTACK))
                if ahead:
                    scores(b + 2, agp, ar, 0)
                if r == 2 and left >= 2 * G - r:
                    prep_q(g + 2)
                if r == 0:
                    pe.wait_ge(v_ready.sem, v_ready.at(g + 1))
                pe.wait_ge(normed.sem, normed.at(b))
                if own:
                    pe.wait_ge(out_copied.sem, out_copied.at(b))
                weigh(b, gp, r, 0)
                scores_t(b, gp, r, 2)
                if ahead:
                    scores(b + 2, agp, ar, 1)
                weigh(b, gp, r, 1)
                scores_t(b, gp, r, 3)
                if ahead:
                    scores(b + 2, agp, ar, 2)
                weigh(b, gp, r, 2)
                weigh(b, gp, r, 3)
                if ahead:
                    scores(b + 2, agp, ar, 3)
                if r == 2 and left >= 2 * G - r:
                    prep_k(g + 2, gp, pair(g, gp, 2))
                if own:
                    pe.wait_ge(normed.sem, normed.at(b + 1))
                    nc.tensor.transpose(psO[:, 256:384], O[:, :, :].rearrange("p h d -> p (h d)"),
                                        ident[:, :]).then_inc(out_turned.sem, 1)
                if ahead:
                    turn_max(b + 2, ar)
                if r == 0 and left >= G:
                    prep_v(g + 1, 1 - gp)
                if r == 1 and left >= 2 * G - r:
                    prep_transpose(g + 2)
                if own:
                    pe.wait_ge(out_copied.sem, out_copied.at(b + 1))
                    if ahead:
                        pe.wait_ge(minus_ready.sem, minus_ready.at(b + 3))
                    nc.tensor.matmul(psM[:, 256:384], oT[:, :], wo[:, :], start=True,
                                     stop=True).then_inc(out_projected.sem, 1)

            pairs(nc.tensor, step)

        @block.scalar
        def _(act):
            def copy_hT(g):
                act.wait_ge(transposed.sem, transposed.at(g + 1))
                nc.scalar.activation(hT[:, :], psH[:, :], ACT.Copy).then_inc(hT_ready.sem, 1)

            def copy_v(g, gp):
                act.wait_ge(v_done.sem, v_done.at(g + 1))
                act.wait_ge(weighed.sem, weighed.at(NBLK * G * (g - 1)))
                nc.scalar.activation(vaug[:, gp, :, :, 0:DH],
                                     psH[:, :].rearrange("p (b h d) -> p b h d", b=G, h=H),
                                     ACT.Copy).then_inc(v_ready.sem, 1)

            copy_hT(0)
            if own:
                copy_v(0, 0)
            copy_hT(1)
            exp_done.credit(nc.scalar)
            if own:
                out_copied.credit(nc.scalar)

            def step(g, gp, r, left):
                b = G * g + r
                for j in range(NBLK):
                    act.wait_ge(scored_t.sem, scored_t.at(NBLK * b + j + 1))
                    act.wait_ge(weighed.sem, weighed.at(NBLK * (b - 1) + j + 1))
                    nc.scalar.activation(PT[:, j, :, :], psT[j % 2][:, :, :], ACT.Exp,
                                         scale=SCALE).then_inc(exp_done.sem, 1)
                if own:
                    act.wait_ge(out_turned.sem, out_turned.at(b + 1))
                    act.wait_ge(out_projected.sem, out_projected.at(b))
                    nc.scalar.activation(oT[:, :], psO[:, 256:384], ACT.Copy).then_inc(out_copied.sem, 1)
                if own and r == 0 and left >= G:
                    copy_v(g + 1, 1 - gp)
                if r == 1 and left >= 2 * G - r:
                    copy_hT(g + 2)

            pairs(nc.scalar, step)

        @block.gpsimd
        def _(pool):
            def rest(n, g):
                pool.wait_ge(hi_ready.sem, hi_ready.at(2 * g + n + 1))
                pool.sem_inc(passed, 1)
                nc.gpsimd.tensor_tensor(full[n][:, :], full[n][:, :], parts[n][:, 0, :],
                                        ALU.subtract).then_inc(rest_ready.sem, 1)

            def low(n, g):
                pool.wait_ge(mid_ready.sem, mid_ready.at(2 * g + n + 1))
                pool.sem_inc(passed, 1)
                nc.gpsimd.tensor_tensor(parts[n][:, 2, :], full[n][:, :], parts[n][:, 1, :],
                                        ALU.subtract).then_inc(lo_ready.sem, 1)

            def root(g):
                pool.wait_ge(stats_ready.sem, stats_ready.at(g + 1))
                pool.sem_inc(passed, 1)
                nc.gpsimd.tensor_scalar(veps[:, :], mv[:, :, 1], EPS, None, ALU.add).then_inc(own_pool.sem, 1)
                pool.wait_ge(own_pool.sem, own_pool.at(g + 2))
                pool.sem_inc(passed, 1)
                nc.gpsimd.tensor_tensor(rstd[:, :], veps[:, :], half_neg[:, :], ALU.pow).then_inc(rstd_ready.sem, 1)

            nc.gpsimd.memset(half_neg[:, :], -0.5).then_inc(own_pool.sem, 1)
            for g in range(2):
                root(g)
                for n in range(2):
                    rest(n, g)
                for n in range(2):
                    low(n, g)

            def step(g, gp, r, left):
                b = G * g + r
                if r == 0 and left >= 2 * G:
                    root(g + 2)
                for j in range(NBLK):
                    if own:
                        pool.wait_ge(exp_done.sem, exp_done.at(NBLK * b + j + 1))
                        pool.sem_inc(passed, 1)
                        nc.gpsimd.affine_select(out=PT[:, j, :, :], in_=PT[:, j, :, :], compare_op=ALU.is_ge,
                                                fill=0.0, base=0, pattern=[[0, HB], [1, 128]],
                                                channel_multiplier=-1).then_inc(selected.sem, 1)
                    if r == 2 and left >= 2 * G - r and j >= 2:
                        rest(j - 2, g + 2)
                    if r == 3 and left >= 2 * G - r and j < 2:
                        low(j, g + 2)

            pairs(nc.gpsimd, step)

        @block.vector
        def _(dve):
            def row_stats(g):
                for r in range(G):
                    nc.vector.bn_stats(stats[:, r, :], X[:, at(G * g + r), :]).then_inc(own_dve.sem, own_dve.one())
                dve.wait_ge(own_dve.sem, own_dve.value())
                if isinstance(g, Lin):
                    dve.sem_inc(passed, 1)
                for r in range(G):
                    ins = nc.vector.bn_aggr(mv[:, r, :], stats[:, r, :])
                ins.then_inc(stats_ready.sem, 1)

            def apply_norm(g):
                dve.wait_ge(rstd_ready.sem, rstd_ready.at(g + 1))
                dve.wait_ge(transposed.sem, transposed.at(g))
                for r in range(G):
                    ins = nc.vector.tensor_scalar(hn[:, r, :], X[:, at(G * g + r), :], mv[:, r, 0:1],
                                                  rstd[:, r:r + 1], ALU.subtract, ALU.mult)
                ins.then_inc(ln_done.sem, 1)

            def take(n, g, gp, nth_before):
                if n == 0:
                    dve.wait_ge(q_done.sem, q_done.at(g + 1))
                else:
                    dve.wait_ge(k_done.sem, k_done.at(g + 1))
                dve.wait_ge(lo_ready.sem, lo_ready.at(2 * g - 1 + n))
                if own:
                    ins = nc.vector.tensor_tensor(full[n][:, :], psP[:, :], pos[:, :], ALU.add)
                elif n == 0:
                    ins = nc.vector.tensor_scalar(full[n][:, :], psP[:, :], bqk[:, 0:1], None, ALU.add)
                else:
                    ins = nc.vector.scalar_tensor_tensor(out=full[n][:, :], in0=psP[:, :], scalar=bqk[:, 1:2],
                                                         in1=km[:, :, :].rearrange("p a t -> p (a t)"),
                                                         op0=ALU.add, op1=ALU.mult)
                ins.then_inc(taken.sem, 1)
                dve.wait_ge(taken.sem, taken.at(2 * g + n + 1))
                dve.wait_ge(hi_spilled[1 - gp].sem, hi_spilled[1 - gp].at(32 * nth_before + 32))
                nc.vector.tensor_copy(parts[n][:, 0, :], full[n][:, :]).then_inc(hi_ready.sem, 1)

            def mid(n, g, gp, nth_before):
                dve.wait_ge(rest_ready.sem, rest_ready.at(2 * g + n + 1))
                dve.wait_ge(lo_spilled[1 - gp].sem, lo_spilled[1 - gp].at(32 * nth_before + 32))
                nc.vector.tensor_copy(parts[n][:, 1, :], full[n][:, :]).then_inc(mid_ready.sem, 1)

            def take_v(g, gp):
                dve.wait_ge(v_done.sem, v_done.at(g + 1))
                dve.wait_ge(weighed.sem, weighed.at(NBLK * G * (g - 1)))
                for r in range(G):
                    ins = nc.vector.tensor_tensor(vaug[:, gp, r, :, 0:DH],
                                                  psH[:, r * 128:(r + 1) * 128].rearrange("p (h d) -> p h d", h=H),
                                                  bv[:, :].rearrange("p (h d) -> p h d", h=H), ALU.add)
                ins.then_inc(v_ready.sem, 1)

            def row_max(b, r, j):
                dve.wait_ge(scored.sem, scored.at(NBLK * b + j + 1))
                nc.vector.tensor_reduce(mx[:, r % 2, HB * j:HB * j + HB], psS[j % 2][:, :, :], AX.X,
                                        ALU.max).then_inc(maxed.sem, 1)

            def minus_max(b, r, nth):
                dve.wait_ge(max_turned.sem, max_turned.at(b + 1))
                dve.wait_ge(row_placed[r % 2].sem, row_placed[r % 2].at(16 * nth))
                nc.vector.tensor_scalar(negm[:, r % 2, :], psM[0:H, 0:128], -1.0, None,
                                        ALU.mult).then_inc(minus_ready.sem, 1)

            def normalise(b, r):
                dve.wait_ge(weighed.sem, weighed.at(NBLK * (b + 1)))
                nc.vector.reciprocal(rden[:, 0, :], outs[:, :, DH]).then_inc(own_dve.sem, own_dve.one())
                dve.wait_ge(own_dve.sem, own_dve.value())
                rd = rden[:, 0, :]
                if own:
                    dve.wait_ge(out_turned.sem, out_turned.at(b))
                else:
                    nc.vector.tensor_tensor(rden[:, 1, :], rden[:, 0, :],
                                                         qm[:, H * (r % 2):H * (r % 2) + H], ALU.mult).then_inc(
                                                             own_dve.sem, own_dve.one())
                    dve.wait_ge(own_dve.sem, own_dve.value())
                    rd = rden[:, 1, :]
                nc.vector.tensor_tensor(O[:, :, :], outs[:, :, 0:DH],
                                        rd.unsqueeze(2).to_broadcast([128, H, DH]), ALU.mult).then_inc(normed.sem, 1)

            def add(b):
                if own:
                    dve.wait_ge(out_projected.sem, out_projected.at(b + 1))
                    src = psM[:, 256:384]
                else:
                    dve.wait_ge(normed.sem, normed.at(b + 1))
                    src = O[:, :, :].rearrange("p h d -> p (h d)")
                if isinstance(b, Lin):
                    src = src.unsqueeze(1)
                nc.vector.tensor_tensor(X[:, at(b), :], X[:, at(b), :], src, ALU.add).then_inc(added.sem, 1)

            nc.vector.memset(ones[:, :], 1.0).then_inc(s_ones, 1)
            nc.vector.memset(vaug[:, :, :, :, DH:DH + 1], 1.0).then_inc(s_ones, 1)
            if first:
                dve.wait_ge(s_x[0], 16)
            if own:
                dve.wait_ge(s_cst, 16)
                nc.vector.tensor_copy(cmask[:, :, :], causal[:, :].unsqueeze(1).to_broadcast([128, HB, 128])
                                      ).then_inc(s_neg, 1)
            else:
                dve.wait_ge(s_cst, 16 * 9)
                nc.vector.tensor_copy(qm[:, :], qmi[:, :]).then_inc(own_dve.sem, own_dve.one())
                nc.vector.tensor_copy(kmf[:, :, :], kmi[:, :, :]).then_inc(own_dve.sem, own_dve.one())
                dve.wait_ge(own_dve.sem, own_dve.value())
                for r in range(G):
                    nc.vector.tensor_scalar(km[:, r, :], kmf[:, r % 2, :], 0.0, None, ALU.not_equal).then_inc(
                        own_dve.sem, own_dve.one())
                nc.vector.tensor_scalar(negrow[:, :, :], kmf[0:H, :, :], 0.0, NEG, ALU.is_equal,
                                        ALU.mult).then_inc(s_neg, 1)
            row_stats(0)
            apply_norm(0)
            dve.wait_ge(s_w, 16 * NW)
            for g in range(2):
                take(0, g, g, -1 + g)
                take(1, g, g, -1 + g)
                mid(0, g, g, -1 + g)
                mid(1, g, g, -1 + g)
                if g == 0:
                    if not own:
                        take_v(0, 0)
                    row_stats(1)
                    apply_norm(1)
            if first:
                dve.wait_ge(s_x[1], 16)
            for b in range(2):
                for j in range(NBLK):
                    row_max(b, b, j)
                minus_max(b, b, 0)
            for s in (normed, added):
                s.credit(nc.vector)

            def step(g, gp, r, left):
                b = G * g + r
                ahead = left >= 2
                if r == 0 and left >= 2 * G:
                    row_stats(g + 2)
                if r == 3 and left >= 2 * G - r:
                    mid(0, g + 2, gp, pair(g, gp, 1))
                    mid(1, g + 2, gp, pair(g, gp, 1))
                if ahead:
                    row_max(b + 2, r, 0)
                if r == 2 and left >= 2 * G - r:
                    take(0, g + 2, gp, pair(g, gp, 1))
                if ahead:
                    row_max(b + 2, r, 1)
                    row_max(b + 2, r, 2)
                normalise(b, r)
                if ahead:
                    row_max(b + 2, r, 3)
                    minus_max(b + 2, r, half(g, gp, r) + 1)
                if not own and r == 0 and left >= G:
                    take_v(g + 1, 1 - gp)
                if r == 0 and left >= 2 * G:
                    apply_norm(g + 2)
                if r == 2 and left >= 2 * G - r:
                    take(1, g + 2, gp, pair(g, gp, 1))
                add(b)

            pairs(nc.vector, step, own_dve, 2 * G + 2 * G * (1 if own else 2))


def scope(nc, prefix):
    ctx, used = ExitStack(), []
    ctx.push(clear(nc, used))

    def sb(name, shape, dt=F32):
        return ctx.enter_context(nc.sbuf_tensor(prefix + name, shape, dt))

    def ps(name, shape, dt=F32):
        return ctx.enter_context(nc.psum_tensor(prefix + name, shape, dt))

    def sem(name):
        s = ctx.enter_context(nc.semaphore(prefix + name))
        used.append(s.num)
        return s

    def signal(name, free=0):
        return Signal(sem(name), free)

    return ctx, sb, ps, sem, signal


def groups(eng, step, tally=None, per=0, pairs=NG // 2):
    with eng.Fori(0, pairs - 1) as i:
        if tally:
            tally.enter(i, per)
        for gp in range(2):
            step(Lin(i, 2, gp), gp, True)
    if tally:
        tally.leave(pairs - 1)
    for gp in range(2):
        step(2 * pairs - 2 + gp, gp, gp == 0)


def parity_count(g, gp, more=0):
    n = (gp + more) // 2 + 1
    return Lin(g.i, 1, n) if isinstance(g, Lin) else (g - gp) // 2 + n


def span(n, width):
    return bass.ds((n * width).value(), width) if isinstance(n, Lin) else slice(n * width, (n + 1) * width)


class RowNorm:

    def __init__(self, nc, X, sb, signal, own_dve, passed, rows=G):
        self.passed = passed
        self.nc, self.X, self.own, self.rows = nc, X, own_dve, rows
        self.stats = sb("stats", [128, rows, 6])
        self.mv = sb("mv", [128, rows, 2])
        self.veps = sb("veps", [128, rows])
        self.power = sb("power", [128, rows])
        self.rstd = sb("rstd", [128, rows])
        self.stats_ready = signal("stats_ready")
        self.eps_added = signal("eps_added")
        self.rstd_ready = signal("rstd_ready")
        self.done = signal("ln_done")

    def start(self, pool):
        self.nc.gpsimd.memset(self.power[:, :], -0.5).then_inc(self.eps_added.sem, 1)

    def take_stats(self, dve, g):
        nc = self.nc
        for r in range(self.rows):
            nc.vector.bn_stats(self.stats[:, r, :], self.X[:, at(self.rows * g + r), :]).then_inc(
                self.own.sem, self.own.one())
        dve.wait_ge(self.own.sem, self.own.value())
        if isinstance(g, Lin):
            dve.sem_inc(self.passed, 1)
        for r in range(self.rows):
            ins = nc.vector.bn_aggr(self.mv[:, r, :], self.stats[:, r, :])
        ins.then_inc(self.stats_ready.sem, 1)

    def root(self, pool, g):
        nc = self.nc
        pool.wait_ge(self.stats_ready.sem, self.stats_ready.at(g + 1))
        pool.sem_inc(self.passed, 1)
        nc.gpsimd.tensor_scalar(self.veps[:, :], self.mv[:, :, 1], EPS, None, ALU.add).then_inc(self.eps_added.sem, 1)
        pool.wait_ge(self.eps_added.sem, self.eps_added.at(g + 2))
        pool.sem_inc(self.passed, 1)
        nc.gpsimd.tensor_tensor(self.rstd[:, :], self.veps[:, :], self.power[:, :],
                                ALU.pow).then_inc(self.rstd_ready.sem, 1)

    def apply(self, dve, g, hn):
        nc = self.nc
        dve.wait_ge(self.rstd_ready.sem, self.rstd_ready.at(g + 1))
        for r in range(self.rows):
            ins = nc.vector.tensor_scalar(hn[:, r, :], self.X[:, at(self.rows * g + r), :], self.mv[:, r, 0:1],
                                          self.rstd[:, r:r + 1], ALU.subtract, ALU.mult)
        ins.then_inc(self.done.sem, 1)


E1, HID, CAP = 8, 512, 20
NJ = HID // 128
HALF = E1 // 2 * CAP


def experts_routed(nc, X, io, consts):
    ident, passed = consts["ident"], consts["passed"]
    ctx, sb, ps, sem, signal = scope(nc, "r_")
    with ctx:
        XG = sb("XG", [128, E1, B, CAP])

        with ExitStack() as inner:
            ctx2, sb, ps, sem, signal = scope(nc, "ra_")
            inner.enter_context(ctx2)
            wr, br, before = sb("wr", [128, E1]), sb("br", [128, E1]), sb("before", [128, 128], BF16)
            beforef = sb("beforef", [128, 128])
            iota8, iota20 = sb("iota8", [128, E1]), sb("iota20", [128, CAP])
            hn, hT = sb("hn", [128, 2, G, 128]), sb("hT", [128, GT])
            lg, mx8 = sb("lg", [128, G, E1]), sb("mx8", [128, G, E1])
            ix8, ixf = sb("ix8", [128, G, E1], U32), sb("ixf", [128, G, 2])
            oh0, oh, ohb = sb("oh0", [128, G, E1]), sb("oh", [128, G, E1]), sb("ohb", [128, G, E1], BF16)
            oh1 = sb("oh1", [128, G, E1])
            dl, ex, sm, rs = sb("dl", [128, G, E1]), sb("ex", [128, G, E1]), sb("sm", [128, G]), sb("rs", [128, G])
            gw, qp = sb("gw", [128, G, E1]), sb("qp", [128, G, E1])
            D, Dw = sb("D", [128, 2, G, E1, CAP]), sb("Dw", [128, 2, G, E1, CAP])
            dwt = sb("dwt", [HALF, 2, G, 2, 128])
            psH, psL, psN = ps("psH", [128, GT]), ps("psL", [128, G, E1]), ps("psN", [128, G, E1])
            psX = [ps(f"psX{n}", [128, 2, E1 * CAP]) for n in range(2)]
            psD = [ps(f"psD{n}", [128, 2, 2, 128]) for n in range(2)]
            own_dve = Tally(sem("own_dve"))
            norm = RowNorm(nc, X, sb, signal, own_dve, passed)
            s_w, s_before = sem("loads"), sem("before")
            turned, hT_ready = signal("turned"), signal("hT_ready", 1)
            logits, biased, shifted, exped = signal("logits", 1), signal("biased", 1), signal("shifted"), signal("exped")
            chosen, counted = signal("chosen"), signal("counted")
            d_ready, dw_ready = signal("d_ready", 1), signal("dw_ready")
            gathered, stored_x = signal("gathered", 4), signal("stored_x", 2)
            dw_turned, dw_copied = signal("dw_turned", 4), signal("dw_copied", 2)
            dw_saved = [signal(f"dw_saved{n}", 16) for n in range(2)]
            block = inner.enter_context(nc.Block())

            @block.sync
            def _(sp):
                for t, name in ((wr, "wr"), (beforef, "before")):
                    sp.dma_start(t[:, :], io[name]).then_inc(s_w, 16)
                for t, name in ((br, "br"), (iota8, "iota8"), (iota20, "iota20")):
                    sp.dma_start(t[:, :], io[name].partition_broadcast(128)).then_inc(s_w, 16)
                for s in dw_saved:
                    s.credit(nc.sync)

                def step(g, gp, more):
                    sp.wait_ge(dw_copied.sem, dw_copied.at(2 * g + 2))
                    sp.sem_inc(passed, 1)
                    dst = io["dwt"][at(g)]
                    sp.dma_start(dst.squeeze(0) if isinstance(g, Lin) else dst,
                                 dwt[:, gp, :, :, :].rearrange("p a b c -> p (a b c)")).then_inc(dw_saved[gp].sem, 16)
                groups(nc.sync, step)
                for s in dw_saved:
                    sp.wait_ge(s.sem, s.at(16 * (NG // 2)))
                    sp.sem_inc(passed, 1)

            @block.tensor
            def _(pe):
                def front(g, gp):
                    pe.wait_ge(norm.done.sem, norm.done.at(g + 1))
                    pe.wait_ge(hT_ready.sem, hT_ready.at(g))
                    for r in range(G):
                        ins = nc.tensor.transpose(psH[:, r * 128:(r + 1) * 128], hn[:, gp, r, :], ident[:, :])
                    ins.then_inc(turned.sem, 1)

                pe.wait_ge(s_w, 16 * 5)
                pe.wait_ge(s_before, 1)
                for s in (logits, gathered, dw_turned):
                    s.credit(nc.tensor)
                front(0, 0)

                def step(g, gp, more):
                    pe.wait_ge(hT_ready.sem, hT_ready.at(g + 1))
                    pe.wait_ge(biased.sem, biased.at(g))
                    for r in range(G):
                        ins = nc.tensor.matmul(psL[:, r, :], hT[:, r * T:(r + 1) * T], wr[:, :], start=True,
                                               stop=True, skip_group_check=True)
                    ins.then_inc(logits.sem, 1)
                    pe.wait_ge(chosen.sem, chosen.at(g + 1))
                    pe.wait_ge(d_ready.sem, d_ready.at(g))
                    nc.tensor.matmul(psN[:, :, :], before[:, :], ohb[:, :, :], start=True,
                                     stop=True).then_inc(counted.sem, 1)
                    if more:
                        front(g + 1, 1 - gp)
                    pe.wait_ge(d_ready.sem, d_ready.at(g + 1))
                    for n in range(2):
                        pe.wait_ge(stored_x.sem, stored_x.at(2 * g + n - 1))
                        for k in range(2):
                            r = 2 * n + k
                            ins = nc.tensor.matmul(psX[n][:, k, :], hn[:, gp, r, :],
                                                   D[:, gp, r, :, :].rearrange("p e c -> p (e c)"),
                                                   start=True, stop=True, skip_group_check=True)
                        ins.then_inc(gathered.sem, 1)
                    pe.wait_ge(dw_ready.sem, dw_ready.at(g + 1))
                    for n in range(2):
                        pe.wait_ge(dw_copied.sem, dw_copied.at(2 * g + n - 1))
                        for k in range(2):
                            for f in range(2):
                                ins = nc.tensor.transpose(
                                    psD[n][0:HALF, k, f, :],
                                    Dw[:, gp, 2 * n + k, 4 * f:4 * f + 4, :].rearrange("p e c -> p (e c)"), ident[:, :])
                        ins.then_inc(dw_turned.sem, 1)
                groups(nc.tensor, step)

            @block.scalar
            def _(act):
                def front(g):
                    act.wait_ge(turned.sem, turned.at(g + 1))
                    act.wait_ge(logits.sem, logits.at(g))
                    nc.scalar.activation(hT[:, :], psH[:, :], ACT.Copy).then_inc(hT_ready.sem, 1)

                for s in (hT_ready, stored_x):
                    s.credit(nc.scalar)
                front(0)

                def step(g, gp, more):
                    act.wait_ge(shifted.sem, shifted.at(g + 1))
                    nc.scalar.activation(ex[:, :, :], dl[:, :, :], ACT.Exp).then_inc(exped.sem, 1)
                    if more:
                        front(g + 1)
                    for n in range(2):
                        act.wait_ge(gathered.sem, gathered.at(2 * g + n + 1))
                        act.sem_inc(passed, 1)
                        b0 = g * G + 2 * n
                        for k in range(2):
                            dst = XG[:, :, at(b0 + k), :]
                            src = psX[n][:, k, :].rearrange("p (e c) -> p e c", e=E1)
                            if isinstance(g, Lin):
                                src = src.unsqueeze(2)
                            ins = nc.scalar.activation(dst, src, ACT.Copy)
                        ins.then_inc(stored_x.sem, 1)
                groups(nc.scalar, step)

            @block.gpsimd
            def _(pool):
                norm.start(pool)
                norm.root(pool, 0)

                def step(g, gp, more):
                    if more:
                        norm.root(pool, g + 1)
                groups(nc.gpsimd, step)

            @block.vector
            def _(dve):
                def wide(t):
                    return t[:, :].unsqueeze(1).to_broadcast([128, G, E1])

                def each(t):
                    return t.to_broadcast([128, G, E1])

                def copy_dw(g, gp):
                    for n in range(2):
                        dve.wait_ge(dw_turned.sem, dw_turned.at(2 * g + n + 1))
                        if n == 0:
                            dve.wait_ge(dw_saved[gp].sem, dw_saved[gp].at(16 * (parity_count(g, gp) - 1)))
                        nc.vector.tensor_copy(dwt[:, gp, 2 * n:2 * n + 2, :, :],
                                              psD[n][0:HALF, :, :, :]).then_inc(dw_copied.sem, 1)

                dve.wait_ge(s_w, 16 * 5)
                nc.vector.tensor_copy(before[:, :], beforef[:, :]).then_inc(s_before, 1)
                for s in (biased, d_ready, dw_copied):
                    s.credit(nc.vector)
                norm.take_stats(dve, 0)
                norm.apply(dve, 0, hn[:, 0, :, :])

                def step(g, gp, more):
                    dve.wait_ge(logits.sem, logits.at(g + 1))
                    nc.vector.tensor_tensor(lg[:, :, :], psL[:, :, :], wide(br), ALU.add).then_inc(biased.sem, 1)
                    dve.wait_ge(biased.sem, biased.at(g + 1))
                    dve.sem_inc(passed, 1)
                    for r in range(G):
                        nc.vector.max(out=mx8[:, r, :], in_=lg[:, r, :]).then_inc(own_dve.sem, own_dve.one())
                    dve.wait_ge(own_dve.sem, own_dve.value())
                    if isinstance(g, Lin):
                        dve.sem_inc(passed, 1)
                    for r in range(G):
                        nc.vector.max_index(ix8[:, r, :], mx8[:, r, :], lg[:, r, :]).then_inc(
                            own_dve.sem, own_dve.one())
                    nc.vector.tensor_tensor(dl[:, :, :], lg[:, :, :], each(mx8[:, :, 0:1]),
                                            ALU.subtract).then_inc(shifted.sem, 1)
                    dve.wait_ge(own_dve.sem, own_dve.value())
                    nc.vector.tensor_copy(ixf[:, :, :], ix8[:, :, 0:2]).then_inc(own_dve.sem, own_dve.one())
                    dve.wait_ge(own_dve.sem, own_dve.value())
                    nc.vector.tensor_tensor(oh0[:, :, :], wide(iota8), each(ixf[:, :, 0:1]), ALU.is_equal).then_inc(
                        own_dve.sem, own_dve.one())
                    nc.vector.tensor_tensor(oh1[:, :, :], wide(iota8), each(ixf[:, :, 1:2]), ALU.is_equal).then_inc(
                        own_dve.sem, own_dve.one())
                    dve.wait_ge(own_dve.sem, own_dve.value())
                    nc.vector.tensor_tensor(oh[:, :, :], oh0[:, :, :], oh1[:, :, :], ALU.add).then_inc(
                        own_dve.sem, own_dve.one())
                    dve.wait_ge(own_dve.sem, own_dve.value())
                    nc.vector.tensor_copy(ohb[:, :, :], oh[:, :, :]).then_inc(chosen.sem, 1)
                    if more:
                        norm.take_stats(dve, g + 1)
                    dve.wait_ge(exped.sem, exped.at(g + 1))
                    nc.vector.tensor_reduce(sm[:, :], ex[:, :, :], AX.X, ALU.add).then_inc(own_dve.sem, own_dve.one())
                    dve.wait_ge(own_dve.sem, own_dve.value())
                    nc.vector.reciprocal(rs[:, :], sm[:, :]).then_inc(own_dve.sem, own_dve.one())
                    dve.wait_ge(own_dve.sem, own_dve.value())
                    nc.vector.tensor_tensor(gw[:, :, :], ex[:, :, :], each(rs[:, :].unsqueeze(2)), ALU.mult).then_inc(
                        own_dve.sem, own_dve.one())
                    dve.wait_ge(own_dve.sem, own_dve.value())
                    nc.vector.tensor_tensor(gw[:, :, :], gw[:, :, :], oh[:, :, :], ALU.mult).then_inc(
                        own_dve.sem, own_dve.one())
                    dve.wait_ge(own_dve.sem, own_dve.value())
                    dve.wait_ge(counted.sem, counted.at(g + 1))
                    nc.vector.scalar_tensor_tensor(out=qp[:, :, :], in0=psN[:, :, :], scalar=1.0,
                                                        in1=oh[:, :, :], op0=ALU.add, op1=ALU.mult).then_inc(
                                                            own_dve.sem, own_dve.one())
                    dve.wait_ge(own_dve.sem, own_dve.value())
                    dve.wait_ge(gathered.sem, gathered.at(2 * g - 2))
                    slots = iota20[:, :].unsqueeze(1).to_broadcast([128, G * E1, CAP])
                    nc.vector.tensor_tensor(D[:, gp, :, :, :].rearrange("p a e c -> p (a e) c"), slots,
                                            qp[:, :, :].rearrange("p a e -> p (a e)").unsqueeze(2)
                                            .to_broadcast([128, G * E1, CAP]), ALU.is_equal).then_inc(d_ready.sem, 1)
                    dve.wait_ge(d_ready.sem, d_ready.at(g + 1))
                    dve.wait_ge(dw_turned.sem, dw_turned.at(2 * g - 2))
                    nc.vector.tensor_tensor(Dw[:, gp, :, :, :].rearrange("p a e c -> p (a e) c"),
                                            D[:, gp, :, :, :].rearrange("p a e c -> p (a e) c"),
                                            gw[:, :, :].rearrange("p a e -> p (a e)").unsqueeze(2)
                                            .to_broadcast([128, G * E1, CAP]), ALU.mult).then_inc(dw_ready.sem, 1)
                    if more:
                        dve.wait_ge(gathered.sem, gathered.at(2 * g))
                        norm.apply(dve, g + 1, hn[:, 1 - gp, :, :])
                    copy_dw(g, gp)
                groups(nc.vector, step, own_dve, 2 * (G + G + 4 + 4 + 1 + G))

        with ExitStack() as inner:
            ctx2, sb, ps, sem, signal = scope(nc, "rb_")
            inner.enter_context(ctx2)
            N2 = B // 2 * CAP
            w1, w2 = sb("w1", [128, 2, HID]), sb("w2", [128, 2, NJ, 128])
            b1, b2 = sb("b1", [128, E1 * NJ]), sb("b2", [128, E1])
            hid = sb("hid", [128, 2, NJ, N2])
            psF = [ps(f"psF{n}", [128, 512]) for n in range(NJ)]
            psY = [ps(f"psY{n}", [128, 512]) for n in range(2)]
            s_b = sem("biases")
            w_ready = [signal(f"w_ready{n}") for n in range(2)]
            first_done, relu_done = signal("first", 4), signal("relu", 4)
            second_done, y_taken = signal("second", 2), signal("y_taken", 2)
            block = inner.enter_context(nc.Block())

            @block.sync
            def _(sp):
                sp.dma_start(b1[:, :], io["b1T"]).then_inc(s_b, 16)
                sp.dma_start(b2[:, :], io["b2T"]).then_inc(s_b, 16)

                def load(e, gp):
                    a1, a2 = io["w1"][at(e)], io["w2"][at(e)]
                    if isinstance(e, Lin):
                        a1, a2 = a1.squeeze(0), a2.squeeze(0)
                    sp.dma_start(w1[:, gp, :], a1).then_inc(w_ready[gp].sem, 16)
                    sp.dma_start(w2[:, gp, :, :], a2.rearrange("(j p) c -> p j c", p=128)).then_inc(w_ready[gp].sem, 16)

                load(0, 0)

                def step(e, gp, more):
                    sp.wait_ge(second_done.sem, second_done.at(2 * e))
                    sp.sem_inc(passed, 1)
                    if more:
                        load(e + 1, 1 - gp)
                groups(nc.sync, step, pairs=E1 // 2)

            @block.tensor
            def _(pe):
                for s in (first_done, second_done):
                    s.credit(nc.tensor)

                def step(e, gp, more):
                    pe.wait_ge(w_ready[gp].sem, w_ready[gp].at(32 * parity_count(e, gp)))
                    for q in range(2):
                        n = 2 * e + q
                        for j in range(NJ):
                            pe.wait_ge(relu_done.sem, relu_done.at(NJ * n + j - 3))
                            rhs = XG[:, at(e), q * B // 2:(q + 1) * B // 2, :]
                            rhs = rhs.rearrange("p a b c -> p (a b c)") if isinstance(e, Lin) \
                                else rhs.rearrange("p b c -> p (b c)")
                            nc.tensor.matmul(psF[j][:, 0:N2], w1[:, gp, j * 128:(j + 1) * 128], rhs,
                                             start=True, stop=True).then_inc(first_done.sem, 1)
                        pe.wait_ge(y_taken.sem, y_taken.at(n - 1))
                        for j in range(NJ):
                            pe.wait_ge(relu_done.sem, relu_done.at(NJ * n + j + 1))
                            ins = nc.tensor.matmul(psY[q][:, 0:N2], w2[:, gp, j, :], hid[:, q, j, :],
                                                   start=(j == 0), stop=(j == NJ - 1))
                        ins.then_inc(second_done.sem, 1)
                groups(nc.tensor, step, pairs=E1 // 2)

            @block.scalar
            def _(act):
                act.wait_ge(s_b, 32)
                relu_done.credit(nc.scalar)

                def step(e, gp, more):
                    for q in range(2):
                        n = 2 * e + q
                        for j in range(NJ):
                            act.wait_ge(first_done.sem, first_done.at(NJ * n + j + 1))
                            if j == 0:
                                act.wait_ge(second_done.sem, second_done.at(n - 1))
                            act.sem_inc(passed, 1)
                            nc.scalar.activation(hid[:, q, j, :], psF[j][:, 0:N2], ACT.Relu,
                                                 bias=b1[:, at1(NJ * e + j)]).then_inc(relu_done.sem, 1)
                groups(nc.scalar, step, pairs=E1 // 2)

            @block.vector
            def _(dve):
                dve.wait_ge(s_b, 32)
                y_taken.credit(nc.vector)

                def step(e, gp, more):
                    for q in range(2):
                        n = 2 * e + q
                        dve.wait_ge(second_done.sem, second_done.at(n + 1))
                        dst = XG[:, at(e), q * B // 2:(q + 1) * B // 2, :]
                        dst = dst.rearrange("p a b c -> p (a b c)") if isinstance(e, Lin) \
                            else dst.rearrange("p b c -> p (b c)")
                        nc.vector.tensor_scalar(dst, psY[q][:, 0:N2], b2[:, at1(e)], None,
                                                ALU.add).then_inc(y_taken.sem, 1)
                groups(nc.vector, step, pairs=E1 // 2)

        with ExitStack() as inner:
            ctx2, sb, ps, sem, signal = scope(nc, "rc_")
            inner.enter_context(ctx2)
            dwt = sb("dwt", [HALF, 2, G, 2, 128])
            ys = sb("ys", [128, 2, G, E1, CAP])
            yv = sb("yv", [HALF, 2, G, 2, 128])
            psV = [ps(f"psV{n}", [128, 2, 2, 128]) for n in range(4)]
            psO = [ps(f"psO{n}", [128, G, 128]) for n in range(2)]
            loaded = [signal(f"loaded{n}") for n in range(2)]
            staged = signal("staged")
            turned, copied = signal("turned", 4), signal("copied", 4)
            mixed, added = signal("mixed", 2), signal("added", 2)
            block = inner.enter_context(nc.Block())

            @block.sync
            def _(sp):
                def load(g, gp):
                    src = io["dwt"][at(g)]
                    sp.dma_start(dwt[:, gp, :, :, :].rearrange("p a b c -> p (a b c)"),
                                 src.squeeze(0) if isinstance(g, Lin) else src).then_inc(loaded[gp].sem, 16)
                load(0, 0)

                def step(g, gp, more):
                    sp.wait_ge(mixed.sem, mixed.at(g))
                    sp.sem_inc(passed, 1)
                    if more:
                        load(g + 1, 1 - gp)
                groups(nc.sync, step)

            @block.gpsimd
            def _(pool):
                def step(g, gp, more):
                    pool.wait_ge(turned.sem, turned.at(2 * g - 2))
                    pool.sem_inc(passed, 1)
                    src = XG[:, :, span(g, G), :].rearrange("p e b c -> p b e c")
                    nc.gpsimd.tensor_copy(ys[:, gp, :, :, :], src).then_inc(staged.sem, 1)
                groups(nc.gpsimd, step)

            @block.tensor
            def _(pe):
                def front(g, gp):
                    pe.wait_ge(staged.sem, staged.at(g + 1))
                    for n in range(2):
                        pe.wait_ge(copied.sem, copied.at(2 * g + n - 3))
                        for k in range(2):
                            for f in range(2):
                                ins = nc.tensor.transpose(
                                    psV[2 * gp + n][0:HALF, k, f, :],
                                    ys[:, gp, 2 * n + k, 4 * f:4 * f + 4, :].rearrange("p e c -> p (e c)"), ident[:, :])
                        ins.then_inc(turned.sem, 1)

                for s in (turned, mixed):
                    s.credit(nc.tensor)
                front(0, 0)

                def step(g, gp, more):
                    if more:
                        front(g + 1, 1 - gp)
                    pe.wait_ge(copied.sem, copied.at(2 * g + 2))
                    pe.wait_ge(loaded[gp].sem, loaded[gp].at(16 * parity_count(g, gp)))
                    pe.wait_ge(added.sem, added.at(g - 1))
                    for r in range(G):
                        for f in range(2):
                            ins = nc.tensor.matmul(psO[gp][:, r, :], dwt[:, gp, r, f, :], yv[:, gp, r, f, :],
                                                   start=(f == 0), stop=(f == 1), skip_group_check=True)
                    ins.then_inc(mixed.sem, 1)
                groups(nc.tensor, step)

            @block.scalar
            def _(act):
                copied.credit(nc.scalar)

                def step(g, gp, more):
                    act.wait_ge(mixed.sem, mixed.at(g - 1))
                    for n in range(2):
                        act.wait_ge(turned.sem, turned.at(2 * g + n + 1))
                        nc.scalar.activation(yv[:, gp, 2 * n:2 * n + 2, :, :], psV[2 * gp + n][0:HALF, :, :, :],
                                             ACT.Copy).then_inc(copied.sem, 1)
                groups(nc.scalar, step)

            @block.vector
            def _(dve):
                added.credit(nc.vector)

                def step(g, gp, more):
                    dve.wait_ge(mixed.sem, mixed.at(g + 1))
                    nc.vector.tensor_tensor(X[:, span(g, G), :], X[:, span(g, G), :], psO[gp][:, :, :],
                                            ALU.add).then_inc(added.sem, 1)
                groups(nc.vector, step)


def at1(n):
    return bass.ds(n.value(), 1) if isinstance(n, Lin) else slice(n, n + 1)


def sequence_attention(nc, X, io, consts):
    ident, passed = consts["ident"], consts["passed"]
    PL = 4
    BLK = 4
    SC = C ** -0.5
    with ExitStack() as outer:
        ctx0, sb, ps, sem, signal = scope(nc, "s_")
        outer.enter_context(ctx0)
        HT = sb("HT", [128, B, T])
        GTt = sb("GTt", [128, B, T])

        with ExitStack() as inner:
            ctx1, sb, ps, sem, signal = scope(nc, "sa_")
            inner.enter_context(ctx1)
            wq, wk, gm = sb("wq", [128, 128]), sb("wk", [128, 128]), sb("gm", [128, 128])
            hn, hT = sb("hn", [128, 2, G, 128]), sb("hT", [128, 2, GT])
            psH = [ps(f"psH{n}", [128, GT]) for n in range(2)]
            psG = [ps(f"psG{n}", [128, GT]) for n in range(2)]
            psW = ps("psW", [128, 128])
            own_dve = Tally(sem("own_dve"))
            norm = RowNorm(nc, X, sb, signal, own_dve, passed)
            s_w, s_gm = sem("loads"), sem("gm")
            turned, hT_ready = signal("turned", 1), signal("hT_ready", 2)
            projected, kept = signal("projected", 2), signal("kept", 2)
            block = inner.enter_context(nc.Block())

            @block.sync
            def _(sp):
                sp.dma_start(wq[:, :], io["s_wq"]).then_inc(s_w, 16)
                sp.dma_start(wk[:, :], io["s_wk"]).then_inc(s_w, 16)

            @block.gpsimd
            def _(pool):
                norm.start(pool)
                norm.root(pool, 0)

                def step(g, gp, more):
                    if more:
                        norm.root(pool, g + 1)
                    pool.wait_ge(hT_ready.sem, hT_ready.at(g + 1))
                    pool.sem_inc(passed, 1)
                    src = hT[:, gp, :].rearrange("p (b t) -> p b t", b=G)
                    nc.gpsimd.tensor_copy(HT[:, span(g, G), :], src).then_inc(kept.sem, 1)
                kept.credit(nc.gpsimd)
                groups(nc.gpsimd, step)

            @block.vector
            def _(dve):
                norm.take_stats(dve, 0)
                norm.apply(dve, 0, hn[:, 0, :, :])
                dve.wait_ge(s_gm, 1)
                nc.vector.tensor_copy(gm[:, :], psW[:, :]).then_inc(s_gm, 1)

                def step(g, gp, more):
                    if more:
                        norm.take_stats(dve, g + 1)
                        dve.wait_ge(turned.sem, turned.at(g))
                        norm.apply(dve, g + 1, hn[:, 1 - gp, :, :])
                groups(nc.vector, step, own_dve, 2 * G)

            @block.tensor
            def _(pe):
                pe.wait_ge(s_w, 32)
                nc.tensor.matmul(psW[:, :], wq[:, :], wk[:, :], start=True, stop=True).then_inc(s_gm, 1)
                pe.wait_ge(s_gm, 2)
                for s in (turned, projected):
                    s.credit(nc.tensor)

                def front(g, gp):
                    pe.wait_ge(norm.done.sem, norm.done.at(g + 1))
                    pe.wait_ge(hT_ready.sem, hT_ready.at(g - 1))
                    for r in range(G):
                        ins = nc.tensor.transpose(psH[gp][:, r * 128:(r + 1) * 128], hn[:, gp, r, :], ident[:, :])
                    ins.then_inc(turned.sem, 1)
                front(0, 0)

                def step(g, gp, more):
                    if more:
                        front(g + 1, 1 - gp)
                    pe.wait_ge(hT_ready.sem, hT_ready.at(g + 1))
                    nc.tensor.matmul(psG[gp][:, :], gm[:, :], hT[:, gp, :], start=True,
                                     stop=True).then_inc(projected.sem, 1)
                groups(nc.tensor, step)

            @block.scalar
            def _(act):
                def front(g, gp):
                    act.wait_ge(turned.sem, turned.at(g + 1))
                    act.wait_ge(projected.sem, projected.at(g - 1))
                    act.wait_ge(kept.sem, kept.at(g - 1))
                    nc.scalar.activation(hT[:, gp, :], psH[gp][:, :], ACT.Copy).then_inc(hT_ready.sem, 1)

                def keep(g, gp):
                    act.wait_ge(projected.sem, projected.at(g + 1))
                    act.sem_inc(passed, 1)
                    src = psG[gp][:, :].rearrange("p (b t) -> p b t", b=G)
                    nc.scalar.activation(GTt[:, span(g, G), :], src, ACT.Copy)
                hT_ready.credit(nc.scalar)
                front(0, 0)

                def step(g, gp, more):
                    keep(g, gp)
                    if more:
                        front(g + 1, 1 - gp)
                groups(nc.scalar, step)

        with ExitStack() as inner:
            ctx1, sb, ps, sem, signal = scope(nc, "sb_")
            inner.enter_context(ctx1)
            mask = sb("mask", [128, 128])
            hs, hv = sb("hs", [128, 2, BLK, 128]), sb("hv", [128, 2, BLK, 129])
            th, ex, em = sb("th", [128, BLK, 128]), sb("ex", [128, BLK, 128]), sb("em", [128, 2, BLK, 128])
            rd, on = sb("rd", [128, BLK]), sb("on", [128, 2, BLK, 128])
            psV, psS = ps("psV", [128, BLK, 128]), ps("psS", [128, BLK, 128])
            psO = [ps(f"psO{n}", [128, 2, 256]) for n in range(2)]
            psT = ps("psT", [128, BLK, 128])
            own_dve = Tally(sem("own_dve"))
            s_w, s_one = sem("loads"), sem("ones")
            staged, turned, hv_ready = signal("staged"), signal("turned", 2), signal("hv_ready", 1)
            scored, tanh_done, exp_done = signal("scored", 2), signal("tanh", 1), signal("exp", 1)
            masked, weighed, normed = signal("masked", 1), signal("weighed", 3), signal("normed", 1)
            back, back_done = signal("back", 2), signal("back_done", 1)
            block = inner.enter_context(nc.Block())

            def places(t, g):
                w = BLK * PL
                return t[:, :, span(g, w)].rearrange("p b (k q) -> p k b q", q=PL)

            @block.sync
            def _(sp):
                sp.dma_start(mask[:, :], io["same_place"]).then_inc(s_w, 16)

            @block.gpsimd
            def _(pool):
                pool.wait_ge(s_w, 16)
                def step(g, gp, more):
                    pool.wait_ge(scored.sem, scored.at(g - 1))
                    pool.sem_inc(passed, 1)
                    nc.gpsimd.tensor_copy(hs[:, gp, :, :].rearrange("p k (b q) -> p k b q", q=PL),
                                          places(HT, g)).then_inc(staged.sem, 1)
                groups(nc.gpsimd, step)

            @block.tensor
            def _(pe):
                for s in (turned, scored, weighed, back):
                    s.credit(nc.tensor)

                def front(g, gp):
                    pe.wait_ge(staged.sem, staged.at(g + 1))
                    pe.wait_ge(hv_ready.sem, hv_ready.at(g))
                    for k in range(BLK):
                        ins = nc.tensor.transpose(psV[:, k, :], hs[:, gp, k, :], ident[:, :])
                    ins.then_inc(turned.sem, 1)
                    pe.wait_ge(tanh_done.sem, tanh_done.at(g))
                    for k in range(BLK):
                        gt = GTt[:, :, span_at(g, BLK * PL, k * PL, PL)]
                        ins = nc.tensor.matmul(psS[:, k, :].rearrange("p (b q) -> p b q", q=PL), hs[:, gp, k, :], gt,
                                               start=True, stop=True, skip_group_check=True)
                    ins.then_inc(scored.sem, 1)

                front(0, 0)
                pe.wait_ge(s_one, 1)

                def step(g, gp, more):
                    if more:
                        front(g + 1, 1 - gp)
                    pe.wait_ge(masked.sem, masked.at(g + 1))
                    pe.wait_ge(hv_ready.sem, hv_ready.at(g + 1))
                    pe.wait_ge(normed.sem, normed.at(g))
                    for k in range(BLK):
                        ins = nc.tensor.matmul(psO[k // 2][:, k % 2, 0:129], em[:, gp, k, :], hv[:, gp, k, :],
                                               start=True, stop=True, skip_group_check=True)
                    ins.then_inc(weighed.sem, 1)
                    pe.wait_ge(normed.sem, normed.at(g + 1))
                    pe.wait_ge(back_done.sem, back_done.at(g))
                    for k in range(BLK):
                        ins = nc.tensor.transpose(psT[:, k, :], on[:, gp, k, :], ident[:, :])
                    ins.then_inc(back.sem, 1)
                groups(nc.tensor, step)

            @block.scalar
            def _(act):
                for s in (hv_ready, tanh_done, exp_done, back_done):
                    s.credit(nc.scalar)

                def front(g, gp):
                    act.wait_ge(turned.sem, turned.at(g + 1))
                    act.wait_ge(weighed.sem, weighed.at(g - 1))
                    nc.scalar.activation(hv[:, gp, :, 0:128], psV[:, :, :], ACT.Copy).then_inc(hv_ready.sem, 1)
                    act.wait_ge(scored.sem, scored.at(g + 1))
                    act.wait_ge(exp_done.sem, exp_done.at(g))
                    nc.scalar.activation(th[:, :, :], psS[:, :, :], ACT.Tanh, scale=SC).then_inc(tanh_done.sem, 1)
                    act.wait_ge(tanh_done.sem, tanh_done.at(g + 1))
                    act.wait_ge(masked.sem, masked.at(g))
                    nc.scalar.activation(ex[:, :, :], th[:, :, :], ACT.Exp).then_inc(exp_done.sem, 1)
                front(0, 0)

                def step(g, gp, more):
                    if more:
                        front(g + 1, 1 - gp)
                    act.wait_ge(back.sem, back.at(g + 1))
                    act.sem_inc(passed, 1)
                    nc.scalar.activation(places(HT, g), psT[:, :, :].rearrange("p k (b q) -> p k b q", q=PL),
                                         ACT.Copy).then_inc(back_done.sem, 1)
                groups(nc.scalar, step)

            @block.vector
            def _(dve):
                nc.vector.memset(hv[:, :, :, 128:129], 1.0).then_inc(s_one, 1)
                dve.wait_ge(s_w, 16)
                for s in (masked, normed):
                    s.credit(nc.vector)

                def front(g, gp):
                    dve.wait_ge(exp_done.sem, exp_done.at(g + 1))
                    dve.wait_ge(weighed.sem, weighed.at(g - 1))
                    nc.vector.tensor_tensor(em[:, gp, :, :], ex[:, :, :],
                                            mask[:, :].unsqueeze(1).to_broadcast([128, BLK, 128]),
                                            ALU.mult).then_inc(masked.sem, 1)
                front(0, 0)

                def step(g, gp, more):
                    if more:
                        front(g + 1, 1 - gp)
                    dve.wait_ge(weighed.sem, weighed.at(g + 1))
                    for n in range(2):
                        nc.vector.reciprocal(rd[:, 2 * n:2 * n + 2], psO[n][:, :, 128]).then_inc(
                            own_dve.sem, own_dve.one())
                    dve.wait_ge(own_dve.sem, own_dve.value())
                    dve.wait_ge(back.sem, back.at(g - 1))
                    for k in range(BLK):
                        ins = nc.vector.tensor_scalar(on[:, gp, k, :], psO[k // 2][:, k % 2, 0:128], rd[:, k:k + 1],
                                                      None, ALU.mult)
                    ins.then_inc(normed.sem, 1)
                groups(nc.vector, step, own_dve, 2 * 2)

        with ExitStack() as inner:
            ctx1, sb, ps, sem, signal = scope(nc, "sc_")
            inner.enter_context(ctx1)
            os_ = sb("os", [128, 2, G, 128])
            psB = [ps(f"psB{n}", [128, G, 128]) for n in range(2)]
            staged, turned, added = signal("staged"), signal("turned", 2), signal("added", 2)
            block = inner.enter_context(nc.Block())

            @block.gpsimd
            def _(pool):
                def step(g, gp, more):
                    pool.wait_ge(turned.sem, turned.at(g - 1))
                    pool.sem_inc(passed, 1)
                    nc.gpsimd.tensor_copy(os_[:, gp, :, :], HT[:, span(g, G), :]).then_inc(staged.sem, 1)
                groups(nc.gpsimd, step)

            @block.tensor
            def _(pe):
                turned.credit(nc.tensor)

                def step(g, gp, more):
                    pe.wait_ge(staged.sem, staged.at(g + 1))
                    pe.wait_ge(added.sem, added.at(g - 1))
                    for r in range(G):
                        ins = nc.tensor.transpose(psB[gp][:, r, :], os_[:, gp, r, :], ident[:, :])
                    ins.then_inc(turned.sem, 1)
                groups(nc.tensor, step)

            @block.vector
            def _(dve):
                added.credit(nc.vector)

                def step(g, gp, more):
                    dve.wait_ge(turned.sem, turned.at(g + 1))
                    nc.vector.tensor_tensor(X[:, span(g, G), :], X[:, span(g, G), :], psB[gp][:, :, :],
                                            ALU.add).then_inc(added.sem, 1)
                groups(nc.vector, step)


def span_at(n, width, offset, size):
    return bass.ds((n * width + offset).value(), size) if isinstance(n, Lin) \
        else slice(n * width + offset, n * width + offset + size)


def context_attention(nc, X, io, consts):
    ident, passed = consts["ident"], consts["passed"]
    SC = C ** -0.5
    ctx, sb, ps, sem, signal = scope(nc, "x_")
    with ctx:
        wq, wk, wv, gm = (sb(n, [128, 128]) for n in ("wq", "wk", "wv", "gm"))
        hn, hT, gT = sb("hn", [128, G, 128]), sb("hT", [128, GT]), sb("gT", [128, GT])
        cT = sb("cT", [128, 2, GT])
        vv = sb("vv", [128, 2, G, 128])
        mx, nm, sm, rs = (sb(n, [128, G]) for n in ("mx", "nm", "sm", "rs"))
        P, PT = sb("P", [128, G, 128]), sb("PT", [128, G, 128])
        psH, psG, psV, psS = (ps(n, [128, GT]) for n in ("psH", "psG", "psV", "psS"))
        psP, psO = ps("psP", [128, GT]), ps("psO", [128, GT])
        own_dve = Tally(sem("own_dve"))
        norm = RowNorm(nc, X, sb, signal, own_dve, passed)
        s_w, s_gm = sem("loads"), sem("gm")
        c_ready = [signal(f"ctx{n}") for n in range(2)]
        turned, hT_ready = signal("turned"), signal("hT_ready", 1)
        projected, gT_ready = signal("projected", 1), signal("gT_ready", 1)
        v_done, v_ready = signal("v_done"), signal("v_ready", 1)
        scored, maxed, exped = signal("scored", 1), signal("maxed"), signal("exp", 1)
        p_turned, p_copied = signal("p_turned", 1), signal("p_copied", 1)
        weighed, added = signal("weighed", 2), signal("added", 1)
        block = ctx.enter_context(nc.Block())

        @block.sync
        def _(sp):
            for t, name in ((wq, "x_wq"), (wk, "x_wk"), (wv, "x_wv")):
                sp.dma_start(t[:, :], io[name]).then_inc(s_w, 16)

            def load(g, gp):
                sp.dma_start(cT[:, gp, :], io["ctxT"][:, span(g, GT)]).then_inc(c_ready[gp].sem, 16)
            load(0, 0)

            def step(g, gp, more):
                sp.wait_ge(scored.sem, scored.at(g))
                sp.sem_inc(passed, 1)
                if more:
                    load(g + 1, 1 - gp)
            groups(nc.sync, step)

        @block.gpsimd
        def _(pool):
            norm.start(pool)
            norm.root(pool, 0)

            def step(g, gp, more):
                if more:
                    norm.root(pool, g + 1)
            groups(nc.gpsimd, step)

        @block.tensor
        def _(pe):
            def front(g, gp):
                pe.wait_ge(norm.done.sem, norm.done.at(g + 1))
                pe.wait_ge(hT_ready.sem, hT_ready.at(g))
                for r in range(G):
                    ins = nc.tensor.transpose(psH[:, r * 128:(r + 1) * 128], hn[:, r, :], ident[:, :])
                ins.then_inc(turned.sem, 1)

            pe.wait_ge(s_w, 16 * 3)
            nc.tensor.matmul(psG[:, 0:128], wq[:, :], wk[:, :], start=True, stop=True).then_inc(s_gm, 1)
            for s in (projected, scored, p_turned, weighed):
                s.credit(nc.tensor)
            front(0, 0)
            pe.wait_ge(s_gm, 2)

            def step(g, gp, more):
                pe.wait_ge(c_ready[gp].sem, c_ready[gp].at(16 * parity_count(g, gp)))
                pe.wait_ge(v_ready.sem, v_ready.at(g))
                for r in range(G):
                    ins = nc.tensor.matmul(psV[:, r * 128:(r + 1) * 128], cT[:, gp, r * T:(r + 1) * T], wv[:, :],
                                           start=True, stop=True, skip_group_check=True)
                ins.then_inc(v_done.sem, 1)
                pe.wait_ge(hT_ready.sem, hT_ready.at(g + 1))
                pe.wait_ge(gT_ready.sem, gT_ready.at(g))
                nc.tensor.matmul(psG[:, :], gm[:, :], hT[:, :], start=True, stop=True).then_inc(projected.sem, 1)
                if more:
                    front(g + 1, 1 - gp)
                pe.wait_ge(gT_ready.sem, gT_ready.at(g + 1))
                pe.wait_ge(exped.sem, exped.at(g))
                for r in range(G):
                    ins = nc.tensor.matmul(psS[:, r * 128:(r + 1) * 128], gT[:, r * T:(r + 1) * T],
                                           cT[:, gp, r * T:(r + 1) * T], start=True, stop=True, skip_group_check=True)
                ins.then_inc(scored.sem, 1)
                pe.wait_ge(exped.sem, exped.at(g + 1))
                pe.wait_ge(p_copied.sem, p_copied.at(g))
                for r in range(G):
                    ins = nc.tensor.transpose(psP[:, r * 128:(r + 1) * 128], P[:, r, :], ident[:, :])
                ins.then_inc(p_turned.sem, 1)
                pe.wait_ge(p_copied.sem, p_copied.at(g + 1))
                pe.wait_ge(v_ready.sem, v_ready.at(g + 1))
                pe.wait_ge(added.sem, added.at(g))
                for r in range(G):
                    ins = nc.tensor.matmul(psO[:, r * 128:(r + 1) * 128], PT[:, r, :], vv[:, gp, r, :],
                                           start=True, stop=True, skip_group_check=True)
                ins.then_inc(weighed.sem, 1)
            groups(nc.tensor, step)

        @block.scalar
        def _(act):
            def front(g):
                act.wait_ge(turned.sem, turned.at(g + 1))
                act.wait_ge(projected.sem, projected.at(g))
                nc.scalar.activation(hT[:, :], psH[:, :], ACT.Copy).then_inc(hT_ready.sem, 1)

            for s in (hT_ready, exped, p_copied, v_ready):
                s.credit(nc.scalar)
            front(0)

            def step(g, gp, more):
                act.wait_ge(v_done.sem, v_done.at(g + 1))
                act.wait_ge(weighed.sem, weighed.at(g - 1))
                nc.scalar.activation(vv[:, gp, :, :].rearrange("p r c -> p (r c)"), psV[:, :],
                                     ACT.Copy).then_inc(v_ready.sem, 1)
                if more:
                    front(g + 1)
                act.wait_ge(maxed.sem, maxed.at(g + 1))
                act.wait_ge(p_turned.sem, p_turned.at(g))
                act.wait_ge(added.sem, added.at(g))
                for r in range(G):
                    ins = nc.scalar.activation(P[:, r, :], psS[:, r * 128:(r + 1) * 128], ACT.Exp,
                                               bias=nm[:, r:r + 1], scale=SC, accum_out=sm[:, r:r + 1])
                ins.then_inc(exped.sem, 1)
                act.wait_ge(p_turned.sem, p_turned.at(g + 1))
                nc.scalar.activation(PT[:, :, :].rearrange("p r c -> p (r c)"), psP[:, :],
                                     ACT.Copy).then_inc(p_copied.sem, 1)
            groups(nc.scalar, step)

        @block.vector
        def _(dve):
            norm.take_stats(dve, 0)
            norm.apply(dve, 0, hn[:, :, :])
            dve.wait_ge(s_gm, 1)
            nc.vector.tensor_copy(gm[:, :], psG[:, 0:128]).then_inc(s_gm, 1)
            for s in (gT_ready, added):
                s.credit(nc.vector)

            def step(g, gp, more):
                dve.wait_ge(projected.sem, projected.at(g + 1))
                dve.wait_ge(scored.sem, scored.at(g))
                nc.vector.tensor_copy(gT[:, :], psG[:, :]).then_inc(gT_ready.sem, 1)
                if more:
                    norm.take_stats(dve, g + 1)
                    norm.apply(dve, g + 1, hn[:, :, :])
                dve.wait_ge(scored.sem, scored.at(g + 1))
                nc.vector.tensor_reduce(mx[:, :], psS[:, :].rearrange("p (r k) -> p r k", r=G),
                                                     AX.X, ALU.max).then_inc(own_dve.sem, own_dve.one())
                dve.wait_ge(own_dve.sem, own_dve.value())
                dve.wait_ge(exped.sem, exped.at(g))
                nc.vector.tensor_scalar(nm[:, :], mx[:, :], -SC, None, ALU.mult).then_inc(maxed.sem, 1)
                dve.wait_ge(exped.sem, exped.at(g + 1))
                nc.vector.reciprocal(rs[:, :], sm[:, :]).then_inc(own_dve.sem, own_dve.one())
                dve.wait_ge(own_dve.sem, own_dve.value())
                dve.wait_ge(weighed.sem, weighed.at(g + 1))
                for r in range(G):
                    xb = X[:, at(G * g + r), :]
                    ins = nc.vector.scalar_tensor_tensor(
                        out=xb, in0=psO[:, r * 128:(r + 1) * 128].unsqueeze(1) if isinstance(g, Lin)
                        else psO[:, r * 128:(r + 1) * 128],
                        scalar=rs[:, r:r + 1], in1=xb, op0=ALU.mult, op1=ALU.add)
                ins.then_inc(added.sem, 1)
            groups(nc.vector, step, own_dve, 2 * (G + 2))


def experts_chosen(nc, X, io, consts):
    passed = consts["passed"]
    N, SL = io["cw"].shape[0], io["idx"].shape[0]
    NT, NA = N // 128, SL // 128
    ctx, sb, ps, sem, signal = scope(nc, "e_")
    with ctx:
        w1, w2 = sb("w1", [128, 2, HID]), sb("w2", [128, 2, NJ, 128])
        b1, b2 = sb("b1", [128, E1 * NJ]), sb("b2", [128, E1, 128])
        cw = sb("cw", [128, NT, E1])
        cwr = sb("cwr", [128, NT, E1])
        cwp = sb("cwp", [128, NT, 3, E1], BF16)
        idi, idf = sb("idi", [128, NA, E1], I32), sb("idf", [128, E1, NA])
        idb = sb("idb", [128, E1, SL], I32)
        idc = sb("idc", [128, 2, NA])
        tokid, iotaN = sb("tokid", [128, NT]), sb("iotaN", [128, N])
        hn, hp = sb("hn", [128, NT, 128]), sb("hp", [128, NT, 3, 128], BF16)
        oh, ohT = sb("oh", [128, 2, NT, SL], BF16), sb("ohT", [128, 2, NA, N], BF16)
        xg, h1 = sb("xg", [128, SL]), sb("h1", [128, NJ, SL])
        ws, yw = sb("ws", [128, NA]), sb("yw", [128, NA, 128])
        yp = sb("yp", [128, 3, NA, 128], BF16)
        psX, psW = ps("psX", [128, SL]), ps("psW", [128, NA, 3])
        psF = [ps(f"psF{n}", [128, 2, SL]) for n in range(2)]
        psY = ps("psY", [128, NA, 128])
        psA = [ps(f"psA{n}", [128, G, 128]) for n in range(2)]
        own_dve = Tally(sem("own_dve"))
        norm = RowNorm(nc, X, sb, signal, own_dve, passed)
        s_c = sem("loads")
        split, idc_ready = signal("split"), signal("idc_ready")
        w_ready = [signal(f"w_ready{n}") for n in range(2)]
        oh_ready, ohT_ready = signal("oh_ready"), signal("ohT_ready")
        gathered, xg_ready = signal("gathered", 1), signal("xg_ready", 1)
        weights = signal("weights", 1)
        first_done, gelu_done = signal("first", 1), signal("gelu", 4)
        second_done, weighted = signal("second", 2), signal("weighted", 1)
        hi_done, rest_done, mid_done, lo_done = (signal(n) for n in ("hi", "rest", "mid", "lo"))
        scattered, added = signal("scattered", 3), signal("added", 2)
        block = ctx.enter_context(nc.Block())

        @block.sync
        def _(sp):
            sp.dma_start(idb[:, :, :].rearrange("p e s -> p (e s)"),
                         io["idxT"].rearrange("e s -> (e s)").partition_broadcast(128)).then_inc(s_c, 16)
            sp.dma_start(tokid[:, :], io["tokid"]).then_inc(s_c, 16)
            sp.dma_start(cw[:, :, :], io["cw"].rearrange("(n p) e -> p n e", p=128)).then_inc(s_c, 16)
            sp.dma_start(idi[:, :, :], io["idx"].rearrange("(a p) e -> p a e", p=128)).then_inc(s_c, 16)
            sp.dma_start(iotaN[:, :], io["iotaN"].partition_broadcast(128)).then_inc(s_c, 16)
            sp.dma_start(b1[:, :], io["eb1T"]).then_inc(s_c, 16)
            sp.dma_start(b2[:, :, :].rearrange("p e c -> p (e c)"),
                         io["eb2"].rearrange("e c -> (e c)").partition_broadcast(128)).then_inc(s_c, 16)

            def load(e, gp):
                a1, a2 = io["ew1"][at(e)], io["ew2"][at(e)]
                if isinstance(e, Lin):
                    a1, a2 = a1.squeeze(0), a2.squeeze(0)
                sp.dma_start(w1[:, gp, :], a1).then_inc(w_ready[gp].sem, 16)
                sp.dma_start(w2[:, gp, :, :], a2.rearrange("(j p) c -> p j c", p=128)).then_inc(w_ready[gp].sem, 16)
            load(0, 0)

            def step(e, gp, more):
                sp.wait_ge(second_done.sem, second_done.at(e))
                sp.sem_inc(passed, 1)
                if more:
                    load(e + 1, 1 - gp)
            groups(nc.sync, step, pairs=E1 // 2)

        @block.tensor
        def _(pe):
            def gather(e, gp):
                pe.wait_ge(oh_ready.sem, oh_ready.at(e + 1))
                pe.wait_ge(xg_ready.sem, xg_ready.at(e))
                for n in range(NT):
                    for k in range(3):
                        ins = nc.tensor.matmul(psX[:, :], hp[:, n, k, :], oh[:, gp, n, :],
                                               start=(n == 0 and k == 0), stop=(n == NT - 1 and k == 2))
                ins.then_inc(gathered.sem, 1)

            def gate(e, gp):
                pe.wait_ge(weighted.sem, weighted.at(e))
                for a in range(NA):
                    for n in range(NT):
                        rhs = cwp[:, n, :, at(e)]
                        if isinstance(e, Lin):
                            rhs = rhs.rearrange("p a b -> p (a b)")
                        ins = nc.tensor.matmul(psW[:, a, :], oh[:, gp, n, a * 128:(a + 1) * 128], rhs,
                                               start=(n == 0), stop=(n == NT - 1), skip_group_check=True)
                ins.then_inc(weights.sem, 1)

            for s in (gathered, weights, first_done, second_done, scattered):
                s.credit(nc.tensor)
            pe.wait_ge(split.sem, split.at(2))
            gather(0, 0)
            gate(0, 0)

            def step(e, gp, more):
                pe.wait_ge(w_ready[gp].sem, w_ready[gp].at(32 * parity_count(e, gp)))
                pe.wait_ge(xg_ready.sem, xg_ready.at(e + 1))
                for j in range(NJ):
                    pe.wait_ge(gelu_done.sem, gelu_done.at(NJ * (e - 1) + j // 2 * 2 + 2))
                    nc.tensor.matmul(psF[j // 2][:, j % 2, :], w1[:, gp, j * 128:(j + 1) * 128], xg[:, :],
                                     start=True, stop=True, skip_group_check=True).then_inc(first_done.sem, 1)
                pe.wait_ge(weighted.sem, weighted.at(e))
                pe.wait_ge(gelu_done.sem, gelu_done.at(NJ * (e + 1)))
                for a in range(NA):
                    for j in range(NJ):
                        ins = nc.tensor.matmul(psY[:, a, :], h1[:, j, a * 128:(a + 1) * 128], w2[:, gp, j, :],
                                               start=(j == 0), stop=(j == NJ - 1), skip_group_check=True)
                ins.then_inc(second_done.sem, 1)
                if more:
                    gather(e + 1, 1 - gp)
                    gate(e + 1, 1 - gp)
                pe.wait_ge(lo_done.sem, lo_done.at(e + 1))
                pe.wait_ge(ohT_ready.sem, ohT_ready.at(e + 1))
                for n in range(NT):
                    if n % G == 0:
                        pe.wait_ge(added.sem, added.at(2 * e + n // G - 1))
                    for a in range(NA):
                        for k in range(3):
                            ins = nc.tensor.matmul(psA[n // G][:, n % G, :], ohT[:, gp, a, n * 128:(n + 1) * 128],
                                                   yp[:, k, a, :], start=(a == 0 and k == 0),
                                                   stop=(a == NA - 1 and k == 2), skip_group_check=True)
                    if n % G == G - 1:
                        ins.then_inc(scattered.sem, 1)
            groups(nc.tensor, step, pairs=E1 // 2)

        @block.scalar
        def _(act):
            for s in (xg_ready, gelu_done):
                s.credit(nc.scalar)
            act.wait_ge(s_c, 16 * 7)

            def copy_x(e):
                act.wait_ge(gathered.sem, gathered.at(e + 1))
                act.wait_ge(first_done.sem, first_done.at(NJ * e))
                nc.scalar.activation(xg[:, :], psX[:, :], ACT.Copy).then_inc(xg_ready.sem, 1)
            copy_x(0)

            def step(e, gp, more):
                for j in range(NJ):
                    act.wait_ge(first_done.sem, first_done.at(NJ * e + j // 2 * 2 + 2))
                    if j == 0:
                        act.wait_ge(second_done.sem, second_done.at(e))
                    act.sem_inc(passed, 1)
                    nc.scalar.activation(h1[:, j, :], psF[j // 2][:, j % 2, :], ACT.Gelu_apprx_tanh,
                                         bias=b1[:, at1(NJ * e + j)]).then_inc(gelu_done.sem, 1)
                if more:
                    copy_x(e + 1)
            groups(nc.scalar, step, pairs=E1 // 2)

        @block.gpsimd
        def _(pool):
            norm.start(pool)
            for g in range(2):
                norm.root(pool, g)
            pool.wait_ge(s_c, 16 * 7)
            pool.wait_ge(split.sem, split.at(3))
            pool.sem_inc(passed, 1)

            def step(e, gp, more):
                pool.wait_ge(scattered.sem, scattered.at(2 * e - 2))
                pool.sem_inc(passed, 1)
                nc.gpsimd.tensor_copy(idc[:, gp, :].unsqueeze(1) if isinstance(e, Lin) else idc[:, gp, :],
                                      idf[:, at(e), :]).then_inc(idc_ready.sem, 1)
                pool.wait_ge(idc_ready.sem, idc_ready.at(e + 1))
                pool.sem_inc(passed, 1)
                for a in range(NA):
                    ins = nc.gpsimd.tensor_scalar(ohT[:, gp, a, :], iotaN[:, :], idc[:, gp, a:a + 1], None,
                                                  ALU.is_equal)
                ins.then_inc(ohT_ready.sem, 1)
            groups(nc.gpsimd, step, pairs=E1 // 2)

        @block.vector
        def _(dve):
            for s in (weighted, added):
                s.credit(nc.vector)
            for g in range(2):
                norm.take_stats(dve, g)
                norm.apply(dve, g, hn[:, G * g:G * g + G, :])
            dve.wait_ge(norm.done.sem, norm.done.at(2))
            dve.wait_ge(s_c, 16 * 7)
            for full_, part, last in ((hn, [hp[:, :, k, :] for k in range(3)], split),
                                      (cw, [cwp[:, :, k, :] for k in range(3)], split)):
                nc.vector.tensor_copy(part[0], full_[:, :, :]).then_inc(own_dve.sem, own_dve.one())
                dve.wait_ge(own_dve.sem, own_dve.value())
                nc.vector.tensor_tensor(full_[:, :, :], full_[:, :, :], part[0], ALU.subtract).then_inc(
                    own_dve.sem, own_dve.one())
                dve.wait_ge(own_dve.sem, own_dve.value())
                nc.vector.tensor_copy(part[1], full_[:, :, :]).then_inc(own_dve.sem, own_dve.one())
                dve.wait_ge(own_dve.sem, own_dve.value())
                nc.vector.tensor_tensor(part[2], full_[:, :, :], part[1], ALU.subtract).then_inc(last.sem, 1)
            nc.vector.tensor_copy(idf[:, :, :].rearrange("p e a -> p a e"), idi[:, :, :]).then_inc(split.sem, 1)

            def mark_slots(e, gp):
                dve.wait_ge(weights.sem, weights.at(e - 1))
                for n in range(NT):
                    src = idb[:, at(e), :]
                    dst = oh[:, gp, n, :]
                    ins = nc.vector.tensor_scalar(dst.unsqueeze(1) if isinstance(e, Lin) else dst, src,
                                                  tokid[:, n:n + 1], None, ALU.is_equal)
                ins.then_inc(oh_ready.sem, 1)
            mark_slots(0, 0)

            def step(e, gp, more):
                if more:
                    mark_slots(e + 1, 1 - gp)
                dve.wait_ge(weights.sem, weights.at(e + 1))
                nc.vector.tensor_reduce(ws[:, :], psW[:, :, :], AX.X, ALU.add).then_inc(own_dve.sem, own_dve.one())
                dve.wait_ge(second_done.sem, second_done.at(e + 1))
                bias = b2[:, at(e), :]
                bias = bias.to_broadcast([128, NA, 128]) if isinstance(e, Lin) \
                    else bias.unsqueeze(1).to_broadcast([128, NA, 128])
                nc.vector.tensor_tensor(yw[:, :, :], psY[:, :, :], bias, ALU.add).then_inc(own_dve.sem, own_dve.one())
                dve.wait_ge(own_dve.sem, own_dve.value())
                nc.vector.tensor_tensor(yw[:, :, :], yw[:, :, :], ws[:, :].unsqueeze(2).to_broadcast([128, NA, 128]),
                                        ALU.mult).then_inc(weighted.sem, 1)
                dve.wait_ge(weighted.sem, weighted.at(e + 1))
                dve.wait_ge(scattered.sem, scattered.at(2 * e))
                nc.vector.tensor_copy(yp[:, 0, :, :], yw[:, :, :]).then_inc(own_dve.sem, own_dve.one())
                dve.wait_ge(own_dve.sem, own_dve.value())
                nc.vector.tensor_tensor(yw[:, :, :], yw[:, :, :], yp[:, 0, :, :], ALU.subtract).then_inc(
                    own_dve.sem, own_dve.one())
                dve.wait_ge(own_dve.sem, own_dve.value())
                nc.vector.tensor_copy(yp[:, 1, :, :], yw[:, :, :]).then_inc(own_dve.sem, own_dve.one())
                dve.wait_ge(own_dve.sem, own_dve.value())
                nc.vector.tensor_tensor(yp[:, 2, :, :], yw[:, :, :], yp[:, 1, :, :],
                                        ALU.subtract).then_inc(lo_done.sem, 1)
                for n in range(2):
                    dve.wait_ge(scattered.sem, scattered.at(2 * e + n + 1))
                    nc.vector.tensor_tensor(X[:, G * n:G * n + G, :], X[:, G * n:G * n + G, :], psA[n][:, :, :],
                                            ALU.add).then_inc(added.sem, 1)
            groups(nc.vector, step, own_dve, 2 * 5, pairs=E1 // 2)


def more_arrays(a):
    place = np.arange(128) % 4
    idx, cw = a["L1_ffn_top_idx"], a["L1_ffn_combine_weights"]
    return {
        "wr": a["L0_ffn_Wr"], "br": a["L0_ffn_br"],
        "before": np.triu(np.ones((T, T), np.float32), 1),
        "iota8": np.arange(E1, dtype=np.float32), "iota20": np.arange(1, CAP + 1, dtype=np.float32),
        "w1": a["L0_ffn_W1"], "w2": a["L0_ffn_W2"],
        "b1T": a["L0_ffn_b1"].reshape(E1 * NJ, 128).T, "b2T": a["L0_ffn_b2"].T,
        "s_wq": a["L1_attn_Wq"], "s_wk": a["L1_attn_Wk"],
        "same_place": (place[:, None] == place[None, :]).astype(np.float32),
        "x_wq": a["L1_xattn_Wq"], "x_wk": a["L1_xattn_Wk"], "x_wv": a["L1_xattn_Wv"].T,
        "idx": idx, "idxT": idx.T, "cw": cw,
        "tokid": np.arange(cw.shape[0], dtype=np.float32).reshape(-1, 128).T,
        "iotaN": np.arange(cw.shape[0], dtype=np.float32),
        "ew1": a["L1_ffn_W1"], "ew2": a["L1_ffn_W2"],
        "eb1T": a["L1_ffn_b1"].reshape(E1 * NJ, 128).T, "eb2": a["L1_ffn_b2"],
    }


def setup(nc, consts, io):
    with ExitStack() as ctx:
        used = []
        ctx.push(clear(nc, used))
        loaded = ctx.enter_context(nc.semaphore("identities"))
        used.append(loaded.num)
        block = ctx.enter_context(nc.Block())

        @block.sync
        def _(sp):
            sp.dma_start(consts["ident"][:, :], io["ident"]).then_inc(loaded, 16)

        @block.vector
        def _(dve):
            dve.wait_ge(loaded, 16)
            nc.vector.tensor_copy(consts["identb"][:, :], consts["ident"][:, :])


def store(nc, X, out):
    with ExitStack() as ctx:
        stored = ctx.enter_context(nc.semaphore("stored"))
        block = ctx.enter_context(nc.Block())

        @block.sync
        def _(sp):
            sp.dma_start(out.rearrange("b t c -> t b c"), X[:, :, :]).then_inc(stored, 16)
            sp.wait_ge(stored, 16)


def build(nc, io, out):
    with ExitStack() as ctx:
        X = ctx.enter_context(nc.sbuf_tensor("X", [128, B, C], F32))
        consts = {"ident": ctx.enter_context(nc.sbuf_tensor("ident", [128, 128], F32)),
                  "identb": ctx.enter_context(nc.sbuf_tensor("identb", [128, 128], BF16)),
                  "passed": ctx.enter_context(nc.semaphore("passed"))}
        setup(nc, consts, io)
        head_attention(nc, "self", X, io, consts, True)
        if STAGES >= 2:
            head_attention(nc, "cross", X, io, consts, False)
        if STAGES >= 3:
            experts_routed(nc, X, io, consts)
        if STAGES >= 4:
            sequence_attention(nc, X, io, consts)
        if STAGES >= 5:
            context_attention(nc, X, io, consts)
        if STAGES >= 6:
            experts_chosen(nc, X, io, consts)
        store(nc, X, out)


STAGES = 6


def kernel(**inputs):
    import concourse.bacc as bacc
    from concourse.bass_utils import run_bass_kernel_spmd as run

    a = {k: np.asarray(v) for k, v in inputs.items()}

    def heads_inner(w):
        return w.reshape(w.shape[:-1] + (H, DH)).swapaxes(-1, -2).reshape(w.shape)

    idx = np.arange(T, dtype=np.float32)
    eps = float(np.finfo(np.float32).eps)
    scale = (1.0 / (np.float32(10000.0) ** (np.arange(0, DH, 2, dtype=np.float32) / DH) + eps)).astype(np.float32)
    ang = idx[:, None] * scale[None, :]
    pos = np.stack([np.sin(ang), np.cos(ang)], axis=-1).reshape(T, DH).astype(np.float32)
    posT = np.tile(np.repeat(pos.T, H, axis=0), (1, G))
    causal = np.triu(np.full((T, T), CAUSAL_BIG, np.float32), 1)
    arrays = {
        "x": a["x"],
        "ident": np.eye(128, dtype=np.float32),
        "pos": posT,
        "causal": causal,
        "a_wq": heads_inner(a["L0_attn_Wq"]), "a_wk": heads_inner(a["L0_attn_Wk"]),
        "a_wv": a["L0_attn_Wv"], "a_wo": a["L0_attn_Wo"],
        "ctxT": a["ctx_1024"].transpose(2, 0, 1).reshape(C, B * T),
        "mask": a["mask_BxS2_ik0"], "maskT": a["mask_BxS2_ik0"].T,
        "c_wq": heads_inner(a["L0_xattn_Wq"].T), "c_wk": heads_inner(a["L0_xattn_Wk"].T), "c_wv": a["L0_xattn_Wv"].T,
        "bqk": np.stack([heads_inner(a["L0_xattn_bq"]), heads_inner(a["L0_xattn_bk"])], axis=1),
        "bv": a["L0_xattn_bv"],
    }
    arrays.update(more_arrays(a))
    nc = bacc.Bacc("TRN2", target_bir_lowering=False, num_devices=1)
    io = {}
    for name in list(arrays):
        arrays[name] = np.ascontiguousarray(arrays[name])
        io[name] = nc.dram_tensor(name + "_dram", arrays[name].shape, mybir.dt.from_np(arrays[name].dtype),
                                  kind="ExternalInput").ap()
    io["spill"] = nc.dram_tensor("spill_dram", [2, 2, 3, 128, GT], BF16, kind="Internal").ap()
    io["dwt"] = nc.dram_tensor("dwt_dram", [NG, E1 // 2 * CAP, G * 2 * 128], F32, kind="Internal").ap()
    out = nc.dram_tensor("out_dram", [B, T, C], F32, kind="ExternalOutput").ap()
    build(nc, io, out)
    r = run(nc, [{k + "_dram": v for k, v in arrays.items()}], core_ids=[0])
    return r.results[0]["out_dram"]
```

```python
import numpy as np

import concourse.bass as bass
from concourse import mybir
from contextlib import ExitStack

F32 = mybir.dt.float32
BF16 = mybir.dt.bfloat16
F16 = mybir.dt.float16
I32 = mybir.dt.int32
U32 = mybir.dt.uint32
ACT = mybir.ActivationFunctionType
ALU = mybir.AluOpType
AX = mybir.AxisListType

B, T, C = 32, 128, 128
G = 4
NG = B // G
H, DH = 16, 8
HB = 4
NBLK = H // HB
GT = G * T
EPS = 1e-5
CAUSAL_BIG = -1e30
NEG = -1e9 * DH ** 0.5
P_SCALE = 2.0 ** 12



class Lin:

    def __init__(self, i, k, c):
        self.i, self.k, self.c = i, k, c

    def __add__(self, n):
        return Lin(self.i, self.k, self.c + n)

    def __sub__(self, n):
        return self + -n

    def __mul__(self, n):
        return Lin(self.i, self.k * n, self.c * n)

    __rmul__, __radd__ = __mul__, __add__

    def value(self):
        return self.i * self.k + self.c


def at(n):
    return bass.ds(n.value(), 1) if isinstance(n, Lin) else n


class Signal:

    def __init__(self, sem, free=0):
        self.sem, self.free = sem, free

    def credit(self, eng):
        eng.sem_inc(self.sem, self.free)

    def at(self, n):
        if isinstance(n, Lin):
            n = n + self.free
            assert n.c >= 1, (n.k, n.c)
            return n.value()
        return n + self.free if n > 0 else 0


def clear(nc, used):
    def end(error, *_):
        if error is None:
            with nc.Block() as block:
                @block.gpsimd
                def _(pool):
                    first = None
                    for n in sorted(used):
                        first = n if first is None else first
                        if n + 1 not in used:
                            pool.sem_clear(range(first, n + 1))
                            first = None
    return end


class Tally:

    def __init__(self, sem):
        self.sem, self.n, self.i, self.per = sem, 0, None, 0

    def one(self):
        self.n += 1
        return 1

    def value(self):
        return self.n if self.i is None else self.i * self.per + self.n

    def enter(self, i, per):
        self.start, self.i, self.per = self.n, i, per

    def leave(self, times):
        assert self.n - self.start == self.per, (self.n - self.start, self.per)
        self.n, self.i = self.start + times * self.per, None


def head_attention(nc, kind, X_before, io, consts, first):
    own = kind == "self"
    X = X_before[:, 1:B + 1, :]
    p = "a_" if own else "c_"
    ROWS = 6 * DH
    KS = ROWS if own else ROWS + 1
    MROW = KS
    KT = KS + 2
    VP = 3
    SCALE = C ** -0.5 if own else DH ** -0.5
    ident, identb, passed = consts["ident"], consts["identb"], consts["passed"]
    Q_PARTS = [0, 0, 0, 1, 1, 2]
    K_RUNS = [(0, 3), (3, 2), (5, 1)]

    used = []
    with ExitStack() as ctx:
        ctx.push(clear(nc, used))

        def sb(name, shape, dt):
            return ctx.enter_context(nc.sbuf_tensor(p + name, shape, dt))

        def ps(name, shape, dt=F32):
            return ctx.enter_context(nc.psum_tensor(p + name, shape, dt))

        def sem(name):
            s = ctx.enter_context(nc.semaphore(p + name))
            used.append(s.num)
            return s

        def signal(name, free=0):
            return Signal(sem(name), free)

        wq, wk, wv = (sb(n, [128, 128], F32) for n in ("wq", "wk", "wv"))
        wo = sb("wo", [128, 128], F32) if own else None
        pos = sb("pos", [128, GT], F32) if own else None
        causal = sb("causal", [128, 128], F32) if own else None
        cmask = sb("cmask", [128, HB, 128], BF16) if own else None
        if not own:
            bqk = sb("bqk", [128, 2], F32)
            bv = sb("bv", [128, 128], F32)
            kmi = sb("kmi", [128, 2, 128], I32)
            km = sb("km", [128, G, 128], F32)
            kmf = sb("kmf", [128, 2, 128], F32)
            negrow = sb("negrow", [H, 2, 128], BF16)
            qmi = sb("qmi", [128, 32], I32)
            qm = sb("qm", [128, 32], F32)
            ctxT = sb("ctxT", [128, 2, GT], F32)
        ones = sb("ones", [H, 2 * GT], BF16)
        stats = sb("stats", [128, G, 6], F32)
        mv = sb("mv", [128, G, 2], F32)
        veps = sb("veps", [128, G], F32)
        half_neg = sb("half_neg", [128, G], F32)
        rstd = sb("rstd", [128, G], F32)
        hn = sb("hn", [128, G, 128], F32)
        hT = sb("hT", [128, GT], F32)
        full = [sb(n, [128, GT], F32) for n in ("qf", "kf")]
        parts = [sb(n, [128, 3, GT], BF16) for n in ("qp", "kp")]
        stack = [sb(n, [64, 2, H, GT], BF16) for n in ("qs", "ks")]
        Qs, Ks = stack
        vf = sb("vf", [128, GT], F32)
        vp = sb("vp", [128, 2, G, H, VP, DH + 1], BF16)
        mx = sb("mx", [128, 2, H], F32)
        negm = sb("negm", [H, 2, 2, 128], BF16)
        PT = sb("PT", [128, 2, HB, 128], F32)
        Ph, Pl = (sb(n, [128, NBLK, HB, 128], F16) for n in ("Ph", "Pl"))
        osum = sb("osum", [128, H, DH + 1], F32)
        rden = sb("rden", [128, 2, H], F32)
        O = sb("O", [128, H, DH], F32)
        oT = sb("oT", [128, 128], F32) if own else None

        psS = [ps(f"psS{n}", [128, HB, 128]) for n in range(2)]
        psT = [ps(f"psT{n}", [128, HB, 128]) for n in range(2)]
        psO = ps("psO", [128, 512])
        psH = ps("psH", [128, 512])
        psP = ps("psP", [128, 512])
        psM = ps("psM", [128, 512])
        outs = psO[:, 0:H * VP * (DH + 1)].rearrange("p (h a) -> p h a", h=H)

        s_w = sem("weights")
        s_x = [sem(f"x{n}") for n in range(2)]
        s_ctx = [signal(f"ctx{n}") for n in range(2)]
        s_cst = sem("constants")
        s_ones = sem("ones")
        s_neg = sem("masked_rows")
        s_rows = sem("fixed_rows")
        ln_done = signal("ln_done")
        stats_ready = signal("stats_ready")
        rstd_ready = signal("rstd_ready")
        transposed = signal("transposed")
        hT_ready = signal("hT_ready")
        q_done = signal("q_projected")
        k_done = signal("k_projected")
        v_done = signal("v_projected")
        v_taken = signal("v_taken")
        v_split = signal("v_split")
        v_rest = signal("v_rest")
        v_ready = signal("v_ready")
        taken = signal("taken")
        hi_ready = signal("hi_ready")
        rest_ready = signal("rest_ready")
        mid_ready = signal("mid_ready")
        lo_ready = signal("lo_ready")
        hi_spilled = [signal(f"hi_spilled{n}") for n in range(2)]
        lo_spilled = [signal(f"lo_spilled{n}") for n in range(2)]
        stacked = [signal(f"stacked{n}") for n in range(2)]
        scored = signal("scored")
        maxed = signal("maxed")
        max_turned = signal("max_turned")
        minus_ready = signal("minus_ready")
        row_placed = [signal(f"row_placed{n}") for n in range(2)]
        scored_t = signal("scored_t", 1)
        exp_done = signal("exp_done")
        selected = signal("selected")
        weighed = signal("weighed", 4)
        normed = signal("normed", 1)
        out_turned = signal("out_turned")
        out_copied = signal("out_copied")
        out_projected = signal("out_projected", 1)
        added = signal("added", 1)
        hi_made, lo_made = signal("probs_hi"), signal("probs_lo", 1)
        negated, inverted = signal("negated"), signal("inverted")
        query_masked = signal("query_masked")
        summed = signal("summed", 1)
        own_pool = signal("own_pool")
        own_dve = Tally(sem("own_dve"))

        NW = 5
        NSTACK = (len(Q_PARTS) + len(K_RUNS)) * 16

        def body(step, i):
            last = isinstance(i, int)
            for gp in range(2):
                g = 2 * i + gp if last else Lin(i, 2, gp)
                for r in range(G):
                    left = B - 1 - (G * g + r) if last else B
                    step(g, gp, r, left)

        def pairs(eng, step, tally=None, per=0):
            with eng.Fori(0, NG // 2 - 1) as i:
                if tally:
                    tally.enter(i, per)
                body(step, i)
            if tally:
                tally.leave(NG // 2 - 1)
            body(step, NG // 2 - 1)

        def pair(g, gp, more):
            n = (gp + more) // 2
            return Lin(g.i, 1, n) if isinstance(g, Lin) else (g - gp) // 2 + n

        def half(g, gp, r, more=0):
            n = 2 * gp + (r + more) // 2
            return Lin(g.i, 4, n) if isinstance(g, Lin) else 4 * ((g - gp) // 2) + n

        block = ctx.enter_context(nc.Block())

        @block.sync
        def _(sp):
            if first:
                xt = io["x"].rearrange("b t c -> t b c")
                sp.dma_start(X[:, 0:2 * G, :], xt[:, 0:2 * G, :]).then_inc(s_x[0], 16)
            sp.dma_start(wq[:, :], io[p + "wq"]).then_inc(s_w, 16)
            sp.dma_start(wk[:, :], io[p + "wk"]).then_inc(s_w, 16)
            sp.dma_start(wv[:, :], io[p + "wv"]).then_inc(s_w, 16)
            if own:
                sp.dma_start(pos[:, :], io["pos"]).then_inc(s_w, 16)
                sp.dma_start(wo[:, :], io[p + "wo"]).then_inc(s_w, 16)
                sp.dma_start(causal[:, :], io["causal"]).then_inc(s_cst, 16)
            else:
                for n in range(2):
                    sp.dma_start(ctxT[:, n, :], io["ctxT"][:, n * GT:(n + 1) * GT]).then_inc(s_ctx[n].sem, 16)
                sp.dma_start(bqk[:, :], io["bqk"]).then_inc(s_w, 16)
                sp.dma_start(bv[:, :], io["bv"].partition_broadcast(128)).then_inc(s_w, 16)
                for d in range(DH):
                    sp.dma_start(kmi[H * d:H * d + H, :, :],
                                 io["mask"].rearrange("(a h) t -> h a t", h=H)).then_inc(s_cst, 16)
                sp.dma_start(qmi[:, :], io["maskT"]).then_inc(s_cst, 16)
            if first:
                sp.dma_start(X[:, 2 * G:B, :], xt[:, 2 * G:B, :]).then_inc(s_x[1], 16)
            sp.wait_ge(s_ones, 4 if own else 3)
            for n in range(2):
                sp.dma_start(Ks[MROW:MROW + 2, n, :, :], ones[:, :]).then_inc(s_rows, 16)
                if not own:
                    sp.dma_start(Qs[ROWS:ROWS + 1, n, :, :], ones[:, 0:GT]).then_inc(s_rows, 16)
            if not own:
                sp.wait_ge(s_neg, 1)
                for n in range(2):
                    for r in range(G):
                        sp.dma_start(Ks[ROWS:ROWS + 1, n, :, r * T:(r + 1) * T],
                                     negrow[:, r % 2, :]).then_inc(s_rows, 16)

            def spill_hi(g, gp):
                for n in range(2):
                    sp.wait_ge(hi_ready.sem, hi_ready.at(2 * g + n + 1))
                    sp.sem_inc(passed, 1)
                    sp.dma_start(io["spill"][gp, n, 0], parts[n][:, 0, :]).then_inc(hi_spilled[gp].sem, 16)

            def spill_rest(g, gp):
                for n in range(2):
                    sp.wait_ge(lo_ready.sem, lo_ready.at(2 * g + n + 1))
                    sp.sem_inc(passed, 1)
                    sp.dma_start(io["spill"][gp, n, 1:3].rearrange("a p t -> p a t"),
                                 parts[n][:, 1:3, :]).then_inc(lo_spilled[gp].sem, 16)

            def fill(g, gp, nth):
                sp.wait_ge(hi_spilled[gp].sem, hi_spilled[gp].at(32 * nth + 32))
                sp.sem_inc(passed, 1)
                sp.wait_ge(lo_spilled[gp].sem, lo_spilled[gp].at(32 * nth + 32))
                sp.sem_inc(passed, 1)
                sp.wait_ge(scored_t.sem, scored_t.at(NBLK * G * (g - 1)))
                sp.sem_inc(passed, 1)
                for row, part in enumerate(Q_PARTS):
                    src = io["spill"][gp, 0, part].rearrange("(d h) t -> d (h t)", h=H)
                    sp.dma_start(Qs[DH * row:DH * row + DH, gp, :, :], src).then_inc(stacked[gp].sem, 16)
                for row, count in K_RUNS:
                    src = io["spill"][gp, 1, 0:count].rearrange("a (d h) t -> (a d) (h t)", h=H)
                    sp.dma_start(Ks[DH * row:DH * (row + count), gp, :, :], src).then_inc(stacked[gp].sem, 16)

            def place_row(b, gp, r):
                sp.wait_ge(minus_ready.sem, minus_ready.at(b + 1))
                sp.sem_inc(passed, 1)
                for a in range(2):
                    sp.dma_start(Qs[MROW + a:MROW + a + 1, gp, :, r * T:(r + 1) * T],
                                 negm[:, r % 2, a, :]).then_inc(row_placed[r % 2].sem, 16)

            def step(g, gp, r, left):
                b = G * g + r
                if r == 0 and left >= G:
                    spill_rest(g + 1, 1 - gp)
                    fill(g + 1, 1 - gp, pair(g, gp, 1))
                if left >= 2:
                    if r < 2:
                        place_row(b + 2, gp, r + 2)
                    else:
                        place_row(b + 2, 1 - gp, r - 2)
                if r == 3 and left >= 2 * G - r:
                    spill_hi(g + 2, gp)
                if not own and r == 0 and left >= 2 * G:
                    sp.wait_ge(v_done.sem, v_done.at(g + 1))
                    sp.sem_inc(passed, 1)
                    lo = (g + 2) * GT
                    src = io["ctxT"][:, bass.ds(lo.value(), GT)] if isinstance(lo, Lin) else io["ctxT"][:, lo:lo + GT]
                    sp.dma_start(ctxT[:, gp, :], src).then_inc(s_ctx[gp].sem, 16)

            spill_hi(0, 0)
            spill_rest(0, 0)
            fill(0, 0, 0)
            spill_hi(1, 1)
            place_row(0, 0, 0)
            place_row(1, 0, 1)
            pairs(nc.sync, step)

        @block.tensor
        def _(pe):
            def prep_transpose(g):
                pe.wait_ge(ln_done.sem, ln_done.at(g + 1))
                pe.wait_ge(v_taken.sem, v_taken.at(g))
                for r in range(G):
                    ins = nc.tensor.transpose(psH[:, r * 128:(r + 1) * 128], hn[:, r, :], ident[:, :])
                ins.then_inc(transposed.sem, 1)

            def prep_q(g):
                pe.wait_ge(hT_ready.sem, hT_ready.at(g + 1))
                pe.wait_ge(taken.sem, taken.at(2 * g))
                nc.tensor.matmul(psP[:, :], wq[:, :], hT[:, :], start=True, stop=True).then_inc(q_done.sem, 1)

            def prep_k(g, gp, nth):
                if not own:
                    pe.wait_ge(s_ctx[gp].sem, s_ctx[gp].at(16 * nth + 16))
                pe.wait_ge(taken.sem, taken.at(2 * g + 1))
                nc.tensor.matmul(psP[:, :], wk[:, :], hT[:, :] if own else ctxT[:, gp, :],
                                 start=True, stop=True).then_inc(k_done.sem, 1)

            def prep_v(g, gp):
                for r in range(G):
                    src = hT[:, r * T:(r + 1) * T] if own else ctxT[:, gp, r * T:(r + 1) * T]
                    ins = nc.tensor.matmul(psH[:, r * 128:(r + 1) * 128], src, wv[:, :], start=True, stop=True)
                ins.then_inc(v_done.sem, 1)

            def causal_part(j):
                nc.tensor.matmul(psS[j % 2][:, :, :], identb[:, :], cmask[:, :, :], start=True, stop=False,
                                 skip_group_check=True)

            def score(gp, r, j, k):
                h = HB * j + k
                return nc.tensor.matmul(psS[j % 2][:, k, :], Qs[0:KS, gp, h, r * T:(r + 1) * T],
                                        Ks[0:KS, gp, h, r * T:(r + 1) * T],
                                        start=not own, stop=True, skip_group_check=True)

            def score_t(gp, r, j, k):
                h = HB * j + k
                return nc.tensor.matmul(psT[j % 2][:, k, :], Ks[0:KT, gp, h, r * T:(r + 1) * T],
                                        Qs[0:KT, gp, h, r * T:(r + 1) * T],
                                        start=True, stop=True, skip_group_check=True)

            def weigh(gp, r, j, k):
                h = HB * j + k
                values = vp[:, gp, r, h, :, :].rearrange("p a d -> p (a d)")
                nc.tensor.matmul(outs[:, h, :], Ph[:, j, k, :], values, start=True, stop=False,
                                 skip_group_check=True)
                return nc.tensor.matmul(outs[:, h, :], Pl[:, j, k, :], values, start=False, stop=True,
                                        skip_group_check=True)

            def turn_max(b, r):
                pe.wait_ge(maxed.sem, maxed.at(NBLK * (b + 1)))
                pe.wait_ge(minus_ready.sem, minus_ready.at(b))
                if own:
                    pe.wait_ge(added.sem, added.at(b - 1))
                nc.tensor.transpose(psM[0:H, 0:128], mx[:, r % 2, :], ident[:, :]).then_inc(max_turned.sem, 1)

            scored_t.credit(nc.tensor)
            pe.wait_ge(s_w, 16 * NW)
            if own:
                pe.wait_ge(s_neg, 1)
            else:
                pe.wait_ge(s_cst, 16 * 9)
            prep_transpose(0)
            prep_q(0)
            prep_k(0, 0, 0)
            prep_v(0, 0)
            prep_transpose(1)
            prep_q(1)
            prep_k(1, 1, 0)
            pe.wait_ge(s_rows, 16 * (2 if own else 12))
            pe.wait_ge(s_ones, 4 if own else 3)
            pe.wait_ge(stacked[0].sem, stacked[0].at(NSTACK))
            for b in range(2):
                for j in range(NBLK):
                    pe.wait_ge(maxed.sem, maxed.at(NBLK * b + j - 1))
                    if own:
                        causal_part(j)
                    for k in range(HB):
                        ins = score(0, b, j, k)
                    ins.then_inc(scored.sem, 1)
                turn_max(b, b)
            pe.wait_ge(maxed.sem, maxed.at(NBLK * 2 - 1))
            if own:
                causal_part(0)
            for k in range(HB):
                ins = score(0, 2, 0, k)
            ins.then_inc(scored.sem, 1)
            pe.wait_ge(row_placed[0].sem, row_placed[0].at(32))
            for j in range(2):
                for k in range(HB):
                    ins = score_t(0, 0, j, k)
                ins.then_inc(scored_t.sem, 1)
            for s in (weighed,) + ((out_projected,) if own else ()):
                s.credit(nc.tensor)

            def turn_out(b):
                pe.wait_ge(added.sem, added.at(b))
                nc.tensor.transpose(psM[:, 128:256], O[:, :, :].rearrange("p h d -> p (h d)"),
                                    ident[:, :]).then_inc(out_turned.sem, 1)

            def project_out(b):
                pe.wait_ge(out_copied.sem, out_copied.at(b + 1))
                nc.tensor.matmul(psM[:, 256:384], oT[:, :], wo[:, :], start=True,
                                 stop=True).then_inc(out_projected.sem, 1)

            def step(g, gp, r, left):
                b = G * g + r
                for j in range(NBLK):
                    tgp, tr = (gp, r) if j < 2 else (gp, r + 1) if r < G - 1 else (1 - gp, 0)
                    if j == 2 and left >= 1:
                        pe.wait_ge(row_placed[(r + 1) % 2].sem,
                                   row_placed[(r + 1) % 2].at(32 * half(g, gp, r, 1) + 32))
                    if j < 2 or left >= 1:
                        pe.wait_ge(exp_done.sem, exp_done.at(NBLK * b + j + 1))
                        for k in range(HB):
                            ins = score_t(tgp, tr, (j + 2) % NBLK, k)
                        ins.then_inc(scored_t.sem, 1)
                    sj, near = (j + 1) % NBLK, j < NBLK - 1
                    sr = r + (2 if near else 3)
                    sgp, sr = (gp, sr) if sr < G else (1 - gp, sr - G)
                    more = left >= (2 if near else 3)
                    if more:
                        if r == 1 and j == 3:
                            pe.wait_ge(stacked[sgp].sem, stacked[sgp].at(NSTACK * pair(g, gp, 1) + NSTACK))
                        pe.wait_ge(maxed.sem, maxed.at(NBLK * (b + 2) + j))
                        if own:
                            causal_part(sj)
                    if j > 0:
                        pe.wait_ge(lo_made.sem, lo_made.at(NBLK * b + j + 1))
                    for k in range(HB):
                        if more:
                            ins = score(sgp, sr, sj, k)
                        if j > 0:
                            done = weigh(gp, r, j, k)
                    if more:
                        ins.then_inc(scored.sem, 1)
                    if j > 0:
                        done.then_inc(weighed.sem, 1)
                    if j == 0:
                        if r == 0:
                            pe.wait_ge(v_ready.sem, v_ready.at(g + 1))
                        pe.wait_ge(summed.sem, summed.at(b))
                        pe.wait_ge(lo_made.sem, lo_made.at(NBLK * b + 1))
                        for k in range(HB):
                            done = weigh(gp, r, 0, k)
                        done.then_inc(weighed.sem, 1)
                    if r == 0 and j == 0 and left >= G:
                        prep_v(g + 1, 1 - gp)
                    if own and j == 1:
                        pe.wait_ge(normed.sem, normed.at(b))
                        if left >= 1:
                            pe.wait_ge(minus_ready.sem, minus_ready.at(b + 2))
                        turn_out(b)
                    if own and j == 2:
                        project_out(b)
                    if r == 0 and j == 3 and left >= 2 * G:
                        prep_transpose(g + 2)
                    if r == 1 and j == 1 and left >= 2 * G - r:
                        prep_q(g + 2)
                    if r == 2 and j == 0 and left >= 2 * G - r:
                        prep_k(g + 2, gp, pair(g, gp, 2))
                if left >= 2:
                    turn_max(b + 2, r)

            pairs(nc.tensor, step)
            if own:
                pe.wait_ge(normed.sem, normed.at(B))
                turn_out(B)
                project_out(B)

        @block.scalar
        def _(act):
            def copy_hT(g):
                act.wait_ge(transposed.sem, transposed.at(g + 1))
                nc.scalar.activation(hT[:, :], psH[:, :], ACT.Copy).then_inc(hT_ready.sem, 1)

            def copy_v(g):
                act.wait_ge(v_done.sem, v_done.at(g + 1))
                act.wait_ge(v_ready.sem, v_ready.at(g))
                nc.scalar.activation(vf[:, :], psH[:, :], ACT.Copy).then_inc(v_taken.sem, 1)

            def part_v(g, gp, a):
                if a == 0:
                    act.wait_ge(v_taken.sem, v_taken.at(g + 1))
                    act.wait_ge(weighed.sem, weighed.at(NBLK * G * (g - 1)))
                else:
                    act.wait_ge(v_rest.sem, v_rest.at(2 * g + a))
                nc.scalar.activation(vp[:, gp, :, :, a, 0:DH], vf[:, :].rearrange("p (b h d) -> p b h d", b=G, h=H),
                                     ACT.Copy).then_inc(v_split.sem if a < 2 else v_ready.sem, 1)

            act.wait_ge(s_ones, 4 if own else 3)
            copy_hT(0)
            if own:
                copy_v(0)
            for a in range(VP):
                part_v(0, 0, a)
            copy_hT(1)

            def exponentials(n, j):
                act.wait_ge(scored_t.sem, scored_t.at(n + 1))
                act.wait_ge(lo_made.sem, lo_made.at(n - 1))
                nc.scalar.activation(PT[:, j % 2, :, :], psT[j % 2][:, :, :], ACT.Exp,
                                     scale=SCALE).then_inc(exp_done.sem, 1)

            def high(n, j):
                if own:
                    act.wait_ge(selected.sem, selected.at(n + 1))
                else:
                    act.wait_ge(exp_done.sem, exp_done.at(n + 1))
                act.wait_ge(weighed.sem, weighed.at(n - NBLK + 1))
                nc.scalar.activation(Ph[:, j, :, :], PT[:, j % 2, :, :], ACT.Copy,
                                     scale=P_SCALE).then_inc(hi_made.sem, 1)

            def copy_out(b):
                act.wait_ge(out_turned.sem, out_turned.at(b + 1))
                act.wait_ge(out_projected.sem, out_projected.at(b))
                nc.scalar.activation(oT[:, :], psM[:, 128:256], ACT.Copy).then_inc(out_copied.sem, 1)

            for j in range(2):
                exponentials(j, j)
            high(0, 0)

            def step(g, gp, r, left):
                b = G * g + r
                for j in range(NBLK):
                    if own and j == 2:
                        copy_out(b)
                    if j < 3 or left >= 1:
                        high(NBLK * b + j + 1, (j + 1) % NBLK)
                    if j < 2 or left >= 1:
                        exponentials(NBLK * b + j + 2, (j + 2) % NBLK)
                    if own and r == 0 and j == 1 and left >= G:
                        copy_v(g + 1)
                    if r == 0 and j == 2 and left >= G:
                        part_v(g + 1, 1 - gp, 0)
                    if r == 1 and j in (0, 2) and left >= G - r:
                        part_v(g + 1, 1 - gp, 1 + j // 2)
                    if r == 1 and j == 0 and left >= 2 * G - r:
                        copy_hT(g + 2)

            pairs(nc.scalar, step)
            if own:
                copy_out(B)

        @block.gpsimd
        def _(pool):
            def rest(n, g):
                pool.wait_ge(hi_ready.sem, hi_ready.at(2 * g + n + 1))
                pool.sem_inc(passed, 1)
                nc.gpsimd.tensor_tensor(full[n][:, :], full[n][:, :], parts[n][:, 0, :],
                                        ALU.subtract).then_inc(rest_ready.sem, 1)

            def low(n, g):
                pool.wait_ge(mid_ready.sem, mid_ready.at(2 * g + n + 1))
                pool.sem_inc(passed, 1)
                nc.gpsimd.tensor_tensor(parts[n][:, 2, :], full[n][:, :], parts[n][:, 1, :],
                                        ALU.subtract).then_inc(lo_ready.sem, 1)

            def root(g):
                pool.wait_ge(stats_ready.sem, stats_ready.at(g + 1))
                pool.sem_inc(passed, 1)
                nc.gpsimd.tensor_scalar(veps[:, :], mv[:, :, 1], EPS, None, ALU.add).then_inc(own_pool.sem, 1)
                pool.wait_ge(own_pool.sem, own_pool.at(g + 2))
                pool.sem_inc(passed, 1)
                nc.gpsimd.tensor_tensor(rstd[:, :], veps[:, :], half_neg[:, :], ALU.pow).then_inc(rstd_ready.sem, 1)

            def select(n, j):
                pool.wait_ge(exp_done.sem, exp_done.at(n + 1))
                pool.sem_inc(passed, 1)
                nc.gpsimd.affine_select(out=PT[:, j % 2, :, :], in_=PT[:, j % 2, :, :], compare_op=ALU.is_ge,
                                        fill=0.0, base=0, pattern=[[0, HB], [1, 128]],
                                        channel_multiplier=-1).then_inc(selected.sem, 1)

            def rest_v(g, gp, a):
                pool.wait_ge(v_split.sem, v_split.at(2 * g + a + 1))
                pool.sem_inc(passed, 1)
                nc.gpsimd.tensor_tensor(vf[:, :].rearrange("p (b h d) -> p b h d", b=G, h=H),
                                        vf[:, :].rearrange("p (b h d) -> p b h d", b=G, h=H),
                                        vp[:, gp, :, :, a, 0:DH], ALU.subtract).then_inc(v_rest.sem, 1)

            def finish(b, r):
                pool.wait_ge(inverted.sem, inverted.at(b + 1))
                rd = rden[:, 0, :]
                if own:
                    pool.wait_ge(out_turned.sem, out_turned.at(b + 1))
                    pool.sem_inc(passed, 1)
                else:
                    pool.sem_inc(passed, 1)
                    nc.gpsimd.tensor_tensor(rden[:, 1, :], rden[:, 0, :], qm[:, H * (r % 2):H * (r % 2) + H],
                                            ALU.mult).then_inc(query_masked.sem, 1)
                    rd = rden[:, 1, :]
                    pool.wait_ge(query_masked.sem, query_masked.at(b + 1))
                    pool.wait_ge(added.sem, added.at(b))
                    pool.sem_inc(passed, 1)
                nc.gpsimd.tensor_tensor(O[:, :, :], osum[:, :, 0:DH], rd.unsqueeze(2).to_broadcast([128, H, DH]),
                                        ALU.mult).then_inc(normed.sem, 1)
                if not own:
                    pool.wait_ge(normed.sem, normed.at(b + 1))
                    pool.sem_inc(passed, 1)
                    out = O[:, :, :].rearrange("p h d -> p (h d)")
                    nc.gpsimd.tensor_tensor(X[:, at(b), :], X[:, at(b), :],
                                            out.unsqueeze(1) if isinstance(b, Lin) else out,
                                            ALU.add).then_inc(added.sem, 1)

            nc.gpsimd.memset(half_neg[:, :], -0.5).then_inc(own_pool.sem, 1)
            for g in range(2):
                root(g)
                for n in range(2):
                    rest(n, g)
                for n in range(2):
                    low(n, g)
                if g == 0:
                    for a in range(VP - 1):
                        rest_v(0, 0, a)
            if own:
                for j in range(2):
                    select(j, j)

            def step(g, gp, r, left):
                b = G * g + r
                for j in range(NBLK):
                    if own and (j < 2 or left >= 1):
                        select(NBLK * b + j + 2, (j + 2) % NBLK)
                    if r == 0 and j == 1 and left >= 2 * G:
                        root(g + 2)
                    if r == 0 and j == 3 and left >= G:
                        rest_v(g + 1, 1 - gp, 0)
                    if r == 1 and j == 1 and left >= G - r:
                        rest_v(g + 1, 1 - gp, 1)
                    if left >= 2 * G - r:
                        if r == 1 and j == 3:
                            rest(0, g + 2)
                        if r == 2 and j == 2:
                            rest(1, g + 2)
                        if r == 2 and j == 3:
                            low(0, g + 2)
                        if r == 3 and j == 2:
                            low(1, g + 2)
                finish(b, r)

            for s in (normed,) + (() if own else (added,)):
                s.credit(nc.gpsimd)
            pairs(nc.gpsimd, step)

        @block.vector
        def _(dve):
            def row_stats(g):
                for r in range(G):
                    nc.vector.bn_stats(stats[:, r, :], X[:, at(G * g + r), :]).then_inc(own_dve.sem, own_dve.one())
                dve.wait_ge(own_dve.sem, own_dve.value())
                if isinstance(g, Lin):
                    dve.sem_inc(passed, 1)
                for r in range(G):
                    ins = nc.vector.bn_aggr(mv[:, r, :], stats[:, r, :])
                ins.then_inc(stats_ready.sem, 1)

            def apply_norm(g):
                dve.wait_ge(rstd_ready.sem, rstd_ready.at(g + 1))
                dve.wait_ge(transposed.sem, transposed.at(g))
                for r in range(G):
                    ins = nc.vector.tensor_scalar(hn[:, r, :], X[:, at(G * g + r), :], mv[:, r, 0:1],
                                                  rstd[:, r:r + 1], ALU.subtract, ALU.mult)
                ins.then_inc(ln_done.sem, 1)

            def take(n, g, gp, nth_before):
                if n == 0:
                    dve.wait_ge(q_done.sem, q_done.at(g + 1))
                else:
                    dve.wait_ge(k_done.sem, k_done.at(g + 1))
                dve.wait_ge(lo_ready.sem, lo_ready.at(2 * g - 1 + n))
                if own:
                    ins = nc.vector.tensor_tensor(full[n][:, :], psP[:, :], pos[:, :], ALU.add)
                elif n == 0:
                    ins = nc.vector.tensor_scalar(full[n][:, :], psP[:, :], bqk[:, 0:1], None, ALU.add)
                else:
                    ins = nc.vector.scalar_tensor_tensor(out=full[n][:, :], in0=psP[:, :], scalar=bqk[:, 1:2],
                                                         in1=km[:, :, :].rearrange("p a t -> p (a t)"),
                                                         op0=ALU.add, op1=ALU.mult)
                ins.then_inc(taken.sem, 1)
                dve.wait_ge(taken.sem, taken.at(2 * g + n + 1))
                dve.wait_ge(hi_spilled[1 - gp].sem, hi_spilled[1 - gp].at(32 * nth_before + 32))
                nc.vector.tensor_copy(parts[n][:, 0, :], full[n][:, :]).then_inc(hi_ready.sem, 1)

            def mid(n, g, gp, nth_before):
                dve.wait_ge(rest_ready.sem, rest_ready.at(2 * g + n + 1))
                dve.wait_ge(lo_spilled[1 - gp].sem, lo_spilled[1 - gp].at(32 * nth_before + 32))
                nc.vector.tensor_copy(parts[n][:, 1, :], full[n][:, :]).then_inc(mid_ready.sem, 1)

            def take_v(g):
                dve.wait_ge(v_done.sem, v_done.at(g + 1))
                dve.wait_ge(v_ready.sem, v_ready.at(g))
                nc.vector.tensor_tensor(vf[:, :].rearrange("p (b c) -> p b c", b=G),
                                        psH[:, :].rearrange("p (b c) -> p b c", b=G),
                                        bv[:, :].unsqueeze(1).to_broadcast([128, G, 128]),
                                        ALU.add).then_inc(v_taken.sem, 1)

            def row_max(b, r, j):
                dve.wait_ge(scored.sem, scored.at(NBLK * b + j + 1))
                nc.vector.tensor_reduce(mx[:, r % 2, HB * j:HB * j + HB], psS[j % 2][:, :, :], AX.X,
                                        ALU.max).then_inc(maxed.sem, 1)

            def minus_max(b, r, nth):
                dve.wait_ge(max_turned.sem, max_turned.at(b + 1))
                dve.wait_ge(row_placed[r % 2].sem, row_placed[r % 2].at(32 * nth))
                nc.vector.tensor_scalar(negm[:, r % 2, 0, :], psM[0:H, 0:128], -1.0, None,
                                        ALU.mult).then_inc(negated.sem, 1)
                dve.wait_ge(negated.sem, negated.at(b + 1))
                nc.vector.scalar_tensor_tensor(out=negm[:, r % 2, 1, :], in0=psM[0:H, 0:128], scalar=-1.0,
                                               in1=negm[:, r % 2, 0, :], op0=ALU.mult,
                                               op1=ALU.subtract).then_inc(minus_ready.sem, 1)

            def low_part(n, j):
                dve.wait_ge(hi_made.sem, hi_made.at(n + 1))
                nc.vector.scalar_tensor_tensor(out=Pl[:, j, :, :], in0=PT[:, j % 2, :, :], scalar=P_SCALE,
                                               in1=Ph[:, j, :, :], op0=ALU.mult,
                                               op1=ALU.subtract).then_inc(lo_made.sem, 1)

            def sum_parts(b):
                dve.wait_ge(weighed.sem, weighed.at(NBLK * (b + 1)))
                dve.wait_ge(normed.sem, normed.at(b))
                nc.vector.tensor_reduce(osum[:, :, :], outs.rearrange("p h (a d) -> p h d a", a=VP), AX.X,
                                        ALU.add).then_inc(summed.sem, 1)
                dve.wait_ge(summed.sem, summed.at(b + 1))
                nc.vector.reciprocal(rden[:, 0, :], osum[:, :, DH]).then_inc(inverted.sem, 1)

            def add(b):
                dve.wait_ge(out_projected.sem, out_projected.at(b + 1))
                src, place = psM[:, 256:384], X_before[:, at(b), :]
                nc.vector.tensor_tensor(place, place, src.unsqueeze(1) if isinstance(b, Lin) else src,
                                        ALU.add).then_inc(added.sem, 1)

            if own:
                nc.vector.memset(O[:, :, :], 0.0).then_inc(s_ones, 1)
                nc.vector.memset(X_before[:, 0, :], 0.0)
            nc.vector.memset(ones[:, :], 1.0).then_inc(s_ones, 1)
            nc.vector.memset(vp[:, :, :, :, 0, DH:DH + 1], 1.0).then_inc(s_ones, 1)
            nc.vector.memset(vp[:, :, :, :, 1:VP, DH:DH + 1], 0.0).then_inc(s_ones, 1)
            if first:
                dve.wait_ge(s_x[0], 16)
            if own:
                dve.wait_ge(s_cst, 16)
                nc.vector.tensor_copy(cmask[:, :, :], causal[:, :].unsqueeze(1).to_broadcast([128, HB, 128])
                                      ).then_inc(s_neg, 1)
            else:
                dve.wait_ge(s_cst, 16 * 9)
                nc.vector.tensor_copy(qm[:, :], qmi[:, :]).then_inc(own_dve.sem, own_dve.one())
                nc.vector.tensor_copy(kmf[:, :, :], kmi[:, :, :]).then_inc(own_dve.sem, own_dve.one())
                dve.wait_ge(own_dve.sem, own_dve.value())
                for r in range(G):
                    nc.vector.tensor_scalar(km[:, r, :], kmf[:, r % 2, :], 0.0, None, ALU.not_equal).then_inc(
                        own_dve.sem, own_dve.one())
                nc.vector.tensor_scalar(negrow[:, :, :], kmf[0:H, :, :], 0.0, NEG, ALU.is_equal,
                                        ALU.mult).then_inc(s_neg, 1)
            row_stats(0)
            apply_norm(0)
            dve.wait_ge(s_w, 16 * NW)
            for g in range(2):
                take(0, g, g, -1 + g)
                take(1, g, g, -1 + g)
                mid(0, g, g, -1 + g)
                mid(1, g, g, -1 + g)
                if g == 0:
                    if not own:
                        take_v(0)
                    row_stats(1)
                    apply_norm(1)
            if first:
                dve.wait_ge(s_x[1], 16)
            for b in range(2):
                for j in range(NBLK):
                    row_max(b, b, j)
                minus_max(b, b, 0)
            for s in (summed, lo_made) + ((added,) if own else ()):
                s.credit(nc.vector)
            low_part(0, 0)
            row_max(2, 2, 0)

            def step(g, gp, r, left):
                b = G * g + r
                ahead = left >= 2
                for j in range(NBLK):
                    if j < 3 or left >= 1:
                        low_part(NBLK * b + j + 1, (j + 1) % NBLK)
                    if j < 3 and ahead:
                        row_max(b + 2, r, j + 1)
                    if own and j == 3:
                        add(b)
                    if j == 3:
                        sum_parts(b)
                        if ahead:
                            minus_max(b + 2, r, half(g, gp, r) + 1)
                    if j == 3 and left >= 3:
                        row_max(b + 3, r + 1, 0)
                    if left >= 2 * G - r:
                        if r == 0 and j == 0:
                            row_stats(g + 2)
                        if r == 0 and j == 2:
                            apply_norm(g + 2)
                        if r == 1 and j == 2:
                            take(0, g + 2, gp, pair(g, gp, 1))
                        if r == 2 and j == 1:
                            take(1, g + 2, gp, pair(g, gp, 1))
                        if r == 2 and j == 2:
                            mid(0, g + 2, gp, pair(g, gp, 1))
                        if r == 3 and j == 0:
                            mid(1, g + 2, gp, pair(g, gp, 1))
                    if not own and r == 0 and j == 1 and left >= G:
                        take_v(g + 1)

            pairs(nc.vector, step, own_dve, 2 * G)
            if own:
                add(B)


def scope(nc, prefix):
    ctx, used = ExitStack(), []
    ctx.push(clear(nc, used))

    def sb(name, shape, dt=F32):
        return ctx.enter_context(nc.sbuf_tensor(prefix + name, shape, dt))

    def ps(name, shape, dt=F32):
        return ctx.enter_context(nc.psum_tensor(prefix + name, shape, dt))

    def sem(name):
        s = ctx.enter_context(nc.semaphore(prefix + name))
        used.append(s.num)
        return s

    def signal(name, free=0):
        return Signal(sem(name), free)

    return ctx, sb, ps, sem, signal


def groups(eng, step, tally=None, per=0, pairs=NG // 2):
    with eng.Fori(0, pairs - 1) as i:
        if tally:
            tally.enter(i, per)
        for gp in range(2):
            step(Lin(i, 2, gp), gp, True)
    if tally:
        tally.leave(pairs - 1)
    for gp in range(2):
        step(2 * pairs - 2 + gp, gp, gp == 0)


def parity_count(g, gp, more=0):
    n = (gp + more) // 2 + 1
    return Lin(g.i, 1, n) if isinstance(g, Lin) else (g - gp) // 2 + n


def span(n, width):
    return bass.ds((n * width).value(), width) if isinstance(n, Lin) else slice(n * width, (n + 1) * width)


class RowNorm:

    def __init__(self, nc, X, sb, signal, own_dve, passed, rows=G):
        self.passed = passed
        self.nc, self.X, self.own, self.rows = nc, X, own_dve, rows
        self.stats = sb("stats", [128, rows, 6])
        self.mv = sb("mv", [128, rows, 2])
        self.veps = sb("veps", [128, rows])
        self.power = sb("power", [128, rows])
        self.rstd = sb("rstd", [128, rows])
        self.stats_ready = signal("stats_ready")
        self.eps_added = signal("eps_added")
        self.rstd_ready = signal("rstd_ready")
        self.done = signal("ln_done")

    def start(self, pool):
        self.nc.gpsimd.memset(self.power[:, :], -0.5).then_inc(self.eps_added.sem, 1)

    def take_stats(self, dve, g):
        nc = self.nc
        for r in range(self.rows):
            nc.vector.bn_stats(self.stats[:, r, :], self.X[:, at(self.rows * g + r), :]).then_inc(
                self.own.sem, self.own.one())
        dve.wait_ge(self.own.sem, self.own.value())
        if isinstance(g, Lin):
            dve.sem_inc(self.passed, 1)
        for r in range(self.rows):
            ins = nc.vector.bn_aggr(self.mv[:, r, :], self.stats[:, r, :])
        ins.then_inc(self.stats_ready.sem, 1)

    def root(self, pool, g):
        nc = self.nc
        pool.wait_ge(self.stats_ready.sem, self.stats_ready.at(g + 1))
        pool.sem_inc(self.passed, 1)
        nc.gpsimd.tensor_scalar(self.veps[:, :], self.mv[:, :, 1], EPS, None, ALU.add).then_inc(self.eps_added.sem, 1)
        pool.wait_ge(self.eps_added.sem, self.eps_added.at(g + 2))
        pool.sem_inc(self.passed, 1)
        nc.gpsimd.tensor_tensor(self.rstd[:, :], self.veps[:, :], self.power[:, :],
                                ALU.pow).then_inc(self.rstd_ready.sem, 1)

    def apply(self, dve, g, hn):
        nc = self.nc
        dve.wait_ge(self.rstd_ready.sem, self.rstd_ready.at(g + 1))
        for r in range(self.rows):
            ins = nc.vector.tensor_scalar(hn[:, r, :], self.X[:, at(self.rows * g + r), :], self.mv[:, r, 0:1],
                                          self.rstd[:, r:r + 1], ALU.subtract, ALU.mult)
        ins.then_inc(self.done.sem, 1)


E1, HID, CAP = 8, 512, 20
NJ = HID // 128
HALF = E1 // 2 * CAP


def experts_routed(nc, X, io, consts):
    ident, passed = consts["ident"], consts["passed"]
    ctx, sb, ps, sem, signal = scope(nc, "r_")
    with ctx:
        XG = sb("XG", [128, E1, B, CAP])

        with ExitStack() as inner:
            ctx2, sb, ps, sem, signal = scope(nc, "ra_")
            inner.enter_context(ctx2)
            wr, br, before = sb("wr", [128, E1]), sb("br", [128, E1]), sb("before", [128, 128], BF16)
            beforef = sb("beforef", [128, 128])
            iota8, iota20 = sb("iota8", [128, E1]), sb("iota20", [128, CAP])
            hn, hT = sb("hn", [128, 2, G, 128]), sb("hT", [128, GT])
            lg, mx8 = sb("lg", [128, G, E1]), sb("mx8", [128, G, E1])
            ix8, ixf = sb("ix8", [128, G, E1], U32), sb("ixf", [128, G, 2])
            oh0, oh, ohb = sb("oh0", [128, G, E1]), sb("oh", [128, G, E1]), sb("ohb", [128, G, E1], BF16)
            oh1 = sb("oh1", [128, G, E1])
            dl, ex, sm, rs = sb("dl", [128, G, E1]), sb("ex", [128, G, E1]), sb("sm", [128, G]), sb("rs", [128, G])
            gw, qp = sb("gw", [128, G, E1]), sb("qp", [128, G, E1])
            D, Dw = sb("D", [128, 2, G, E1, CAP]), sb("Dw", [128, 2, G, E1, CAP])
            dwt = sb("dwt", [HALF, 2, G, 2, 128])
            psH, psL, psN = ps("psH", [128, GT]), ps("psL", [128, G, E1]), ps("psN", [128, G, E1])
            psX = [ps(f"psX{n}", [128, 2, E1 * CAP]) for n in range(2)]
            psD = [ps(f"psD{n}", [128, 2, 2, 128]) for n in range(2)]
            own_dve = Tally(sem("own_dve"))
            norm = RowNorm(nc, X, sb, signal, own_dve, passed)
            s_w, s_before = sem("loads"), sem("before")
            turned, hT_ready = signal("turned"), signal("hT_ready", 1)
            logits, biased, shifted, exped = signal("logits", 1), signal("biased", 1), signal("shifted"), signal("exped")
            chosen, counted = signal("chosen"), signal("counted")
            d_ready, dw_ready = signal("d_ready", 1), signal("dw_ready")
            gathered, stored_x = signal("gathered", 4), signal("stored_x", 2)
            dw_turned, dw_copied = signal("dw_turned", 4), signal("dw_copied", 2)
            dw_saved = [signal(f"dw_saved{n}", 16) for n in range(2)]
            block = inner.enter_context(nc.Block())

            @block.sync
            def _(sp):
                for t, name in ((wr, "wr"), (beforef, "before")):
                    sp.dma_start(t[:, :], io[name]).then_inc(s_w, 16)
                for t, name in ((br, "br"), (iota8, "iota8"), (iota20, "iota20")):
                    sp.dma_start(t[:, :], io[name].partition_broadcast(128)).then_inc(s_w, 16)
                for s in dw_saved:
                    s.credit(nc.sync)

                def step(g, gp, more):
                    sp.wait_ge(dw_copied.sem, dw_copied.at(2 * g + 2))
                    sp.sem_inc(passed, 1)
                    dst = io["dwt"][at(g)]
                    sp.dma_start(dst.squeeze(0) if isinstance(g, Lin) else dst,
                                 dwt[:, gp, :, :, :].rearrange("p a b c -> p (a b c)")).then_inc(dw_saved[gp].sem, 16)
                groups(nc.sync, step)
                for s in dw_saved:
                    sp.wait_ge(s.sem, s.at(16 * (NG // 2)))
                    sp.sem_inc(passed, 1)

            @block.tensor
            def _(pe):
                def front(g, gp):
                    pe.wait_ge(norm.done.sem, norm.done.at(g + 1))
                    pe.wait_ge(hT_ready.sem, hT_ready.at(g))
                    for r in range(G):
                        ins = nc.tensor.transpose(psH[:, r * 128:(r + 1) * 128], hn[:, gp, r, :], ident[:, :])
                    ins.then_inc(turned.sem, 1)

                pe.wait_ge(s_w, 16 * 5)
                pe.wait_ge(s_before, 1)
                for s in (logits, gathered, dw_turned):
                    s.credit(nc.tensor)
                front(0, 0)

                def step(g, gp, more):
                    pe.wait_ge(hT_ready.sem, hT_ready.at(g + 1))
                    pe.wait_ge(biased.sem, biased.at(g))
                    for r in range(G):
                        ins = nc.tensor.matmul(psL[:, r, :], hT[:, r * T:(r + 1) * T], wr[:, :], start=True,
                                               stop=True, skip_group_check=True)
                    ins.then_inc(logits.sem, 1)
                    pe.wait_ge(chosen.sem, chosen.at(g + 1))
                    pe.wait_ge(d_ready.sem, d_ready.at(g))
                    nc.tensor.matmul(psN[:, :, :], before[:, :], ohb[:, :, :], start=True,
                                     stop=True).then_inc(counted.sem, 1)
                    if more:
                        front(g + 1, 1 - gp)
                    pe.wait_ge(d_ready.sem, d_ready.at(g + 1))
                    for n in range(2):
                        pe.wait_ge(stored_x.sem, stored_x.at(2 * g + n - 1))
                        for k in range(2):
                            r = 2 * n + k
                            ins = nc.tensor.matmul(psX[n][:, k, :], hn[:, gp, r, :],
                                                   D[:, gp, r, :, :].rearrange("p e c -> p (e c)"),
                                                   start=True, stop=True, skip_group_check=True)
                        ins.then_inc(gathered.sem, 1)
                    pe.wait_ge(dw_ready.sem, dw_ready.at(g + 1))
                    for n in range(2):
                        pe.wait_ge(dw_copied.sem, dw_copied.at(2 * g + n - 1))
                        for k in range(2):
                            for f in range(2):
                                ins = nc.tensor.transpose(
                                    psD[n][0:HALF, k, f, :],
                                    Dw[:, gp, 2 * n + k, 4 * f:4 * f + 4, :].rearrange("p e c -> p (e c)"), ident[:, :])
                        ins.then_inc(dw_turned.sem, 1)
                groups(nc.tensor, step)

            @block.scalar
            def _(act):
                def front(g):
                    act.wait_ge(turned.sem, turned.at(g + 1))
                    act.wait_ge(logits.sem, logits.at(g))
                    nc.scalar.activation(hT[:, :], psH[:, :], ACT.Copy).then_inc(hT_ready.sem, 1)

                for s in (hT_ready, stored_x):
                    s.credit(nc.scalar)
                front(0)

                def step(g, gp, more):
                    act.wait_ge(shifted.sem, shifted.at(g + 1))
                    nc.scalar.activation(ex[:, :, :], dl[:, :, :], ACT.Exp).then_inc(exped.sem, 1)
                    if more:
                        front(g + 1)
                    for n in range(2):
                        act.wait_ge(gathered.sem, gathered.at(2 * g + n + 1))
                        act.sem_inc(passed, 1)
                        b0 = g * G + 2 * n
                        for k in range(2):
                            dst = XG[:, :, at(b0 + k), :]
                            src = psX[n][:, k, :].rearrange("p (e c) -> p e c", e=E1)
                            if isinstance(g, Lin):
                                src = src.unsqueeze(2)
                            ins = nc.scalar.activation(dst, src, ACT.Copy)
                        ins.then_inc(stored_x.sem, 1)
                groups(nc.scalar, step)

            @block.gpsimd
            def _(pool):
                norm.start(pool)
                norm.root(pool, 0)

                def step(g, gp, more):
                    if more:
                        norm.root(pool, g + 1)
                groups(nc.gpsimd, step)

            @block.vector
            def _(dve):
                def wide(t):
                    return t[:, :].unsqueeze(1).to_broadcast([128, G, E1])

                def each(t):
                    return t.to_broadcast([128, G, E1])

                def copy_dw(g, gp):
                    for n in range(2):
                        dve.wait_ge(dw_turned.sem, dw_turned.at(2 * g + n + 1))
                        if n == 0:
                            dve.wait_ge(dw_saved[gp].sem, dw_saved[gp].at(16 * (parity_count(g, gp) - 1)))
                        nc.vector.tensor_copy(dwt[:, gp, 2 * n:2 * n + 2, :, :],
                                              psD[n][0:HALF, :, :, :]).then_inc(dw_copied.sem, 1)

                dve.wait_ge(s_w, 16 * 5)
                nc.vector.tensor_copy(before[:, :], beforef[:, :]).then_inc(s_before, 1)
                for s in (biased, d_ready, dw_copied):
                    s.credit(nc.vector)
                norm.take_stats(dve, 0)
                norm.apply(dve, 0, hn[:, 0, :, :])

                def step(g, gp, more):
                    dve.wait_ge(logits.sem, logits.at(g + 1))
                    nc.vector.tensor_tensor(lg[:, :, :], psL[:, :, :], wide(br), ALU.add).then_inc(biased.sem, 1)
                    dve.wait_ge(biased.sem, biased.at(g + 1))
                    dve.sem_inc(passed, 1)
                    for r in range(G):
                        nc.vector.max(out=mx8[:, r, :], in_=lg[:, r, :]).then_inc(own_dve.sem, own_dve.one())
                    dve.wait_ge(own_dve.sem, own_dve.value())
                    if isinstance(g, Lin):
                        dve.sem_inc(passed, 1)
                    for r in range(G):
                        nc.vector.max_index(ix8[:, r, :], mx8[:, r, :], lg[:, r, :]).then_inc(
                            own_dve.sem, own_dve.one())
                    nc.vector.tensor_tensor(dl[:, :, :], lg[:, :, :], each(mx8[:, :, 0:1]),
                                            ALU.subtract).then_inc(shifted.sem, 1)
                    dve.wait_ge(own_dve.sem, own_dve.value())
                    nc.vector.tensor_copy(ixf[:, :, :], ix8[:, :, 0:2]).then_inc(own_dve.sem, own_dve.one())
                    dve.wait_ge(own_dve.sem, own_dve.value())
                    nc.vector.tensor_tensor(oh0[:, :, :], wide(iota8), each(ixf[:, :, 0:1]), ALU.is_equal).then_inc(
                        own_dve.sem, own_dve.one())
                    nc.vector.tensor_tensor(oh1[:, :, :], wide(iota8), each(ixf[:, :, 1:2]), ALU.is_equal).then_inc(
                        own_dve.sem, own_dve.one())
                    dve.wait_ge(own_dve.sem, own_dve.value())
                    nc.vector.tensor_tensor(oh[:, :, :], oh0[:, :, :], oh1[:, :, :], ALU.add).then_inc(
                        own_dve.sem, own_dve.one())
                    dve.wait_ge(own_dve.sem, own_dve.value())
                    nc.vector.tensor_copy(ohb[:, :, :], oh[:, :, :]).then_inc(chosen.sem, 1)
                    if more:
                        norm.take_stats(dve, g + 1)
                    dve.wait_ge(exped.sem, exped.at(g + 1))
                    nc.vector.tensor_reduce(sm[:, :], ex[:, :, :], AX.X, ALU.add).then_inc(own_dve.sem, own_dve.one())
                    dve.wait_ge(own_dve.sem, own_dve.value())
                    nc.vector.reciprocal(rs[:, :], sm[:, :]).then_inc(own_dve.sem, own_dve.one())
                    dve.wait_ge(own_dve.sem, own_dve.value())
                    nc.vector.tensor_tensor(gw[:, :, :], ex[:, :, :], each(rs[:, :].unsqueeze(2)), ALU.mult).then_inc(
                        own_dve.sem, own_dve.one())
                    dve.wait_ge(own_dve.sem, own_dve.value())
                    nc.vector.tensor_tensor(gw[:, :, :], gw[:, :, :], oh[:, :, :], ALU.mult).then_inc(
                        own_dve.sem, own_dve.one())
                    dve.wait_ge(own_dve.sem, own_dve.value())
                    dve.wait_ge(counted.sem, counted.at(g + 1))
                    nc.vector.scalar_tensor_tensor(out=qp[:, :, :], in0=psN[:, :, :], scalar=1.0,
                                                        in1=oh[:, :, :], op0=ALU.add, op1=ALU.mult).then_inc(
                                                            own_dve.sem, own_dve.one())
                    dve.wait_ge(own_dve.sem, own_dve.value())
                    dve.wait_ge(gathered.sem, gathered.at(2 * g - 2))
                    slots = iota20[:, :].unsqueeze(1).to_broadcast([128, G * E1, CAP])
                    nc.vector.tensor_tensor(D[:, gp, :, :, :].rearrange("p a e c -> p (a e) c"), slots,
                                            qp[:, :, :].rearrange("p a e -> p (a e)").unsqueeze(2)
                                            .to_broadcast([128, G * E1, CAP]), ALU.is_equal).then_inc(d_ready.sem, 1)
                    dve.wait_ge(d_ready.sem, d_ready.at(g + 1))
                    dve.wait_ge(dw_turned.sem, dw_turned.at(2 * g - 2))
                    nc.vector.tensor_tensor(Dw[:, gp, :, :, :].rearrange("p a e c -> p (a e) c"),
                                            D[:, gp, :, :, :].rearrange("p a e c -> p (a e) c"),
                                            gw[:, :, :].rearrange("p a e -> p (a e)").unsqueeze(2)
                                            .to_broadcast([128, G * E1, CAP]), ALU.mult).then_inc(dw_ready.sem, 1)
                    if more:
                        dve.wait_ge(gathered.sem, gathered.at(2 * g))
                        norm.apply(dve, g + 1, hn[:, 1 - gp, :, :])
                    copy_dw(g, gp)
                groups(nc.vector, step, own_dve, 2 * (G + G + 4 + 4 + 1 + G))

        with ExitStack() as inner:
            ctx2, sb, ps, sem, signal = scope(nc, "rb_")
            inner.enter_context(ctx2)
            N2 = B // 2 * CAP
            w1, w2 = sb("w1", [128, 2, HID]), sb("w2", [128, 2, NJ, 128])
            b1, b2 = sb("b1", [128, E1 * NJ]), sb("b2", [128, E1])
            hid = sb("hid", [128, 2, NJ, N2])
            psF = [ps(f"psF{n}", [128, 512]) for n in range(NJ)]
            psY = [ps(f"psY{n}", [128, 512]) for n in range(2)]
            s_b = sem("biases")
            w_ready = [signal(f"w_ready{n}") for n in range(2)]
            first_done, relu_done = signal("first", 4), signal("relu", 4)
            second_done, y_taken = signal("second", 2), signal("y_taken", 2)
            block = inner.enter_context(nc.Block())

            @block.sync
            def _(sp):
                sp.dma_start(b1[:, :], io["b1T"]).then_inc(s_b, 16)
                sp.dma_start(b2[:, :], io["b2T"]).then_inc(s_b, 16)

                def load(e, gp):
                    a1, a2 = io["w1"][at(e)], io["w2"][at(e)]
                    if isinstance(e, Lin):
                        a1, a2 = a1.squeeze(0), a2.squeeze(0)
                    sp.dma_start(w1[:, gp, :], a1).then_inc(w_ready[gp].sem, 16)
                    sp.dma_start(w2[:, gp, :, :], a2.rearrange("(j p) c -> p j c", p=128)).then_inc(w_ready[gp].sem, 16)

                load(0, 0)

                def step(e, gp, more):
                    sp.wait_ge(second_done.sem, second_done.at(2 * e))
                    sp.sem_inc(passed, 1)
                    if more:
                        load(e + 1, 1 - gp)
                groups(nc.sync, step, pairs=E1 // 2)

            @block.tensor
            def _(pe):
                for s in (first_done, second_done):
                    s.credit(nc.tensor)

                def step(e, gp, more):
                    pe.wait_ge(w_ready[gp].sem, w_ready[gp].at(32 * parity_count(e, gp)))
                    for q in range(2):
                        n = 2 * e + q
                        for j in range(NJ):
                            pe.wait_ge(relu_done.sem, relu_done.at(NJ * n + j - 3))
                            rhs = XG[:, at(e), q * B // 2:(q + 1) * B // 2, :]
                            rhs = rhs.rearrange("p a b c -> p (a b c)") if isinstance(e, Lin) \
                                else rhs.rearrange("p b c -> p (b c)")
                            nc.tensor.matmul(psF[j][:, 0:N2], w1[:, gp, j * 128:(j + 1) * 128], rhs,
                                             start=True, stop=True).then_inc(first_done.sem, 1)
                        pe.wait_ge(y_taken.sem, y_taken.at(n - 1))
                        for j in range(NJ):
                            pe.wait_ge(relu_done.sem, relu_done.at(NJ * n + j + 1))
                            ins = nc.tensor.matmul(psY[q][:, 0:N2], w2[:, gp, j, :], hid[:, q, j, :],
                                                   start=(j == 0), stop=(j == NJ - 1))
                        ins.then_inc(second_done.sem, 1)
                groups(nc.tensor, step, pairs=E1 // 2)

            @block.scalar
            def _(act):
                act.wait_ge(s_b, 32)
                relu_done.credit(nc.scalar)

                def step(e, gp, more):
                    for q in range(2):
                        n = 2 * e + q
                        for j in range(NJ):
                            act.wait_ge(first_done.sem, first_done.at(NJ * n + j + 1))
                            if j == 0:
                                act.wait_ge(second_done.sem, second_done.at(n - 1))
                            act.sem_inc(passed, 1)
                            nc.scalar.activation(hid[:, q, j, :], psF[j][:, 0:N2], ACT.Relu,
                                                 bias=b1[:, at1(NJ * e + j)]).then_inc(relu_done.sem, 1)
                groups(nc.scalar, step, pairs=E1 // 2)

            @block.vector
            def _(dve):
                dve.wait_ge(s_b, 32)
                y_taken.credit(nc.vector)

                def step(e, gp, more):
                    for q in range(2):
                        n = 2 * e + q
                        dve.wait_ge(second_done.sem, second_done.at(n + 1))
                        dst = XG[:, at(e), q * B // 2:(q + 1) * B // 2, :]
                        dst = dst.rearrange("p a b c -> p (a b c)") if isinstance(e, Lin) \
                            else dst.rearrange("p b c -> p (b c)")
                        nc.vector.tensor_scalar(dst, psY[q][:, 0:N2], b2[:, at1(e)], None,
                                                ALU.add).then_inc(y_taken.sem, 1)
                groups(nc.vector, step, pairs=E1 // 2)

        with ExitStack() as inner:
            ctx2, sb, ps, sem, signal = scope(nc, "rc_")
            inner.enter_context(ctx2)
            dwt = sb("dwt", [HALF, 2, G, 2, 128])
            ys = sb("ys", [128, 2, G, E1, CAP])
            yv = sb("yv", [HALF, 2, G, 2, 128])
            psV = [ps(f"psV{n}", [128, 2, 2, 128]) for n in range(4)]
            psO = [ps(f"psO{n}", [128, G, 128]) for n in range(2)]
            loaded = [signal(f"loaded{n}") for n in range(2)]
            staged = signal("staged")
            turned, copied = signal("turned", 4), signal("copied", 4)
            mixed, added = signal("mixed", 2), signal("added", 2)
            block = inner.enter_context(nc.Block())

            @block.sync
            def _(sp):
                def load(g, gp):
                    src = io["dwt"][at(g)]
                    sp.dma_start(dwt[:, gp, :, :, :].rearrange("p a b c -> p (a b c)"),
                                 src.squeeze(0) if isinstance(g, Lin) else src).then_inc(loaded[gp].sem, 16)
                load(0, 0)

                def step(g, gp, more):
                    sp.wait_ge(mixed.sem, mixed.at(g))
                    sp.sem_inc(passed, 1)
                    if more:
                        load(g + 1, 1 - gp)
                groups(nc.sync, step)

            @block.gpsimd
            def _(pool):
                def step(g, gp, more):
                    pool.wait_ge(turned.sem, turned.at(2 * g - 2))
                    pool.sem_inc(passed, 1)
                    src = XG[:, :, span(g, G), :].rearrange("p e b c -> p b e c")
                    nc.gpsimd.tensor_copy(ys[:, gp, :, :, :], src).then_inc(staged.sem, 1)
                groups(nc.gpsimd, step)

            @block.tensor
            def _(pe):
                def front(g, gp):
                    pe.wait_ge(staged.sem, staged.at(g + 1))
                    for n in range(2):
                        pe.wait_ge(copied.sem, copied.at(2 * g + n - 3))
                        for k in range(2):
                            for f in range(2):
                                ins = nc.tensor.transpose(
                                    psV[2 * gp + n][0:HALF, k, f, :],
                                    ys[:, gp, 2 * n + k, 4 * f:4 * f + 4, :].rearrange("p e c -> p (e c)"), ident[:, :])
                        ins.then_inc(turned.sem, 1)

                for s in (turned, mixed):
                    s.credit(nc.tensor)
                front(0, 0)

                def step(g, gp, more):
                    if more:
                        front(g + 1, 1 - gp)
                    pe.wait_ge(copied.sem, copied.at(2 * g + 2))
                    pe.wait_ge(loaded[gp].sem, loaded[gp].at(16 * parity_count(g, gp)))
                    pe.wait_ge(added.sem, added.at(g - 1))
                    for r in range(G):
                        for f in range(2):
                            ins = nc.tensor.matmul(psO[gp][:, r, :], dwt[:, gp, r, f, :], yv[:, gp, r, f, :],
                                                   start=(f == 0), stop=(f == 1), skip_group_check=True)
                    ins.then_inc(mixed.sem, 1)
                groups(nc.tensor, step)

            @block.scalar
            def _(act):
                copied.credit(nc.scalar)

                def step(g, gp, more):
                    act.wait_ge(mixed.sem, mixed.at(g - 1))
                    for n in range(2):
                        act.wait_ge(turned.sem, turned.at(2 * g + n + 1))
                        nc.scalar.activation(yv[:, gp, 2 * n:2 * n + 2, :, :], psV[2 * gp + n][0:HALF, :, :, :],
                                             ACT.Copy).then_inc(copied.sem, 1)
                groups(nc.scalar, step)

            @block.vector
            def _(dve):
                added.credit(nc.vector)

                def step(g, gp, more):
                    dve.wait_ge(mixed.sem, mixed.at(g + 1))
                    nc.vector.tensor_tensor(X[:, span(g, G), :], X[:, span(g, G), :], psO[gp][:, :, :],
                                            ALU.add).then_inc(added.sem, 1)
                groups(nc.vector, step)


def at1(n):
    return bass.ds(n.value(), 1) if isinstance(n, Lin) else slice(n, n + 1)


def sequence_attention(nc, X, io, consts):
    ident, passed = consts["ident"], consts["passed"]
    PL = 4
    BLK = 4
    SC = C ** -0.5
    with ExitStack() as outer:
        ctx0, sb, ps, sem, signal = scope(nc, "s_")
        outer.enter_context(ctx0)
        HT = sb("HT", [128, B, T])
        GTt = sb("GTt", [128, B, T])

        with ExitStack() as inner:
            ctx1, sb, ps, sem, signal = scope(nc, "sa_")
            inner.enter_context(ctx1)
            wq, wk, gm = sb("wq", [128, 128]), sb("wk", [128, 128]), sb("gm", [128, 128])
            hn, hT = sb("hn", [128, 2, G, 128]), sb("hT", [128, 2, GT])
            psH = [ps(f"psH{n}", [128, GT]) for n in range(2)]
            psG = [ps(f"psG{n}", [128, GT]) for n in range(2)]
            psW = ps("psW", [128, 128])
            own_dve = Tally(sem("own_dve"))
            norm = RowNorm(nc, X, sb, signal, own_dve, passed)
            s_w, s_gm = sem("loads"), sem("gm")
            turned, hT_ready = signal("turned", 1), signal("hT_ready", 2)
            projected, kept = signal("projected", 2), signal("kept", 2)
            block = inner.enter_context(nc.Block())

            @block.sync
            def _(sp):
                sp.dma_start(wq[:, :], io["s_wq"]).then_inc(s_w, 16)
                sp.dma_start(wk[:, :], io["s_wk"]).then_inc(s_w, 16)

            @block.gpsimd
            def _(pool):
                norm.start(pool)
                norm.root(pool, 0)

                def step(g, gp, more):
                    if more:
                        norm.root(pool, g + 1)
                    pool.wait_ge(hT_ready.sem, hT_ready.at(g + 1))
                    pool.sem_inc(passed, 1)
                    src = hT[:, gp, :].rearrange("p (b t) -> p b t", b=G)
                    nc.gpsimd.tensor_copy(HT[:, span(g, G), :], src).then_inc(kept.sem, 1)
                kept.credit(nc.gpsimd)
                groups(nc.gpsimd, step)

            @block.vector
            def _(dve):
                norm.take_stats(dve, 0)
                norm.apply(dve, 0, hn[:, 0, :, :])
                dve.wait_ge(s_gm, 1)
                nc.vector.tensor_copy(gm[:, :], psW[:, :]).then_inc(s_gm, 1)

                def step(g, gp, more):
                    if more:
                        norm.take_stats(dve, g + 1)
                        dve.wait_ge(turned.sem, turned.at(g))
                        norm.apply(dve, g + 1, hn[:, 1 - gp, :, :])
                groups(nc.vector, step, own_dve, 2 * G)

            @block.tensor
            def _(pe):
                pe.wait_ge(s_w, 32)
                nc.tensor.matmul(psW[:, :], wq[:, :], wk[:, :], start=True, stop=True).then_inc(s_gm, 1)
                pe.wait_ge(s_gm, 2)
                for s in (turned, projected):
                    s.credit(nc.tensor)

                def front(g, gp):
                    pe.wait_ge(norm.done.sem, norm.done.at(g + 1))
                    pe.wait_ge(hT_ready.sem, hT_ready.at(g - 1))
                    for r in range(G):
                        ins = nc.tensor.transpose(psH[gp][:, r * 128:(r + 1) * 128], hn[:, gp, r, :], ident[:, :])
                    ins.then_inc(turned.sem, 1)
                front(0, 0)

                def step(g, gp, more):
                    if more:
                        front(g + 1, 1 - gp)
                    pe.wait_ge(hT_ready.sem, hT_ready.at(g + 1))
                    nc.tensor.matmul(psG[gp][:, :], gm[:, :], hT[:, gp, :], start=True,
                                     stop=True).then_inc(projected.sem, 1)
                groups(nc.tensor, step)

            @block.scalar
            def _(act):
                def front(g, gp):
                    act.wait_ge(turned.sem, turned.at(g + 1))
                    act.wait_ge(projected.sem, projected.at(g - 1))
                    act.wait_ge(kept.sem, kept.at(g - 1))
                    nc.scalar.activation(hT[:, gp, :], psH[gp][:, :], ACT.Copy).then_inc(hT_ready.sem, 1)

                def keep(g, gp):
                    act.wait_ge(projected.sem, projected.at(g + 1))
                    act.sem_inc(passed, 1)
                    src = psG[gp][:, :].rearrange("p (b t) -> p b t", b=G)
                    nc.scalar.activation(GTt[:, span(g, G), :], src, ACT.Copy)
                hT_ready.credit(nc.scalar)
                front(0, 0)

                def step(g, gp, more):
                    keep(g, gp)
                    if more:
                        front(g + 1, 1 - gp)
                groups(nc.scalar, step)

        with ExitStack() as inner:
            ctx1, sb, ps, sem, signal = scope(nc, "sb_")
            inner.enter_context(ctx1)
            mask = sb("mask", [128, 128])
            hs, hv = sb("hs", [128, 2, BLK, 128]), sb("hv", [128, 2, BLK, 129])
            th, ex, em = sb("th", [128, BLK, 128]), sb("ex", [128, BLK, 128]), sb("em", [128, 2, BLK, 128])
            rd, on = sb("rd", [128, BLK]), sb("on", [128, 2, BLK, 128])
            psV, psS = ps("psV", [128, BLK, 128]), ps("psS", [128, BLK, 128])
            psO = [ps(f"psO{n}", [128, 2, 256]) for n in range(2)]
            psT = ps("psT", [128, BLK, 128])
            own_dve = Tally(sem("own_dve"))
            s_w, s_one = sem("loads"), sem("ones")
            staged, turned, hv_ready = signal("staged"), signal("turned", 2), signal("hv_ready", 1)
            scored, tanh_done, exp_done = signal("scored", 2), signal("tanh", 1), signal("exp", 1)
            masked, weighed, normed = signal("masked", 1), signal("weighed", 3), signal("normed", 1)
            back, back_done = signal("back", 2), signal("back_done", 1)
            block = inner.enter_context(nc.Block())

            def places(t, g):
                w = BLK * PL
                return t[:, :, span(g, w)].rearrange("p b (k q) -> p k b q", q=PL)

            @block.sync
            def _(sp):
                sp.dma_start(mask[:, :], io["same_place"]).then_inc(s_w, 16)

            @block.gpsimd
            def _(pool):
                pool.wait_ge(s_w, 16)
                def step(g, gp, more):
                    pool.wait_ge(scored.sem, scored.at(g - 1))
                    pool.sem_inc(passed, 1)
                    nc.gpsimd.tensor_copy(hs[:, gp, :, :].rearrange("p k (b q) -> p k b q", q=PL),
                                          places(HT, g)).then_inc(staged.sem, 1)
                groups(nc.gpsimd, step)

            @block.tensor
            def _(pe):
                for s in (turned, scored, weighed, back):
                    s.credit(nc.tensor)

                def front(g, gp):
                    pe.wait_ge(staged.sem, staged.at(g + 1))
                    pe.wait_ge(hv_ready.sem, hv_ready.at(g))
                    for k in range(BLK):
                        ins = nc.tensor.transpose(psV[:, k, :], hs[:, gp, k, :], ident[:, :])
                    ins.then_inc(turned.sem, 1)
                    pe.wait_ge(tanh_done.sem, tanh_done.at(g))
                    for k in range(BLK):
                        gt = GTt[:, :, span_at(g, BLK * PL, k * PL, PL)]
                        ins = nc.tensor.matmul(psS[:, k, :].rearrange("p (b q) -> p b q", q=PL), hs[:, gp, k, :], gt,
                                               start=True, stop=True, skip_group_check=True)
                    ins.then_inc(scored.sem, 1)

                front(0, 0)
                pe.wait_ge(s_one, 1)

                def step(g, gp, more):
                    if more:
                        front(g + 1, 1 - gp)
                    pe.wait_ge(masked.sem, masked.at(g + 1))
                    pe.wait_ge(hv_ready.sem, hv_ready.at(g + 1))
                    pe.wait_ge(normed.sem, normed.at(g))
                    for k in range(BLK):
                        ins = nc.tensor.matmul(psO[k // 2][:, k % 2, 0:129], em[:, gp, k, :], hv[:, gp, k, :],
                                               start=True, stop=True, skip_group_check=True)
                    ins.then_inc(weighed.sem, 1)
                    pe.wait_ge(normed.sem, normed.at(g + 1))
                    pe.wait_ge(back_done.sem, back_done.at(g))
                    for k in range(BLK):
                        ins = nc.tensor.transpose(psT[:, k, :], on[:, gp, k, :], ident[:, :])
                    ins.then_inc(back.sem, 1)
                groups(nc.tensor, step)

            @block.scalar
            def _(act):
                for s in (hv_ready, tanh_done, exp_done, back_done):
                    s.credit(nc.scalar)

                def front(g, gp):
                    act.wait_ge(turned.sem, turned.at(g + 1))
                    act.wait_ge(weighed.sem, weighed.at(g - 1))
                    nc.scalar.activation(hv[:, gp, :, 0:128], psV[:, :, :], ACT.Copy).then_inc(hv_ready.sem, 1)
                    act.wait_ge(scored.sem, scored.at(g + 1))
                    act.wait_ge(exp_done.sem, exp_done.at(g))
                    nc.scalar.activation(th[:, :, :], psS[:, :, :], ACT.Tanh, scale=SC).then_inc(tanh_done.sem, 1)
                    act.wait_ge(tanh_done.sem, tanh_done.at(g + 1))
                    act.wait_ge(masked.sem, masked.at(g))
                    nc.scalar.activation(ex[:, :, :], th[:, :, :], ACT.Exp).then_inc(exp_done.sem, 1)
                front(0, 0)

                def step(g, gp, more):
                    if more:
                        front(g + 1, 1 - gp)
                    act.wait_ge(back.sem, back.at(g + 1))
                    act.sem_inc(passed, 1)
                    nc.scalar.activation(places(HT, g), psT[:, :, :].rearrange("p k (b q) -> p k b q", q=PL),
                                         ACT.Copy).then_inc(back_done.sem, 1)
                groups(nc.scalar, step)

            @block.vector
            def _(dve):
                nc.vector.memset(hv[:, :, :, 128:129], 1.0).then_inc(s_one, 1)
                dve.wait_ge(s_w, 16)
                for s in (masked, normed):
                    s.credit(nc.vector)

                def front(g, gp):
                    dve.wait_ge(exp_done.sem, exp_done.at(g + 1))
                    dve.wait_ge(weighed.sem, weighed.at(g - 1))
                    nc.vector.tensor_tensor(em[:, gp, :, :], ex[:, :, :],
                                            mask[:, :].unsqueeze(1).to_broadcast([128, BLK, 128]),
                                            ALU.mult).then_inc(masked.sem, 1)
                front(0, 0)

                def step(g, gp, more):
                    if more:
                        front(g + 1, 1 - gp)
                    dve.wait_ge(weighed.sem, weighed.at(g + 1))
                    for n in range(2):
                        nc.vector.reciprocal(rd[:, 2 * n:2 * n + 2], psO[n][:, :, 128]).then_inc(
                            own_dve.sem, own_dve.one())
                    dve.wait_ge(own_dve.sem, own_dve.value())
                    dve.wait_ge(back.sem, back.at(g - 1))
                    for k in range(BLK):
                        ins = nc.vector.tensor_scalar(on[:, gp, k, :], psO[k // 2][:, k % 2, 0:128], rd[:, k:k + 1],
                                                      None, ALU.mult)
                    ins.then_inc(normed.sem, 1)
                groups(nc.vector, step, own_dve, 2 * 2)

        with ExitStack() as inner:
            ctx1, sb, ps, sem, signal = scope(nc, "sc_")
            inner.enter_context(ctx1)
            os_ = sb("os", [128, 2, G, 128])
            psB = [ps(f"psB{n}", [128, G, 128]) for n in range(2)]
            staged, turned, added = signal("staged"), signal("turned", 2), signal("added", 2)
            block = inner.enter_context(nc.Block())

            @block.gpsimd
            def _(pool):
                def step(g, gp, more):
                    pool.wait_ge(turned.sem, turned.at(g - 1))
                    pool.sem_inc(passed, 1)
                    nc.gpsimd.tensor_copy(os_[:, gp, :, :], HT[:, span(g, G), :]).then_inc(staged.sem, 1)
                groups(nc.gpsimd, step)

            @block.tensor
            def _(pe):
                turned.credit(nc.tensor)

                def step(g, gp, more):
                    pe.wait_ge(staged.sem, staged.at(g + 1))
                    pe.wait_ge(added.sem, added.at(g - 1))
                    for r in range(G):
                        ins = nc.tensor.transpose(psB[gp][:, r, :], os_[:, gp, r, :], ident[:, :])
                    ins.then_inc(turned.sem, 1)
                groups(nc.tensor, step)

            @block.vector
            def _(dve):
                added.credit(nc.vector)

                def step(g, gp, more):
                    dve.wait_ge(turned.sem, turned.at(g + 1))
                    nc.vector.tensor_tensor(X[:, span(g, G), :], X[:, span(g, G), :], psB[gp][:, :, :],
                                            ALU.add).then_inc(added.sem, 1)
                groups(nc.vector, step)


def span_at(n, width, offset, size):
    return bass.ds((n * width + offset).value(), size) if isinstance(n, Lin) \
        else slice(n * width + offset, n * width + offset + size)


def context_attention(nc, X, io, consts):
    ident, passed = consts["ident"], consts["passed"]
    SC = C ** -0.5
    ctx, sb, ps, sem, signal = scope(nc, "x_")
    with ctx:
        wq, wk, wv, gm = (sb(n, [128, 128]) for n in ("wq", "wk", "wv", "gm"))
        hn, hT, gT = sb("hn", [128, G, 128]), sb("hT", [128, GT]), sb("gT", [128, GT])
        cT = sb("cT", [128, 2, GT])
        vv = sb("vv", [128, 2, G, 128])
        mx, nm, sm, rs = (sb(n, [128, G]) for n in ("mx", "nm", "sm", "rs"))
        P, PT = sb("P", [128, G, 128]), sb("PT", [128, G, 128])
        psH, psG, psV, psS = (ps(n, [128, GT]) for n in ("psH", "psG", "psV", "psS"))
        psP, psO = ps("psP", [128, GT]), ps("psO", [128, GT])
        own_dve = Tally(sem("own_dve"))
        norm = RowNorm(nc, X, sb, signal, own_dve, passed)
        s_w, s_gm = sem("loads"), sem("gm")
        c_ready = [signal(f"ctx{n}") for n in range(2)]
        turned, hT_ready = signal("turned"), signal("hT_ready", 1)
        projected, gT_ready = signal("projected", 1), signal("gT_ready", 1)
        v_done, v_ready = signal("v_done"), signal("v_ready", 1)
        scored, maxed, exped = signal("scored", 1), signal("maxed"), signal("exp", 1)
        p_turned, p_copied = signal("p_turned", 1), signal("p_copied", 1)
        weighed, added = signal("weighed", 2), signal("added", 1)
        block = ctx.enter_context(nc.Block())

        @block.sync
        def _(sp):
            for t, name in ((wq, "x_wq"), (wk, "x_wk"), (wv, "x_wv")):
                sp.dma_start(t[:, :], io[name]).then_inc(s_w, 16)

            def load(g, gp):
                sp.dma_start(cT[:, gp, :], io["ctxT"][:, span(g, GT)]).then_inc(c_ready[gp].sem, 16)
            load(0, 0)

            def step(g, gp, more):
                sp.wait_ge(scored.sem, scored.at(g))
                sp.sem_inc(passed, 1)
                if more:
                    load(g + 1, 1 - gp)
            groups(nc.sync, step)

        @block.gpsimd
        def _(pool):
            norm.start(pool)
            norm.root(pool, 0)

            def step(g, gp, more):
                if more:
                    norm.root(pool, g + 1)
            groups(nc.gpsimd, step)

        @block.tensor
        def _(pe):
            def front(g, gp):
                pe.wait_ge(norm.done.sem, norm.done.at(g + 1))
                pe.wait_ge(hT_ready.sem, hT_ready.at(g))
                for r in range(G):
                    ins = nc.tensor.transpose(psH[:, r * 128:(r + 1) * 128], hn[:, r, :], ident[:, :])
                ins.then_inc(turned.sem, 1)

            pe.wait_ge(s_w, 16 * 3)
            nc.tensor.matmul(psG[:, 0:128], wq[:, :], wk[:, :], start=True, stop=True).then_inc(s_gm, 1)
            for s in (projected, scored, p_turned, weighed):
                s.credit(nc.tensor)
            front(0, 0)
            pe.wait_ge(s_gm, 2)

            def step(g, gp, more):
                pe.wait_ge(c_ready[gp].sem, c_ready[gp].at(16 * parity_count(g, gp)))
                pe.wait_ge(v_ready.sem, v_ready.at(g))
                for r in range(G):
                    ins = nc.tensor.matmul(psV[:, r * 128:(r + 1) * 128], cT[:, gp, r * T:(r + 1) * T], wv[:, :],
                                           start=True, stop=True, skip_group_check=True)
                ins.then_inc(v_done.sem, 1)
                pe.wait_ge(hT_ready.sem, hT_ready.at(g + 1))
                pe.wait_ge(gT_ready.sem, gT_ready.at(g))
                nc.tensor.matmul(psG[:, :], gm[:, :], hT[:, :], start=True, stop=True).then_inc(projected.sem, 1)
                if more:
                    front(g + 1, 1 - gp)
                pe.wait_ge(gT_ready.sem, gT_ready.at(g + 1))
                pe.wait_ge(exped.sem, exped.at(g))
                for r in range(G):
                    ins = nc.tensor.matmul(psS[:, r * 128:(r + 1) * 128], gT[:, r * T:(r + 1) * T],
                                           cT[:, gp, r * T:(r + 1) * T], start=True, stop=True, skip_group_check=True)
                ins.then_inc(scored.sem, 1)
                pe.wait_ge(exped.sem, exped.at(g + 1))
                pe.wait_ge(p_copied.sem, p_copied.at(g))
                for r in range(G):
                    ins = nc.tensor.transpose(psP[:, r * 128:(r + 1) * 128], P[:, r, :], ident[:, :])
                ins.then_inc(p_turned.sem, 1)
                pe.wait_ge(p_copied.sem, p_copied.at(g + 1))
                pe.wait_ge(v_ready.sem, v_ready.at(g + 1))
                pe.wait_ge(added.sem, added.at(g))
                for r in range(G):
                    ins = nc.tensor.matmul(psO[:, r * 128:(r + 1) * 128], PT[:, r, :], vv[:, gp, r, :],
                                           start=True, stop=True, skip_group_check=True)
                ins.then_inc(weighed.sem, 1)
            groups(nc.tensor, step)

        @block.scalar
        def _(act):
            def front(g):
                act.wait_ge(turned.sem, turned.at(g + 1))
                act.wait_ge(projected.sem, projected.at(g))
                nc.scalar.activation(hT[:, :], psH[:, :], ACT.Copy).then_inc(hT_ready.sem, 1)

            for s in (hT_ready, exped, p_copied, v_ready):
                s.credit(nc.scalar)
            front(0)

            def step(g, gp, more):
                act.wait_ge(v_done.sem, v_done.at(g + 1))
                act.wait_ge(weighed.sem, weighed.at(g - 1))
                nc.scalar.activation(vv[:, gp, :, :].rearrange("p r c -> p (r c)"), psV[:, :],
                                     ACT.Copy).then_inc(v_ready.sem, 1)
                if more:
                    front(g + 1)
                act.wait_ge(maxed.sem, maxed.at(g + 1))
                act.wait_ge(p_turned.sem, p_turned.at(g))
                act.wait_ge(added.sem, added.at(g))
                for r in range(G):
                    ins = nc.scalar.activation(P[:, r, :], psS[:, r * 128:(r + 1) * 128], ACT.Exp,
                                               bias=nm[:, r:r + 1], scale=SC, accum_out=sm[:, r:r + 1])
                ins.then_inc(exped.sem, 1)
                act.wait_ge(p_turned.sem, p_turned.at(g + 1))
                nc.scalar.activation(PT[:, :, :].rearrange("p r c -> p (r c)"), psP[:, :],
                                     ACT.Copy).then_inc(p_copied.sem, 1)
            groups(nc.scalar, step)

        @block.vector
        def _(dve):
            norm.take_stats(dve, 0)
            norm.apply(dve, 0, hn[:, :, :])
            dve.wait_ge(s_gm, 1)
            nc.vector.tensor_copy(gm[:, :], psG[:, 0:128]).then_inc(s_gm, 1)
            for s in (gT_ready, added):
                s.credit(nc.vector)

            def step(g, gp, more):
                dve.wait_ge(projected.sem, projected.at(g + 1))
                dve.wait_ge(scored.sem, scored.at(g))
                nc.vector.tensor_copy(gT[:, :], psG[:, :]).then_inc(gT_ready.sem, 1)
                if more:
                    norm.take_stats(dve, g + 1)
                    norm.apply(dve, g + 1, hn[:, :, :])
                dve.wait_ge(scored.sem, scored.at(g + 1))
                nc.vector.tensor_reduce(mx[:, :], psS[:, :].rearrange("p (r k) -> p r k", r=G),
                                                     AX.X, ALU.max).then_inc(own_dve.sem, own_dve.one())
                dve.wait_ge(own_dve.sem, own_dve.value())
                dve.wait_ge(exped.sem, exped.at(g))
                nc.vector.tensor_scalar(nm[:, :], mx[:, :], -SC, None, ALU.mult).then_inc(maxed.sem, 1)
                dve.wait_ge(exped.sem, exped.at(g + 1))
                nc.vector.reciprocal(rs[:, :], sm[:, :]).then_inc(own_dve.sem, own_dve.one())
                dve.wait_ge(own_dve.sem, own_dve.value())
                dve.wait_ge(weighed.sem, weighed.at(g + 1))
                for r in range(G):
                    xb = X[:, at(G * g + r), :]
                    ins = nc.vector.scalar_tensor_tensor(
                        out=xb, in0=psO[:, r * 128:(r + 1) * 128].unsqueeze(1) if isinstance(g, Lin)
                        else psO[:, r * 128:(r + 1) * 128],
                        scalar=rs[:, r:r + 1], in1=xb, op0=ALU.mult, op1=ALU.add)
                ins.then_inc(added.sem, 1)
            groups(nc.vector, step, own_dve, 2 * (G + 2))


def experts_chosen(nc, X, io, consts):
    passed = consts["passed"]
    N, SL = io["cw"].shape[0], io["idx"].shape[0]
    NT, NA = N // 128, SL // 128
    ctx, sb, ps, sem, signal = scope(nc, "e_")
    with ctx:
        w1, w2 = sb("w1", [128, 2, HID]), sb("w2", [128, 2, NJ, 128])
        b1, b2 = sb("b1", [128, E1 * NJ]), sb("b2", [128, E1, 128])
        cw = sb("cw", [128, NT, E1])
        cwr = sb("cwr", [128, NT, E1])
        cwp = sb("cwp", [128, NT, 3, E1], BF16)
        idi, idf = sb("idi", [128, NA, E1], I32), sb("idf", [128, E1, NA])
        idb = sb("idb", [128, E1, SL], I32)
        idc = sb("idc", [128, 2, NA])
        tokid, iotaN = sb("tokid", [128, NT]), sb("iotaN", [128, N])
        hn, hp = sb("hn", [128, NT, 128]), sb("hp", [128, NT, 3, 128], BF16)
        oh, ohT = sb("oh", [128, 2, NT, SL], BF16), sb("ohT", [128, 2, NA, N], BF16)
        xg, h1 = sb("xg", [128, SL]), sb("h1", [128, NJ, SL])
        ws, yw = sb("ws", [128, NA]), sb("yw", [128, NA, 128])
        yp = sb("yp", [128, 3, NA, 128], BF16)
        psX, psW = ps("psX", [128, SL]), ps("psW", [128, NA, 3])
        psF = [ps(f"psF{n}", [128, 2, SL]) for n in range(2)]
        psY = ps("psY", [128, NA, 128])
        psA = [ps(f"psA{n}", [128, G, 128]) for n in range(2)]
        own_dve = Tally(sem("own_dve"))
        norm = RowNorm(nc, X, sb, signal, own_dve, passed)
        s_c = sem("loads")
        split, idc_ready = signal("split"), signal("idc_ready")
        w_ready = [signal(f"w_ready{n}") for n in range(2)]
        oh_ready, ohT_ready = signal("oh_ready"), signal("ohT_ready")
        gathered, xg_ready = signal("gathered", 1), signal("xg_ready", 1)
        weights = signal("weights", 1)
        first_done, gelu_done = signal("first", 1), signal("gelu", 4)
        second_done, weighted = signal("second", 2), signal("weighted", 1)
        hi_done, rest_done, mid_done, lo_done = (signal(n) for n in ("hi", "rest", "mid", "lo"))
        scattered, added = signal("scattered", 3), signal("added", 2)
        block = ctx.enter_context(nc.Block())

        @block.sync
        def _(sp):
            sp.dma_start(idb[:, :, :].rearrange("p e s -> p (e s)"),
                         io["idxT"].rearrange("e s -> (e s)").partition_broadcast(128)).then_inc(s_c, 16)
            sp.dma_start(tokid[:, :], io["tokid"]).then_inc(s_c, 16)
            sp.dma_start(cw[:, :, :], io["cw"].rearrange("(n p) e -> p n e", p=128)).then_inc(s_c, 16)
            sp.dma_start(idi[:, :, :], io["idx"].rearrange("(a p) e -> p a e", p=128)).then_inc(s_c, 16)
            sp.dma_start(iotaN[:, :], io["iotaN"].partition_broadcast(128)).then_inc(s_c, 16)
            sp.dma_start(b1[:, :], io["eb1T"]).then_inc(s_c, 16)
            sp.dma_start(b2[:, :, :].rearrange("p e c -> p (e c)"),
                         io["eb2"].rearrange("e c -> (e c)").partition_broadcast(128)).then_inc(s_c, 16)

            def load(e, gp):
                a1, a2 = io["ew1"][at(e)], io["ew2"][at(e)]
                if isinstance(e, Lin):
                    a1, a2 = a1.squeeze(0), a2.squeeze(0)
                sp.dma_start(w1[:, gp, :], a1).then_inc(w_ready[gp].sem, 16)
                sp.dma_start(w2[:, gp, :, :], a2.rearrange("(j p) c -> p j c", p=128)).then_inc(w_ready[gp].sem, 16)
            load(0, 0)

            def step(e, gp, more):
                sp.wait_ge(second_done.sem, second_done.at(e))
                sp.sem_inc(passed, 1)
                if more:
                    load(e + 1, 1 - gp)
            groups(nc.sync, step, pairs=E1 // 2)

        @block.tensor
        def _(pe):
            def gather(e, gp):
                pe.wait_ge(oh_ready.sem, oh_ready.at(e + 1))
                pe.wait_ge(xg_ready.sem, xg_ready.at(e))
                for n in range(NT):
                    for k in range(3):
                        ins = nc.tensor.matmul(psX[:, :], hp[:, n, k, :], oh[:, gp, n, :],
                                               start=(n == 0 and k == 0), stop=(n == NT - 1 and k == 2))
                ins.then_inc(gathered.sem, 1)

            def gate(e, gp):
                pe.wait_ge(weighted.sem, weighted.at(e))
                for a in range(NA):
                    for n in range(NT):
                        rhs = cwp[:, n, :, at(e)]
                        if isinstance(e, Lin):
                            rhs = rhs.rearrange("p a b -> p (a b)")
                        ins = nc.tensor.matmul(psW[:, a, :], oh[:, gp, n, a * 128:(a + 1) * 128], rhs,
                                               start=(n == 0), stop=(n == NT - 1), skip_group_check=True)
                ins.then_inc(weights.sem, 1)

            for s in (gathered, weights, first_done, second_done, scattered):
                s.credit(nc.tensor)
            pe.wait_ge(split.sem, split.at(2))
            gather(0, 0)
            gate(0, 0)

            def step(e, gp, more):
                pe.wait_ge(w_ready[gp].sem, w_ready[gp].at(32 * parity_count(e, gp)))
                pe.wait_ge(xg_ready.sem, xg_ready.at(e + 1))
                for j in range(NJ):
                    pe.wait_ge(gelu_done.sem, gelu_done.at(NJ * (e - 1) + j // 2 * 2 + 2))
                    nc.tensor.matmul(psF[j // 2][:, j % 2, :], w1[:, gp, j * 128:(j + 1) * 128], xg[:, :],
                                     start=True, stop=True, skip_group_check=True).then_inc(first_done.sem, 1)
                pe.wait_ge(weighted.sem, weighted.at(e))
                pe.wait_ge(gelu_done.sem, gelu_done.at(NJ * (e + 1)))
                for a in range(NA):
                    for j in range(NJ):
                        ins = nc.tensor.matmul(psY[:, a, :], h1[:, j, a * 128:(a + 1) * 128], w2[:, gp, j, :],
                                               start=(j == 0), stop=(j == NJ - 1), skip_group_check=True)
                ins.then_inc(second_done.sem, 1)
                if more:
                    gather(e + 1, 1 - gp)
                    gate(e + 1, 1 - gp)
                pe.wait_ge(lo_done.sem, lo_done.at(e + 1))
                pe.wait_ge(ohT_ready.sem, ohT_ready.at(e + 1))
                for n in range(NT):
                    if n % G == 0:
                        pe.wait_ge(added.sem, added.at(2 * e + n // G - 1))
                    for a in range(NA):
                        for k in range(3):
                            ins = nc.tensor.matmul(psA[n // G][:, n % G, :], ohT[:, gp, a, n * 128:(n + 1) * 128],
                                                   yp[:, k, a, :], start=(a == 0 and k == 0),
                                                   stop=(a == NA - 1 and k == 2), skip_group_check=True)
                    if n % G == G - 1:
                        ins.then_inc(scattered.sem, 1)
            groups(nc.tensor, step, pairs=E1 // 2)

        @block.scalar
        def _(act):
            for s in (xg_ready, gelu_done):
                s.credit(nc.scalar)
            act.wait_ge(s_c, 16 * 7)

            def copy_x(e):
                act.wait_ge(gathered.sem, gathered.at(e + 1))
                act.wait_ge(first_done.sem, first_done.at(NJ * e))
                nc.scalar.activation(xg[:, :], psX[:, :], ACT.Copy).then_inc(xg_ready.sem, 1)
            copy_x(0)

            def step(e, gp, more):
                for j in range(NJ):
                    act.wait_ge(first_done.sem, first_done.at(NJ * e + j // 2 * 2 + 2))
                    if j == 0:
                        act.wait_ge(second_done.sem, second_done.at(e))
                    act.sem_inc(passed, 1)
                    nc.scalar.activation(h1[:, j, :], psF[j // 2][:, j % 2, :], ACT.Gelu_apprx_tanh,
                                         bias=b1[:, at1(NJ * e + j)]).then_inc(gelu_done.sem, 1)
                if more:
                    copy_x(e + 1)
            groups(nc.scalar, step, pairs=E1 // 2)

        @block.gpsimd
        def _(pool):
            norm.start(pool)
            for g in range(2):
                norm.root(pool, g)
            pool.wait_ge(s_c, 16 * 7)
            pool.wait_ge(split.sem, split.at(3))
            pool.sem_inc(passed, 1)

            def step(e, gp, more):
                pool.wait_ge(scattered.sem, scattered.at(2 * e - 2))
                pool.sem_inc(passed, 1)
                nc.gpsimd.tensor_copy(idc[:, gp, :].unsqueeze(1) if isinstance(e, Lin) else idc[:, gp, :],
                                      idf[:, at(e), :]).then_inc(idc_ready.sem, 1)
                pool.wait_ge(idc_ready.sem, idc_ready.at(e + 1))
                pool.sem_inc(passed, 1)
                for a in range(NA):
                    ins = nc.gpsimd.tensor_scalar(ohT[:, gp, a, :], iotaN[:, :], idc[:, gp, a:a + 1], None,
                                                  ALU.is_equal)
                ins.then_inc(ohT_ready.sem, 1)
            groups(nc.gpsimd, step, pairs=E1 // 2)

        @block.vector
        def _(dve):
            for s in (weighted, added):
                s.credit(nc.vector)
            for g in range(2):
                norm.take_stats(dve, g)
                norm.apply(dve, g, hn[:, G * g:G * g + G, :])
            dve.wait_ge(norm.done.sem, norm.done.at(2))
            dve.wait_ge(s_c, 16 * 7)
            for full_, part, last in ((hn, [hp[:, :, k, :] for k in range(3)], split),
                                      (cw, [cwp[:, :, k, :] for k in range(3)], split)):
                nc.vector.tensor_copy(part[0], full_[:, :, :]).then_inc(own_dve.sem, own_dve.one())
                dve.wait_ge(own_dve.sem, own_dve.value())
                nc.vector.tensor_tensor(full_[:, :, :], full_[:, :, :], part[0], ALU.subtract).then_inc(
                    own_dve.sem, own_dve.one())
                dve.wait_ge(own_dve.sem, own_dve.value())
                nc.vector.tensor_copy(part[1], full_[:, :, :]).then_inc(own_dve.sem, own_dve.one())
                dve.wait_ge(own_dve.sem, own_dve.value())
                nc.vector.tensor_tensor(part[2], full_[:, :, :], part[1], ALU.subtract).then_inc(last.sem, 1)
            nc.vector.tensor_copy(idf[:, :, :].rearrange("p e a -> p a e"), idi[:, :, :]).then_inc(split.sem, 1)

            def mark_slots(e, gp):
                dve.wait_ge(weights.sem, weights.at(e - 1))
                for n in range(NT):
                    src = idb[:, at(e), :]
                    dst = oh[:, gp, n, :]
                    ins = nc.vector.tensor_scalar(dst.unsqueeze(1) if isinstance(e, Lin) else dst, src,
                                                  tokid[:, n:n + 1], None, ALU.is_equal)
                ins.then_inc(oh_ready.sem, 1)
            mark_slots(0, 0)

            def step(e, gp, more):
                if more:
                    mark_slots(e + 1, 1 - gp)
                dve.wait_ge(weights.sem, weights.at(e + 1))
                nc.vector.tensor_reduce(ws[:, :], psW[:, :, :], AX.X, ALU.add).then_inc(own_dve.sem, own_dve.one())
                dve.wait_ge(second_done.sem, second_done.at(e + 1))
                bias = b2[:, at(e), :]
                bias = bias.to_broadcast([128, NA, 128]) if isinstance(e, Lin) \
                    else bias.unsqueeze(1).to_broadcast([128, NA, 128])
                nc.vector.tensor_tensor(yw[:, :, :], psY[:, :, :], bias, ALU.add).then_inc(own_dve.sem, own_dve.one())
                dve.wait_ge(own_dve.sem, own_dve.value())
                nc.vector.tensor_tensor(yw[:, :, :], yw[:, :, :], ws[:, :].unsqueeze(2).to_broadcast([128, NA, 128]),
                                        ALU.mult).then_inc(weighted.sem, 1)
                dve.wait_ge(weighted.sem, weighted.at(e + 1))
                dve.wait_ge(scattered.sem, scattered.at(2 * e))
                nc.vector.tensor_copy(yp[:, 0, :, :], yw[:, :, :]).then_inc(own_dve.sem, own_dve.one())
                dve.wait_ge(own_dve.sem, own_dve.value())
                nc.vector.tensor_tensor(yw[:, :, :], yw[:, :, :], yp[:, 0, :, :], ALU.subtract).then_inc(
                    own_dve.sem, own_dve.one())
                dve.wait_ge(own_dve.sem, own_dve.value())
                nc.vector.tensor_copy(yp[:, 1, :, :], yw[:, :, :]).then_inc(own_dve.sem, own_dve.one())
                dve.wait_ge(own_dve.sem, own_dve.value())
                nc.vector.tensor_tensor(yp[:, 2, :, :], yw[:, :, :], yp[:, 1, :, :],
                                        ALU.subtract).then_inc(lo_done.sem, 1)
                for n in range(2):
                    dve.wait_ge(scattered.sem, scattered.at(2 * e + n + 1))
                    nc.vector.tensor_tensor(X[:, G * n:G * n + G, :], X[:, G * n:G * n + G, :], psA[n][:, :, :],
                                            ALU.add).then_inc(added.sem, 1)
            groups(nc.vector, step, own_dve, 2 * 5, pairs=E1 // 2)


def more_arrays(a):
    place = np.arange(128) % 4
    idx, cw = a["L1_ffn_top_idx"], a["L1_ffn_combine_weights"]
    return {
        "wr": a["L0_ffn_Wr"], "br": a["L0_ffn_br"],
        "before": np.triu(np.ones((T, T), np.float32), 1),
        "iota8": np.arange(E1, dtype=np.float32), "iota20": np.arange(1, CAP + 1, dtype=np.float32),
        "w1": a["L0_ffn_W1"], "w2": a["L0_ffn_W2"],
        "b1T": a["L0_ffn_b1"].reshape(E1 * NJ, 128).T, "b2T": a["L0_ffn_b2"].T,
        "s_wq": a["L1_attn_Wq"], "s_wk": a["L1_attn_Wk"],
        "same_place": (place[:, None] == place[None, :]).astype(np.float32),
        "x_wq": a["L1_xattn_Wq"], "x_wk": a["L1_xattn_Wk"], "x_wv": a["L1_xattn_Wv"].T,
        "idx": idx, "idxT": idx.T, "cw": cw,
        "tokid": np.arange(cw.shape[0], dtype=np.float32).reshape(-1, 128).T,
        "iotaN": np.arange(cw.shape[0], dtype=np.float32),
        "ew1": a["L1_ffn_W1"], "ew2": a["L1_ffn_W2"],
        "eb1T": a["L1_ffn_b1"].reshape(E1 * NJ, 128).T, "eb2": a["L1_ffn_b2"],
    }


def setup(nc, consts, io):
    with ExitStack() as ctx:
        used = []
        ctx.push(clear(nc, used))
        loaded = ctx.enter_context(nc.semaphore("identities"))
        used.append(loaded.num)
        block = ctx.enter_context(nc.Block())

        @block.sync
        def _(sp):
            sp.dma_start(consts["ident"][:, :], io["ident"]).then_inc(loaded, 16)

        @block.vector
        def _(dve):
            dve.wait_ge(loaded, 16)
            nc.vector.tensor_copy(consts["identb"][:, :], consts["ident"][:, :])


def store(nc, X, out):
    with ExitStack() as ctx:
        stored = ctx.enter_context(nc.semaphore("stored"))
        block = ctx.enter_context(nc.Block())

        @block.sync
        def _(sp):
            sp.dma_start(out.rearrange("b t c -> t b c"), X[:, :, :]).then_inc(stored, 16)
            sp.wait_ge(stored, 16)


def build(nc, io, out):
    with ExitStack() as ctx:
        X_before = ctx.enter_context(nc.sbuf_tensor("X", [128, B + 1, C], F32))
        X = X_before[:, 1:B + 1, :]
        consts = {"ident": ctx.enter_context(nc.sbuf_tensor("ident", [128, 128], F32)),
                  "identb": ctx.enter_context(nc.sbuf_tensor("identb", [128, 128], BF16)),
                  "passed": ctx.enter_context(nc.semaphore("passed"))}
        setup(nc, consts, io)
        head_attention(nc, "self", X_before, io, consts, True)
        if STAGES >= 2:
            head_attention(nc, "cross", X_before, io, consts, False)
        if STAGES >= 3:
            experts_routed(nc, X, io, consts)
        if STAGES >= 4:
            sequence_attention(nc, X, io, consts)
        if STAGES >= 5:
            context_attention(nc, X, io, consts)
        if STAGES >= 6:
            experts_chosen(nc, X, io, consts)
        store(nc, X, out)


STAGES = 6


def kernel(**inputs):
    import concourse.bacc as bacc
    from concourse.bass_utils import run_bass_kernel_spmd as run

    a = {k: np.asarray(v) for k, v in inputs.items()}

    def heads_inner(w):
        return w.reshape(w.shape[:-1] + (H, DH)).swapaxes(-1, -2).reshape(w.shape)

    idx = np.arange(T, dtype=np.float32)
    eps = float(np.finfo(np.float32).eps)
    scale = (1.0 / (np.float32(10000.0) ** (np.arange(0, DH, 2, dtype=np.float32) / DH) + eps)).astype(np.float32)
    ang = idx[:, None] * scale[None, :]
    pos = np.stack([np.sin(ang), np.cos(ang)], axis=-1).reshape(T, DH).astype(np.float32)
    posT = np.tile(np.repeat(pos.T, H, axis=0), (1, G))
    causal = np.triu(np.full((T, T), CAUSAL_BIG, np.float32), 1)
    arrays = {
        "x": a["x"],
        "ident": np.eye(128, dtype=np.float32),
        "pos": posT,
        "causal": causal,
        "a_wq": heads_inner(a["L0_attn_Wq"]), "a_wk": heads_inner(a["L0_attn_Wk"]),
        "a_wv": a["L0_attn_Wv"], "a_wo": a["L0_attn_Wo"],
        "ctxT": a["ctx_1024"].transpose(2, 0, 1).reshape(C, B * T),
        "mask": a["mask_BxS2_ik0"], "maskT": a["mask_BxS2_ik0"].T,
        "c_wq": heads_inner(a["L0_xattn_Wq"].T), "c_wk": heads_inner(a["L0_xattn_Wk"].T), "c_wv": a["L0_xattn_Wv"].T,
        "bqk": np.stack([heads_inner(a["L0_xattn_bq"]), heads_inner(a["L0_xattn_bk"])], axis=1),
        "bv": a["L0_xattn_bv"],
    }
    arrays.update(more_arrays(a))
    nc = bacc.Bacc("TRN2", target_bir_lowering=False, num_devices=1)
    io = {}
    for name in list(arrays):
        arrays[name] = np.ascontiguousarray(arrays[name])
        io[name] = nc.dram_tensor(name + "_dram", arrays[name].shape, mybir.dt.from_np(arrays[name].dtype),
                                  kind="ExternalInput").ap()
    io["spill"] = nc.dram_tensor("spill_dram", [2, 2, 3, 128, GT], BF16, kind="Internal").ap()
    io["dwt"] = nc.dram_tensor("dwt_dram", [NG, E1 // 2 * CAP, G * 2 * 128], F32, kind="Internal").ap()
    out = nc.dram_tensor("out_dram", [B, T, C], F32, kind="ExternalOutput").ap()
    build(nc, io, out)
    r = run(nc, [{k + "_dram": v for k, v in arrays.items()}], core_ids=[0])
    return r.results[0]["out_dram"]
```

```python
import numpy as np

import concourse.bass as bass
from concourse import mybir
from contextlib import ExitStack

F32 = mybir.dt.float32
BF16 = mybir.dt.bfloat16
F16 = mybir.dt.float16
I32 = mybir.dt.int32
U32 = mybir.dt.uint32
ACT = mybir.ActivationFunctionType
ALU = mybir.AluOpType
AX = mybir.AxisListType

B, T, C = 32, 128, 128
G = 4
NG = B // G
H, DH = 16, 8
HB = 4
NBLK = H // HB
GT = G * T
EPS = 1e-5
CAUSAL_BIG = -1e30
NEG = -1e9 * DH ** 0.5
P_SCALE = 2.0 ** 12



class Lin:

    def __init__(self, i, k, c):
        self.i, self.k, self.c = i, k, c

    def __add__(self, n):
        return Lin(self.i, self.k, self.c + n)

    def __sub__(self, n):
        return self + -n

    def __mul__(self, n):
        return Lin(self.i, self.k * n, self.c * n)

    __rmul__, __radd__ = __mul__, __add__

    def value(self):
        return self.i * self.k + self.c


def at(n):
    return bass.ds(n.value(), 1) if isinstance(n, Lin) else n


class Signal:

    def __init__(self, sem, free=0):
        self.sem, self.free = sem, free

    def credit(self, eng):
        eng.sem_inc(self.sem, self.free)

    def at(self, n):
        if isinstance(n, Lin):
            n = n + self.free
            assert n.c >= 1, (n.k, n.c)
            return n.value()
        return n + self.free if n > 0 else 0


def clear(nc, used):
    def end(error, *_):
        if error is None:
            with nc.Block() as block:
                @block.gpsimd
                def _(pool):
                    first = None
                    for n in sorted(used):
                        first = n if first is None else first
                        if n + 1 not in used:
                            pool.sem_clear(range(first, n + 1))
                            first = None
    return end


class Tally:

    def __init__(self, sem):
        self.sem, self.n, self.i, self.per = sem, 0, None, 0

    def one(self):
        self.n += 1
        return 1

    def value(self):
        return self.n if self.i is None else self.i * self.per + self.n

    def enter(self, i, per):
        self.start, self.i, self.per = self.n, i, per

    def leave(self, times):
        assert self.n - self.start == self.per, (self.n - self.start, self.per)
        self.n, self.i = self.start + times * self.per, None


def head_attention(nc, kind, X_before, io, consts, first):
    own = kind == "self"
    X = X_before[:, 1:B + 1, :]
    p = "a_" if own else "c_"
    ROWS = 6 * DH
    KS = ROWS if own else ROWS + 1
    MROW = KS
    KT = KS + 2
    VP = 3
    SCALE = C ** -0.5 if own else DH ** -0.5
    ident, identb, passed = consts["ident"], consts["identb"], consts["passed"]
    Q_PARTS = [0, 0, 0, 1, 1, 2]
    K_RUNS = [(0, 3), (3, 2), (5, 1)]

    used = []
    with ExitStack() as ctx:
        ctx.push(clear(nc, used))

        def sb(name, shape, dt):
            return ctx.enter_context(nc.sbuf_tensor(p + name, shape, dt))

        def ps(name, shape, dt=F32):
            return ctx.enter_context(nc.psum_tensor(p + name, shape, dt))

        def sem(name):
            s = ctx.enter_context(nc.semaphore(p + name))
            used.append(s.num)
            return s

        def signal(name, free=0):
            return Signal(sem(name), free)

        wq, wk, wv = (sb(n, [128, 128], F32) for n in ("wq", "wk", "wv"))
        wo = sb("wo", [128, 128], F32) if own else None
        pos = sb("pos", [128, GT], F32) if own else None
        causal = sb("causal", [128, 128], F32) if own else None
        cmask = sb("cmask", [128, HB, 128], BF16) if own else None
        if not own:
            bqk = sb("bqk", [128, 2], F32)
            bv = sb("bv", [128, 128], F32)
            kmi = sb("kmi", [128, 2, 128], I32)
            km = sb("km", [128, G, 128], F32)
            kmf = sb("kmf", [128, 2, 128], F32)
            negrow = sb("negrow", [H, 2, 128], BF16)
            qmi = sb("qmi", [128, 32], I32)
            qm = sb("qm", [128, 32], F32)
            ctxT = sb("ctxT", [128, 2, GT], F32)
        ones = sb("ones", [H, 2 * GT], BF16)
        stats = sb("stats", [128, G, 6], F32)
        mv = sb("mv", [128, G, 2], F32)
        veps = sb("veps", [128, G], F32)
        half_neg = sb("half_neg", [128, G], F32)
        rstd = sb("rstd", [128, G], F32)
        hn = sb("hn", [128, G, 128], F32)
        hT = sb("hT", [128, GT], F32)
        full = [sb(n, [128, GT], F32) for n in ("qf", "kf")]
        parts = [sb(n, [128, 3, GT], BF16) for n in ("qp", "kp")]
        stack = [sb(n, [64, 2, H, GT], BF16) for n in ("qs", "ks")]
        Qs, Ks = stack
        vf = sb("vf", [128, GT], F32)
        vp = sb("vp", [128, 2, G, H, VP, DH + 1], BF16)
        mx = sb("mx", [128, 2, H], F32)
        negm = sb("negm", [H, 2, 2, 128], BF16)
        PT = sb("PT", [128, NBLK, HB, 128], F32)
        Ph, Pl = (sb(n, [128, NBLK, HB, 128], F16) for n in ("Ph", "Pl"))
        osum = sb("osum", [128, H, DH + 1], F32)
        rden = sb("rden", [128, 2, H], F32)
        O = sb("O", [128, H, DH], F32)
        oT = sb("oT", [128, 128], F32) if own else None

        psS = [ps(f"psS{n}", [128, HB, 128]) for n in range(2)]
        psT = [ps(f"psT{n}", [128, HB, 128]) for n in range(2)]
        psO = [ps(f"psO{n}", [128, 512]) for n in range(2)]
        psH = ps("psH", [128, 512])
        psM = ps("psM", [128, 512])
        outs = [t[:, 0:H * VP * (DH + 1)].rearrange("p (h a) -> p h a", h=H) for t in psO]

        s_w = sem("weights")
        s_x = [sem(f"x{n}") for n in range(2)]
        s_ctx = [signal(f"ctx{n}") for n in range(2)]
        s_cst = sem("constants")
        s_ones = sem("ones")
        s_neg = sem("masked_rows")
        s_rows = sem("fixed_rows")
        ln_done = signal("ln_done")
        stats_ready = signal("stats_ready")
        rstd_ready = signal("rstd_ready")
        transposed = signal("transposed")
        hT_ready = signal("hT_ready")
        q_done = signal("q_projected")
        k_done = signal("k_projected")
        v_done = signal("v_projected")
        v_taken = signal("v_taken")
        v_split = signal("v_split")
        v_rest = signal("v_rest")
        v_ready = signal("v_ready")
        taken = signal("taken")
        hi_ready = signal("hi_ready")
        rest_ready = signal("rest_ready")
        mid_ready = signal("mid_ready")
        lo_ready = signal("lo_ready")
        hi_spilled = [signal(f"hi_spilled{n}") for n in range(2)]
        lo_spilled = [signal(f"lo_spilled{n}") for n in range(2)]
        stacked = [signal(f"stacked{n}") for n in range(2)]
        scored = signal("scored")
        maxed = signal("maxed")
        max_turned = signal("max_turned")
        minus_ready = signal("minus_ready")
        row_placed = [signal(f"row_placed{n}") for n in range(2)]
        scored_t = signal("scored_t", 1)
        exp_done = signal("exp_done")
        selected = signal("selected")
        weighed = signal("weighed", 4)
        normed = signal("normed", 1)
        out_turned = signal("out_turned")
        out_copied = signal("out_copied")
        out_projected = signal("out_projected", 1)
        added = signal("added", 1)
        hi_made, lo_made = signal("probs_hi"), signal("probs_lo", 1)
        negated, inverted = signal("negated"), signal("inverted")
        query_masked = signal("query_masked")
        summed = signal("summed", 2)
        own_pool = signal("own_pool")
        own_dve = Tally(sem("own_dve"))

        NW = 5
        NSTACK = (len(Q_PARTS) + len(K_RUNS)) * 16

        def body(step, i):
            last = isinstance(i, int)
            for gp in range(2):
                g = 2 * i + gp if last else Lin(i, 2, gp)
                for r in range(G):
                    left = B - 1 - (G * g + r) if last else B
                    step(g, gp, r, left)

        def pairs(eng, step, tally=None, per=0):
            with eng.Fori(0, NG // 2 - 1) as i:
                if tally:
                    tally.enter(i, per)
                body(step, i)
            if tally:
                tally.leave(NG // 2 - 1)
            body(step, NG // 2 - 1)

        def pair(g, gp, more):
            n = (gp + more) // 2
            return Lin(g.i, 1, n) if isinstance(g, Lin) else (g - gp) // 2 + n

        def half(g, gp, r, more=0):
            n = 2 * gp + (r + more) // 2
            return Lin(g.i, 4, n) if isinstance(g, Lin) else 4 * ((g - gp) // 2) + n

        block = ctx.enter_context(nc.Block())

        @block.sync
        def _(sp):
            if first:
                xt = io["x"].rearrange("b t c -> t b c")
                sp.dma_start(X[:, 0:2 * G, :], xt[:, 0:2 * G, :]).then_inc(s_x[0], 16)
            sp.dma_start(wq[:, :], io[p + "wq"]).then_inc(s_w, 16)
            sp.dma_start(wk[:, :], io[p + "wk"]).then_inc(s_w, 16)
            sp.dma_start(wv[:, :], io[p + "wv"]).then_inc(s_w, 16)
            if own:
                sp.dma_start(pos[:, :], io["pos"]).then_inc(s_w, 16)
                sp.dma_start(wo[:, :], io[p + "wo"]).then_inc(s_w, 16)
                sp.dma_start(causal[:, :], io["causal"]).then_inc(s_cst, 16)
            else:
                for n in range(2):
                    sp.dma_start(ctxT[:, n, :], io["ctxT"][:, n * GT:(n + 1) * GT]).then_inc(s_ctx[n].sem, 16)
                sp.dma_start(bqk[:, :], io["bqk"]).then_inc(s_w, 16)
                sp.dma_start(bv[:, :], io["bv"].partition_broadcast(128)).then_inc(s_w, 16)
                for d in range(DH):
                    sp.dma_start(kmi[H * d:H * d + H, :, :],
                                 io["mask"].rearrange("(a h) t -> h a t", h=H)).then_inc(s_cst, 16)
                sp.dma_start(qmi[:, :], io["maskT"]).then_inc(s_cst, 16)
            if first:
                sp.dma_start(X[:, 2 * G:B, :], xt[:, 2 * G:B, :]).then_inc(s_x[1], 16)
            sp.wait_ge(s_ones, 4 if own else 3)
            for n in range(2):
                sp.dma_start(Ks[MROW:MROW + 2, n, :, :], ones[:, :]).then_inc(s_rows, 16)
                if not own:
                    sp.dma_start(Qs[ROWS:ROWS + 1, n, :, :], ones[:, 0:GT]).then_inc(s_rows, 16)
            if not own:
                sp.wait_ge(s_neg, 1)
                for n in range(2):
                    for r in range(G):
                        sp.dma_start(Ks[ROWS:ROWS + 1, n, :, r * T:(r + 1) * T],
                                     negrow[:, r % 2, :]).then_inc(s_rows, 16)

            def spill_hi(g, gp):
                for n in range(2):
                    sp.wait_ge(hi_ready.sem, hi_ready.at(2 * g + n + 1))
                    sp.sem_inc(passed, 1)
                    sp.dma_start(io["spill"][gp, n, 0], parts[n][:, 0, :]).then_inc(hi_spilled[gp].sem, 16)

            def spill_rest(g, gp):
                for n in range(2):
                    sp.wait_ge(lo_ready.sem, lo_ready.at(2 * g + n + 1))
                    sp.sem_inc(passed, 1)
                    sp.dma_start(io["spill"][gp, n, 1:3].rearrange("a p t -> p a t"),
                                 parts[n][:, 1:3, :]).then_inc(lo_spilled[gp].sem, 16)

            def fill(gp, rows):
                for row in rows:
                    src = io["spill"][gp, 0, Q_PARTS[row]].rearrange("(d h) t -> d (h t)", h=H)
                    sp.dma_start(Qs[DH * row:DH * row + DH, gp, :, :], src).then_inc(stacked[gp].sem, 16)

            def fill_high(g, gp, nth):
                sp.wait_ge(hi_spilled[gp].sem, hi_spilled[gp].at(32 * nth + 32))
                sp.sem_inc(passed, 1)
                sp.wait_ge(scored_t.sem, scored_t.at(NBLK * G * (g - 1)))
                sp.sem_inc(passed, 1)
                fill(gp, range(3))

            def fill_rest(gp, nth):
                sp.wait_ge(lo_spilled[gp].sem, lo_spilled[gp].at(32 * nth + 32))
                sp.sem_inc(passed, 1)
                fill(gp, range(3, len(Q_PARTS)))
                for row, count in K_RUNS:
                    src = io["spill"][gp, 1, 0:count].rearrange("a (d h) t -> (a d) (h t)", h=H)
                    sp.dma_start(Ks[DH * row:DH * (row + count), gp, :, :], src).then_inc(stacked[gp].sem, 16)

            def place_row(b, gp, r):
                sp.wait_ge(minus_ready.sem, minus_ready.at(b + 1))
                sp.sem_inc(passed, 1)
                for a in range(2):
                    sp.dma_start(Qs[MROW + a:MROW + a + 1, gp, :, r * T:(r + 1) * T],
                                 negm[:, r % 2, a, :]).then_inc(row_placed[r % 2].sem, 16)

            def step(g, gp, r, left):
                b = G * g + r
                if r == 0 and left >= G:
                    spill_rest(g + 1, 1 - gp)
                    fill_high(g + 1, 1 - gp, pair(g, gp, 1))
                    fill_rest(1 - gp, pair(g, gp, 1))
                if left >= 2:
                    if r < 2:
                        place_row(b + 2, gp, r + 2)
                    else:
                        place_row(b + 2, 1 - gp, r - 2)
                if r == 3 and left >= 2 * G - r:
                    spill_hi(g + 2, gp)
                if not own and r == 0 and left >= 2 * G:
                    sp.wait_ge(v_done.sem, v_done.at(g + 1))
                    sp.sem_inc(passed, 1)
                    lo = (g + 2) * GT
                    src = io["ctxT"][:, bass.ds(lo.value(), GT)] if isinstance(lo, Lin) else io["ctxT"][:, lo:lo + GT]
                    sp.dma_start(ctxT[:, gp, :], src).then_inc(s_ctx[gp].sem, 16)

            spill_hi(0, 0)
            fill_high(0, 0, 0)
            spill_rest(0, 0)
            fill_rest(0, 0)
            spill_hi(1, 1)
            place_row(0, 0, 0)
            place_row(1, 0, 1)
            pairs(nc.sync, step)

        @block.tensor
        def _(pe):
            def prep_transpose(g):
                pe.wait_ge(ln_done.sem, ln_done.at(g + 1))
                pe.wait_ge(v_taken.sem, v_taken.at(g))
                for r in range(G):
                    ins = nc.tensor.transpose(psH[:, r * 128:(r + 1) * 128], hn[:, r, :], ident[:, :])
                ins.then_inc(transposed.sem, 1)

            def prep_q(g):
                pe.wait_ge(hT_ready.sem, hT_ready.at(g + 1))
                pe.wait_ge(taken.sem, taken.at(2 * g))
                nc.tensor.matmul(psH[:, :], wq[:, :], hT[:, :], start=True, stop=True).then_inc(q_done.sem, 1)

            def prep_k(g, gp, nth):
                if not own:
                    pe.wait_ge(s_ctx[gp].sem, s_ctx[gp].at(16 * nth + 16))
                pe.wait_ge(taken.sem, taken.at(2 * g + 1))
                nc.tensor.matmul(psH[:, :], wk[:, :], hT[:, :] if own else ctxT[:, gp, :],
                                 start=True, stop=True).then_inc(k_done.sem, 1)

            def prep_v(g, gp):
                pe.wait_ge(taken.sem, taken.at(2 * g + 2))
                for r in range(G):
                    src = hT[:, r * T:(r + 1) * T] if own else ctxT[:, gp, r * T:(r + 1) * T]
                    ins = nc.tensor.matmul(psH[:, r * 128:(r + 1) * 128], src, wv[:, :], start=True, stop=True)
                ins.then_inc(v_done.sem, 1)

            def causal_part(j):
                nc.tensor.matmul(psS[j % 2][:, :, :], identb[:, :], cmask[:, :, :], start=True, stop=False,
                                 skip_group_check=True)

            def score(gp, r, j, k):
                h = HB * j + k
                return nc.tensor.matmul(psS[j % 2][:, k, :], Qs[0:KS, gp, h, r * T:(r + 1) * T],
                                        Ks[0:KS, gp, h, r * T:(r + 1) * T],
                                        start=not own, stop=True, skip_group_check=True)

            def score_t(gp, r, j, k):
                h = HB * j + k
                return nc.tensor.matmul(psT[j % 2][:, k, :], Ks[0:KT, gp, h, r * T:(r + 1) * T],
                                        Qs[0:KT, gp, h, r * T:(r + 1) * T],
                                        start=True, stop=True, skip_group_check=True)

            def weigh(gp, r, j, k):
                h = HB * j + k
                values = vp[:, gp, r, h, :, :].rearrange("p a d -> p (a d)")
                nc.tensor.matmul(outs[r % 2][:, h, :], Ph[:, j, k, :], values, start=True, stop=False,
                                 skip_group_check=True)
                return nc.tensor.matmul(outs[r % 2][:, h, :], Pl[:, j, k, :], values, start=False, stop=True,
                                        skip_group_check=True)

            def turn_max(b, r):
                pe.wait_ge(maxed.sem, maxed.at(NBLK * (b + 1)))
                pe.wait_ge(minus_ready.sem, minus_ready.at(b))
                if own:
                    pe.wait_ge(added.sem, added.at(b - 2))
                nc.tensor.transpose(psM[0:H, 0:128], mx[:, r % 2, :], ident[:, :]).then_inc(max_turned.sem, 1)

            scored_t.credit(nc.tensor)
            pe.wait_ge(s_w, 16 * NW)
            if own:
                pe.wait_ge(s_neg, 1)
            else:
                pe.wait_ge(s_cst, 16 * 9)
            prep_transpose(0)
            prep_q(0)
            prep_k(0, 0, 0)
            prep_v(0, 0)
            prep_transpose(1)
            prep_q(1)
            prep_k(1, 1, 0)
            pe.wait_ge(s_rows, 16 * (2 if own else 12))
            pe.wait_ge(s_ones, 4 if own else 3)
            pe.wait_ge(stacked[0].sem, stacked[0].at(NSTACK))
            for n in range(NBLK * 2 + 3):
                pe.wait_ge(maxed.sem, maxed.at(n - 1))
                if own:
                    causal_part(n % NBLK)
                for k in range(HB):
                    ins = score(0, n // NBLK, n % NBLK, k)
                ins.then_inc(scored.sem, 1)
                if n in (NBLK, 2 * NBLK):
                    turn_max(n // NBLK - 1, n // NBLK - 1)
            pe.wait_ge(row_placed[0].sem, row_placed[0].at(32))
            for j in range(3):
                pe.wait_ge(exp_done.sem, exp_done.at(j - 1))
                for k in range(HB):
                    ins = score_t(0, 0, j, k)
                ins.then_inc(scored_t.sem, 1)
            for s in (weighed,) + ((out_projected,) if own else ()):
                s.credit(nc.tensor)

            def turn_out(b):
                pe.wait_ge(added.sem, added.at(b))
                nc.tensor.transpose(psM[:, 128:256], O[:, :, :].rearrange("p h d -> p (h d)"),
                                    ident[:, :]).then_inc(out_turned.sem, 1)

            def project_out(b):
                pe.wait_ge(out_copied.sem, out_copied.at(b + 1))
                nc.tensor.matmul(psM[:, 256:384], oT[:, :], wo[:, :], start=True,
                                 stop=True).then_inc(out_projected.sem, 1)

            def step(g, gp, r, left):
                b = G * g + r
                for j in range(NBLK):
                    tgp, tr = (gp, r) if j < 1 else (gp, r + 1) if r < G - 1 else (1 - gp, 0)
                    if j == 1 and left >= 1:
                        pe.wait_ge(row_placed[(r + 1) % 2].sem,
                                   row_placed[(r + 1) % 2].at(32 * half(g, gp, r, 1) + 32))
                    if j < 1 or left >= 1:
                        pe.wait_ge(exp_done.sem, exp_done.at(NBLK * b + j + 2))
                        for k in range(HB):
                            ins = score_t(tgp, tr, (j + 3) % NBLK, k)
                        ins.then_inc(scored_t.sem, 1)
                    if own and j == 2:
                        pe.wait_ge(normed.sem, normed.at(b))
                        if left >= 2:
                            pe.wait_ge(minus_ready.sem, minus_ready.at(b + 3))
                        turn_out(b)
                    sj, near = (j + 3) % NBLK, j < 1
                    sr = r + (2 if near else 3)
                    sgp, sr = (gp, sr) if sr < G else (1 - gp, sr - G)
                    more = left >= (2 if near else 3)
                    if more:
                        if r == 1 and j == 1:
                            pe.wait_ge(stacked[sgp].sem, stacked[sgp].at(NSTACK * pair(g, gp, 1) + NSTACK))
                        pe.wait_ge(maxed.sem, maxed.at(NBLK * (b + 2) + j + 2))
                        if own:
                            causal_part(sj)
                    if r == 0 and j == 0:
                        pe.wait_ge(v_ready.sem, v_ready.at(g + 1))
                    if j == 0:
                        pe.wait_ge(summed.sem, summed.at(b - 1))
                    pe.wait_ge(lo_made.sem, lo_made.at(NBLK * b + j + 1))
                    for k in range(HB):
                        if j == 1 and k == HB // 2 and left >= 2:
                            turn_max(b + 2, r)
                        if more:
                            ins = score(sgp, sr, sj, k)
                        done = weigh(gp, r, j, k)
                    if more:
                        ins.then_inc(scored.sem, 1)
                    done.then_inc(weighed.sem, 1)
                    if r == 0 and j == 0 and left >= G:
                        prep_v(g + 1, 1 - gp)
                    if own and j == 2:
                        project_out(b)
                    if r == 0 and j == 3 and left >= 2 * G:
                        prep_transpose(g + 2)
                    if r == 1 and j == 1 and left >= 2 * G - r:
                        prep_q(g + 2)
                    if r == 2 and j == 0 and left >= 2 * G - r:
                        prep_k(g + 2, gp, pair(g, gp, 2))

            pairs(nc.tensor, step)
            if own:
                pe.wait_ge(normed.sem, normed.at(B))
                turn_out(B)
                project_out(B)

        @block.scalar
        def _(act):
            def copy_hT(g):
                act.wait_ge(transposed.sem, transposed.at(g + 1))
                nc.scalar.activation(hT[:, :], psH[:, :], ACT.Copy).then_inc(hT_ready.sem, 1)

            def copy_v(g):
                act.wait_ge(v_done.sem, v_done.at(g + 1))
                act.wait_ge(v_ready.sem, v_ready.at(g))
                nc.scalar.activation(vf[:, :], psH[:, :], ACT.Copy).then_inc(v_taken.sem, 1)

            def part_v(g, gp, a):
                if a == 0:
                    act.wait_ge(v_taken.sem, v_taken.at(g + 1))
                    act.wait_ge(weighed.sem, weighed.at(NBLK * G * (g - 1)))
                else:
                    act.wait_ge(v_rest.sem, v_rest.at(2 * g + a))
                nc.scalar.activation(vp[:, gp, :, :, a, 0:DH], vf[:, :].rearrange("p (b h d) -> p b h d", b=G, h=H),
                                     ACT.Copy).then_inc(v_split.sem if a < 2 else v_ready.sem, 1)

            def high_qk(n, g, gp, nth_before):
                act.wait_ge(taken.sem, taken.at(2 * g + n + 1))
                act.wait_ge(hi_spilled[1 - gp].sem, hi_spilled[1 - gp].at(32 * nth_before + 32))
                nc.scalar.activation(parts[n][:, 0, :], full[n][:, :], ACT.Copy).then_inc(hi_ready.sem, 1)

            def mid_qk(n, g, gp, nth_before):
                act.wait_ge(rest_ready.sem, rest_ready.at(2 * g + n + 1))
                act.wait_ge(lo_spilled[1 - gp].sem, lo_spilled[1 - gp].at(32 * nth_before + 32))
                nc.scalar.activation(parts[n][:, 1, :], full[n][:, :], ACT.Copy).then_inc(mid_ready.sem, 1)

            act.wait_ge(s_ones, 4 if own else 3)
            for g in range(2):
                copy_hT(g)
                high_qk(0, g, g, -1 + g)
                high_qk(1, g, g, -1 + g)
                mid_qk(0, g, g, -1 + g)
                mid_qk(1, g, g, -1 + g)
                if own and g == 0:
                    copy_v(0)
            for a in range(VP):
                part_v(0, 0, a)

            def exponentials(n, j):
                act.wait_ge(scored_t.sem, scored_t.at(n + 1))
                act.wait_ge(lo_made.sem, lo_made.at(n - NBLK + 1))
                nc.scalar.activation(PT[:, j, :, :], psT[j % 2][:, :, :], ACT.Exp,
                                     scale=SCALE).then_inc(exp_done.sem, 1)

            def high(n, j):
                if own:
                    act.wait_ge(selected.sem, selected.at(n + 1))
                else:
                    act.wait_ge(exp_done.sem, exp_done.at(n + 1))
                act.wait_ge(weighed.sem, weighed.at(n - NBLK + 1))
                nc.scalar.activation(Ph[:, j, :, :], PT[:, j, :, :], ACT.Copy,
                                     scale=P_SCALE).then_inc(hi_made.sem, 1)

            def copy_out(b):
                act.wait_ge(out_turned.sem, out_turned.at(b + 1))
                act.wait_ge(out_projected.sem, out_projected.at(b))
                nc.scalar.activation(oT[:, :], psM[:, 128:256], ACT.Copy).then_inc(out_copied.sem, 1)

            for j in range(3):
                exponentials(j, j)
            for j in range(2):
                high(j, j)

            def step(g, gp, r, left):
                b = G * g + r
                for j in range(NBLK):
                    if j < 1 or left >= 1:
                        exponentials(NBLK * b + j + 3, (j + 3) % NBLK)
                    if own and j == 2:
                        copy_out(b)
                    if j < 2 or left >= 1:
                        high(NBLK * b + j + 2, (j + 2) % NBLK)
                    if own and r == 0 and j == 1 and left >= G:
                        copy_v(g + 1)
                    if r == 0 and j == 2 and left >= G:
                        part_v(g + 1, 1 - gp, 0)
                    if r == 1 and j in (0, 2) and left >= G - r:
                        part_v(g + 1, 1 - gp, 1 + j // 2)
                    if left >= 2 * G - r:
                        if r == 1 and j == 0:
                            copy_hT(g + 2)
                        if r == 1 and j == 3:
                            high_qk(0, g + 2, gp, pair(g, gp, 1))
                        if r == 2 and j == 2:
                            high_qk(1, g + 2, gp, pair(g, gp, 1))
                        if r == 2 and j == 3:
                            mid_qk(0, g + 2, gp, pair(g, gp, 1))
                        if r == 3 and j == 1:
                            mid_qk(1, g + 2, gp, pair(g, gp, 1))

            pairs(nc.scalar, step)
            if own:
                copy_out(B)

        @block.gpsimd
        def _(pool):
            def rest(n, g):
                pool.wait_ge(hi_ready.sem, hi_ready.at(2 * g + n + 1))
                pool.sem_inc(passed, 1)
                nc.gpsimd.tensor_tensor(full[n][:, :], full[n][:, :], parts[n][:, 0, :],
                                        ALU.subtract).then_inc(rest_ready.sem, 1)

            def low(n, g):
                pool.wait_ge(mid_ready.sem, mid_ready.at(2 * g + n + 1))
                pool.sem_inc(passed, 1)
                nc.gpsimd.tensor_tensor(parts[n][:, 2, :], full[n][:, :], parts[n][:, 1, :],
                                        ALU.subtract).then_inc(lo_ready.sem, 1)

            def root(g):
                pool.wait_ge(stats_ready.sem, stats_ready.at(g + 1))
                pool.sem_inc(passed, 1)
                nc.gpsimd.tensor_scalar(veps[:, :], mv[:, :, 1], EPS, None, ALU.add).then_inc(own_pool.sem, 1)
                pool.wait_ge(own_pool.sem, own_pool.at(g + 2))
                pool.sem_inc(passed, 1)
                nc.gpsimd.tensor_tensor(rstd[:, :], veps[:, :], half_neg[:, :], ALU.pow).then_inc(rstd_ready.sem, 1)

            def select(n, j):
                pool.wait_ge(exp_done.sem, exp_done.at(n + 1))
                pool.sem_inc(passed, 1)
                nc.gpsimd.affine_select(out=PT[:, j, :, :], in_=PT[:, j, :, :], compare_op=ALU.is_ge,
                                        fill=0.0, base=0, pattern=[[0, HB], [1, 128]],
                                        channel_multiplier=-1).then_inc(selected.sem, 1)

            def rest_v(g, gp, a):
                pool.wait_ge(v_split.sem, v_split.at(2 * g + a + 1))
                pool.sem_inc(passed, 1)
                nc.gpsimd.tensor_tensor(vf[:, :].rearrange("p (b h d) -> p b h d", b=G, h=H),
                                        vf[:, :].rearrange("p (b h d) -> p b h d", b=G, h=H),
                                        vp[:, gp, :, :, a, 0:DH], ALU.subtract).then_inc(v_rest.sem, 1)

            def finish(b, r):
                pool.wait_ge(inverted.sem, inverted.at(b + 1))
                rd = rden[:, 0, :]
                if own:
                    pool.wait_ge(out_turned.sem, out_turned.at(b + 1))
                    pool.sem_inc(passed, 1)
                else:
                    pool.sem_inc(passed, 1)
                    nc.gpsimd.tensor_tensor(rden[:, 1, :], rden[:, 0, :], qm[:, H * (r % 2):H * (r % 2) + H],
                                            ALU.mult).then_inc(query_masked.sem, 1)
                    rd = rden[:, 1, :]
                    pool.wait_ge(query_masked.sem, query_masked.at(b + 1))
                    pool.wait_ge(added.sem, added.at(b))
                    pool.sem_inc(passed, 1)
                nc.gpsimd.tensor_tensor(O[:, :, :], osum[:, :, 0:DH], rd.unsqueeze(2).to_broadcast([128, H, DH]),
                                        ALU.mult).then_inc(normed.sem, 1)
                if not own:
                    pool.wait_ge(normed.sem, normed.at(b + 1))
                    pool.sem_inc(passed, 1)
                    out = O[:, :, :].rearrange("p h d -> p (h d)")
                    nc.gpsimd.tensor_tensor(X[:, at(b), :], X[:, at(b), :],
                                            out.unsqueeze(1) if isinstance(b, Lin) else out,
                                            ALU.add).then_inc(added.sem, 1)

            nc.gpsimd.memset(half_neg[:, :], -0.5).then_inc(own_pool.sem, 1)
            root(0)
            root(1)
            for g in range(2):
                for n in range(2):
                    rest(n, g)
                for n in range(2):
                    low(n, g)
            for a in range(VP - 1):
                rest_v(0, 0, a)
            if own:
                for j in range(3):
                    select(j, j)

            def step(g, gp, r, left):
                b = G * g + r
                for j in range(NBLK):
                    if own and (j < 1 or left >= 1):
                        select(NBLK * b + j + 3, (j + 3) % NBLK)
                    if r == 0 and j == 1 and left >= 2 * G:
                        root(g + 2)
                    if r == 0 and j == 3 and left >= G:
                        rest_v(g + 1, 1 - gp, 0)
                    if r == 1 and j == 1 and left >= G - r:
                        rest_v(g + 1, 1 - gp, 1)
                    if left >= 2 * G - r:
                        if r == 1 and j == 3:
                            rest(0, g + 2)
                        if r == 2 and j == 2:
                            rest(1, g + 2)
                        if r == 3 and j == 0:
                            low(0, g + 2)
                        if r == 3 and j == 2:
                            low(1, g + 2)
                finish(b, r)

            for s in (normed,) + (() if own else (added,)):
                s.credit(nc.gpsimd)
            pairs(nc.gpsimd, step)

        @block.vector
        def _(dve):
            def row_stats(g):
                for r in range(G):
                    nc.vector.bn_stats(stats[:, r, :], X[:, at(G * g + r), :]).then_inc(own_dve.sem, own_dve.one())
                dve.wait_ge(own_dve.sem, own_dve.value())
                if isinstance(g, Lin):
                    dve.sem_inc(passed, 1)
                for r in range(G):
                    ins = nc.vector.bn_aggr(mv[:, r, :], stats[:, r, :])
                ins.then_inc(stats_ready.sem, 1)

            def apply_norm(g):
                dve.wait_ge(rstd_ready.sem, rstd_ready.at(g + 1))
                dve.wait_ge(transposed.sem, transposed.at(g))
                for r in range(G):
                    ins = nc.vector.tensor_scalar(hn[:, r, :], X[:, at(G * g + r), :], mv[:, r, 0:1],
                                                  rstd[:, r:r + 1], ALU.subtract, ALU.mult)
                ins.then_inc(ln_done.sem, 1)

            def take(n, g):
                if n == 0:
                    dve.wait_ge(q_done.sem, q_done.at(g + 1))
                else:
                    dve.wait_ge(k_done.sem, k_done.at(g + 1))
                dve.wait_ge(lo_ready.sem, lo_ready.at(2 * g - 1 + n))
                if own:
                    ins = nc.vector.tensor_tensor(full[n][:, :], psH[:, :], pos[:, :], ALU.add)
                elif n == 0:
                    ins = nc.vector.tensor_scalar(full[n][:, :], psH[:, :], bqk[:, 0:1], None, ALU.add)
                else:
                    ins = nc.vector.scalar_tensor_tensor(out=full[n][:, :], in0=psH[:, :], scalar=bqk[:, 1:2],
                                                         in1=km[:, :, :].rearrange("p a t -> p (a t)"),
                                                         op0=ALU.add, op1=ALU.mult)
                ins.then_inc(taken.sem, 1)

            def take_v(g):
                dve.wait_ge(v_done.sem, v_done.at(g + 1))
                dve.wait_ge(v_ready.sem, v_ready.at(g))
                nc.vector.tensor_tensor(vf[:, :].rearrange("p (b c) -> p b c", b=G),
                                        psH[:, :].rearrange("p (b c) -> p b c", b=G),
                                        bv[:, :].unsqueeze(1).to_broadcast([128, G, 128]),
                                        ALU.add).then_inc(v_taken.sem, 1)

            def row_max(b, r, j):
                dve.wait_ge(scored.sem, scored.at(NBLK * b + j + 1))
                nc.vector.tensor_reduce(mx[:, r % 2, HB * j:HB * j + HB], psS[j % 2][:, :, :], AX.X,
                                        ALU.max).then_inc(maxed.sem, 1)

            def minus_max(b, r, nth):
                dve.wait_ge(max_turned.sem, max_turned.at(b + 1))
                dve.wait_ge(row_placed[r % 2].sem, row_placed[r % 2].at(32 * nth))
                nc.vector.tensor_scalar(negm[:, r % 2, 0, :], psM[0:H, 0:128], -1.0, None,
                                        ALU.mult).then_inc(negated.sem, 1)
                dve.wait_ge(negated.sem, negated.at(b + 1))
                nc.vector.scalar_tensor_tensor(out=negm[:, r % 2, 1, :], in0=psM[0:H, 0:128], scalar=-1.0,
                                               in1=negm[:, r % 2, 0, :], op0=ALU.mult,
                                               op1=ALU.subtract).then_inc(minus_ready.sem, 1)

            def low_part(n, j):
                dve.wait_ge(hi_made.sem, hi_made.at(n + 1))
                nc.vector.scalar_tensor_tensor(out=Pl[:, j, :, :], in0=PT[:, j, :, :], scalar=P_SCALE,
                                               in1=Ph[:, j, :, :], op0=ALU.mult,
                                               op1=ALU.subtract).then_inc(lo_made.sem, 1)

            def sum_parts(b, r):
                dve.wait_ge(weighed.sem, weighed.at(NBLK * (b + 1)))
                dve.wait_ge(normed.sem, normed.at(b))
                nc.vector.tensor_reduce(osum[:, :, :], outs[r % 2].rearrange("p h (a d) -> p h d a", a=VP), AX.X,
                                        ALU.add).then_inc(summed.sem, 1)
                dve.wait_ge(summed.sem, summed.at(b + 1))
                nc.vector.reciprocal(rden[:, 0, :], osum[:, :, DH]).then_inc(inverted.sem, 1)

            def add(b):
                dve.wait_ge(out_projected.sem, out_projected.at(b + 1))
                src, place = psM[:, 256:384], X_before[:, at(b), :]
                nc.vector.tensor_tensor(place, place, src.unsqueeze(1) if isinstance(b, Lin) else src,
                                        ALU.add).then_inc(added.sem, 1)

            if own:
                nc.vector.memset(O[:, :, :], 0.0).then_inc(s_ones, 1)
                nc.vector.memset(X_before[:, 0, :], 0.0)
            nc.vector.memset(ones[:, :], 1.0).then_inc(s_ones, 1)
            nc.vector.memset(vp[:, :, :, :, 0, DH:DH + 1], 1.0).then_inc(s_ones, 1)
            nc.vector.memset(vp[:, :, :, :, 1:VP, DH:DH + 1], 0.0).then_inc(s_ones, 1)
            if first:
                dve.wait_ge(s_x[0], 16)
            if own:
                dve.wait_ge(s_cst, 16)
                nc.vector.tensor_copy(cmask[:, :, :], causal[:, :].unsqueeze(1).to_broadcast([128, HB, 128])
                                      ).then_inc(s_neg, 1)
            else:
                dve.wait_ge(s_cst, 16 * 9)
                nc.vector.tensor_copy(qm[:, :], qmi[:, :]).then_inc(own_dve.sem, own_dve.one())
                nc.vector.tensor_copy(kmf[:, :, :], kmi[:, :, :]).then_inc(own_dve.sem, own_dve.one())
                dve.wait_ge(own_dve.sem, own_dve.value())
                for r in range(G):
                    nc.vector.tensor_scalar(km[:, r, :], kmf[:, r % 2, :], 0.0, None, ALU.not_equal).then_inc(
                        own_dve.sem, own_dve.one())
                nc.vector.tensor_scalar(negrow[:, :, :], kmf[0:H, :, :], 0.0, NEG, ALU.is_equal,
                                        ALU.mult).then_inc(s_neg, 1)
            row_stats(0)
            apply_norm(0)
            row_stats(1)
            dve.wait_ge(s_w, 16 * NW)
            take(0, 0)
            apply_norm(1)
            take(1, 0)
            if not own:
                take_v(0)
            take(0, 1)
            take(1, 1)
            if first:
                dve.wait_ge(s_x[1], 16)
            for n in range(NBLK * 2 + 1):
                row_max(n // NBLK, n // NBLK, n % NBLK)
                if n in (NBLK, 2 * NBLK):
                    minus_max(n // NBLK - 1, n // NBLK - 1, 0)
            for s in (summed, lo_made) + ((added,) if own else ()):
                s.credit(nc.vector)
            for j in range(2):
                low_part(j, j)
                row_max(2, 2, j + 1)

            def step(g, gp, r, left):
                b = G * g + r
                ahead = left >= 2
                for j in range(NBLK):
                    if own and j == 3:
                        add(b)
                    if j < 1 and ahead:
                        row_max(b + 2, r, 3)
                    if j == 1 and ahead:
                        minus_max(b + 2, r, half(g, gp, r) + 1)
                    if j >= 1 and left >= 3:
                        row_max(b + 3, r + 1, j - 1)
                    if j < 2 or left >= 1:
                        low_part(NBLK * b + j + 2, (j + 2) % NBLK)
                    if j == 3:
                        sum_parts(b, r)
                    if left >= 2 * G - r:
                        if r == 0 and j == 0:
                            row_stats(g + 2)
                        if r == 0 and j == 2:
                            apply_norm(g + 2)
                        if r == 1 and j == 2:
                            take(0, g + 2)
                        if r == 2 and j == 1:
                            take(1, g + 2)
                    if not own and r == 0 and j == 1 and left >= G:
                        take_v(g + 1)

            pairs(nc.vector, step, own_dve, 2 * G)
            if own:
                add(B)


def scope(nc, prefix):
    ctx, used = ExitStack(), []
    ctx.push(clear(nc, used))

    def sb(name, shape, dt=F32):
        return ctx.enter_context(nc.sbuf_tensor(prefix + name, shape, dt))

    def ps(name, shape, dt=F32):
        return ctx.enter_context(nc.psum_tensor(prefix + name, shape, dt))

    def sem(name):
        s = ctx.enter_context(nc.semaphore(prefix + name))
        used.append(s.num)
        return s

    def signal(name, free=0):
        return Signal(sem(name), free)

    return ctx, sb, ps, sem, signal


def groups(eng, step, tally=None, per=0, pairs=NG // 2):
    with eng.Fori(0, pairs - 1) as i:
        if tally:
            tally.enter(i, per)
        for gp in range(2):
            step(Lin(i, 2, gp), gp, 2)
    if tally:
        tally.leave(pairs - 1)
    for gp in range(2):
        step(2 * pairs - 2 + gp, gp, 1 - gp)


def parity_count(g, gp, more=0):
    n = (gp + more) // 2 + 1
    return Lin(g.i, 1, n) if isinstance(g, Lin) else (g - gp) // 2 + n


def span(n, width):
    return bass.ds((n * width).value(), width) if isinstance(n, Lin) else slice(n * width, (n + 1) * width)


class RowNorm:

    def __init__(self, nc, X, sb, signal, own_dve, passed, rows=G):
        self.passed = passed
        self.nc, self.X, self.own, self.rows = nc, X, own_dve, rows
        self.stats = sb("stats", [128, 2, rows, 6])
        self.mv = sb("mv", [128, 2, rows, 2])
        self.veps = sb("veps", [128, 2, rows])
        self.power = sb("power", [128, rows])
        self.rstd = sb("rstd", [128, 2, rows])
        self.stats_ready = signal("stats_ready")
        self.eps_added = signal("eps_added")
        self.rstd_ready = signal("rstd_ready")
        self.done = signal("ln_done")

    def start(self, pool):
        self.nc.gpsimd.memset(self.power[:, :], -0.5).then_inc(self.eps_added.sem, 1)

    def take_stats(self, dve, g, gp=0):
        nc = self.nc
        for r in range(self.rows):
            nc.vector.bn_stats(self.stats[:, gp, r, :], self.X[:, at(self.rows * g + r), :]).then_inc(
                self.own.sem, self.own.one())
        dve.wait_ge(self.own.sem, self.own.value())
        if isinstance(g, Lin):
            dve.sem_inc(self.passed, 1)
        for r in range(self.rows):
            ins = nc.vector.bn_aggr(self.mv[:, gp, r, :], self.stats[:, gp, r, :])
        ins.then_inc(self.stats_ready.sem, 1)

    def root(self, pool, g, gp=0):
        nc = self.nc
        pool.wait_ge(self.stats_ready.sem, self.stats_ready.at(g + 1))
        pool.sem_inc(self.passed, 1)
        nc.gpsimd.tensor_scalar(self.veps[:, gp, :], self.mv[:, gp, :, 1], EPS, None, ALU.add).then_inc(
            self.eps_added.sem, 1)
        pool.wait_ge(self.eps_added.sem, self.eps_added.at(g + 2))
        pool.sem_inc(self.passed, 1)
        nc.gpsimd.tensor_tensor(self.rstd[:, gp, :], self.veps[:, gp, :], self.power[:, :],
                                ALU.pow).then_inc(self.rstd_ready.sem, 1)

    def apply(self, dve, g, hn, gp=0):
        nc = self.nc
        dve.wait_ge(self.rstd_ready.sem, self.rstd_ready.at(g + 1))
        for r in range(self.rows):
            ins = nc.vector.tensor_scalar(hn[:, r, :], self.X[:, at(self.rows * g + r), :], self.mv[:, gp, r, 0:1],
                                          self.rstd[:, gp, r:r + 1], ALU.subtract, ALU.mult)
        ins.then_inc(self.done.sem, 1)


E1, HID, CAP = 8, 512, 20
NJ = HID // 128
HALF = E1 // 2 * CAP


def experts_routed(nc, X, io, consts):
    ident, passed = consts["ident"], consts["passed"]
    ctx, sb, ps, sem, signal = scope(nc, "r_")
    with ctx:
        XG = sb("XG", [128, E1, B, CAP])

        with ExitStack() as inner:
            ctx2, sb, ps, sem, signal = scope(nc, "ra_")
            inner.enter_context(ctx2)
            wr, br, before = sb("wr", [128, E1]), sb("br", [128, E1]), sb("before", [128, 128], BF16)
            beforef = sb("beforef", [128, 128])
            iota8, iota20 = sb("iota8", [128, E1]), sb("iota20", [128, CAP])
            hn, hT = sb("hn", [128, 2, G, 128]), sb("hT", [128, GT])
            lg, mx8 = sb("lg", [128, G, E1]), sb("mx8", [128, G, E1])
            ix8, ixf = sb("ix8", [128, G, E1], U32), sb("ixf", [128, G, 2])
            oh0, oh, ohb = sb("oh0", [128, G, E1]), sb("oh", [128, G, E1]), sb("ohb", [128, G, E1], BF16)
            oh1 = sb("oh1", [128, G, E1])
            dl, ex, sm, rs = sb("dl", [128, G, E1]), sb("ex", [128, G, E1]), sb("sm", [128, G]), sb("rs", [128, G])
            gw, qp = sb("gw", [128, G, E1]), sb("qp", [128, G, E1])
            D, Dw = sb("D", [128, 2, G, E1, CAP]), sb("Dw", [128, 2, G, E1, CAP])
            dwt = sb("dwt", [HALF, 2, G, 2, 128])
            psH, psL, psN = ps("psH", [128, GT]), ps("psL", [128, G, E1]), ps("psN", [128, G, E1])
            psX = [ps(f"psX{n}", [128, 2, E1 * CAP]) for n in range(2)]
            psD = [ps(f"psD{n}", [128, 2, 2, 128]) for n in range(2)]
            own_dve = Tally(sem("own_dve"))
            norm = RowNorm(nc, X, sb, signal, own_dve, passed)
            s_w, s_before = sem("loads"), sem("before")
            turned, hT_ready = signal("turned"), signal("hT_ready")
            logits, biased, shifted, exped = (signal(n) for n in ("logits", "biased", "shifted", "exped"))
            chosen, counted = signal("chosen"), signal("counted")
            d_ready, dw_ready = signal("d_ready"), signal("dw_ready")
            gathered, stored_x = signal("gathered", 4), signal("stored_x", 2)
            dw_turned, dw_copied = signal("dw_turned", 4), signal("dw_copied", 2)
            dw_saved = [signal(f"dw_saved{n}", 16) for n in range(2)]
            block = inner.enter_context(nc.Block())

            @block.sync
            def _(sp):
                for t, name in ((wr, "wr"), (beforef, "before")):
                    sp.dma_start(t[:, :], io[name]).then_inc(s_w, 16)
                for t, name in ((br, "br"), (iota8, "iota8"), (iota20, "iota20")):
                    sp.dma_start(t[:, :], io[name].partition_broadcast(128)).then_inc(s_w, 16)
                for s in dw_saved:
                    s.credit(nc.sync)

                def step(g, gp, more):
                    sp.wait_ge(dw_copied.sem, dw_copied.at(2 * g + 2))
                    sp.sem_inc(passed, 1)
                    dst = io["dwt"][at(g)]
                    sp.dma_start(dst.squeeze(0) if isinstance(g, Lin) else dst,
                                 dwt[:, gp, :, :, :].rearrange("p a b c -> p (a b c)")).then_inc(dw_saved[gp].sem, 16)
                groups(nc.sync, step)
                for s in dw_saved:
                    sp.wait_ge(s.sem, s.at(16 * (NG // 2)))
                    sp.sem_inc(passed, 1)

            @block.tensor
            def _(pe):
                def front(g, gp):
                    pe.wait_ge(norm.done.sem, norm.done.at(g + 1))
                    pe.wait_ge(hT_ready.sem, hT_ready.at(g))
                    for r in range(G):
                        ins = nc.tensor.transpose(psH[:, r * 128:(r + 1) * 128], hn[:, gp, r, :], ident[:, :])
                    ins.then_inc(turned.sem, 1)

                def logits_of(g):
                    pe.wait_ge(hT_ready.sem, hT_ready.at(g + 1))
                    pe.wait_ge(biased.sem, biased.at(g))
                    for r in range(G):
                        ins = nc.tensor.matmul(psL[:, r, :], hT[:, r * T:(r + 1) * T], wr[:, :], start=True,
                                               stop=True, skip_group_check=True)
                    ins.then_inc(logits.sem, 1)

                def count(g):
                    pe.wait_ge(chosen.sem, chosen.at(g + 1))
                    pe.wait_ge(d_ready.sem, d_ready.at(g))
                    nc.tensor.matmul(psN[:, :, :], before[:, :], ohb[:, :, :], start=True,
                                     stop=True).then_inc(counted.sem, 1)

                for s in (gathered, dw_turned):
                    s.credit(nc.tensor)
                pe.wait_ge(s_w, 16 * 5)
                pe.wait_ge(s_before, 1)
                front(0, 0)
                logits_of(0)
                front(1, 1)
                count(0)

                def step(g, gp, more):
                    if more:
                        logits_of(g + 1)
                    pe.wait_ge(d_ready.sem, d_ready.at(g + 1))
                    for n in range(2):
                        pe.wait_ge(stored_x.sem, stored_x.at(2 * g + n - 1))
                        for k in range(2):
                            r = 2 * n + k
                            ins = nc.tensor.matmul(psX[n][:, k, :], hn[:, gp, r, :],
                                                   D[:, gp, r, :, :].rearrange("p e c -> p (e c)"),
                                                   start=True, stop=True, skip_group_check=True)
                        ins.then_inc(gathered.sem, 1)
                    if more:
                        count(g + 1)
                    pe.wait_ge(dw_ready.sem, dw_ready.at(g + 1))
                    for n in range(2):
                        pe.wait_ge(dw_copied.sem, dw_copied.at(2 * g + n - 1))
                        for k in range(2):
                            for f in range(2):
                                ins = nc.tensor.transpose(
                                    psD[n][0:HALF, k, f, :],
                                    Dw[:, gp, 2 * n + k, 4 * f:4 * f + 4, :].rearrange("p e c -> p (e c)"), ident[:, :])
                        ins.then_inc(dw_turned.sem, 1)
                    if more == 2:
                        front(g + 2, gp)
                groups(nc.tensor, step)

            @block.scalar
            def _(act):
                def front(g):
                    act.wait_ge(turned.sem, turned.at(g + 1))
                    act.wait_ge(logits.sem, logits.at(g))
                    nc.scalar.activation(hT[:, :], psH[:, :], ACT.Copy).then_inc(hT_ready.sem, 1)

                def exponentials(g):
                    act.wait_ge(shifted.sem, shifted.at(g + 1))
                    nc.scalar.activation(ex[:, :, :], dl[:, :, :], ACT.Exp).then_inc(exped.sem, 1)

                stored_x.credit(nc.scalar)
                front(0)
                front(1)
                exponentials(0)

                def step(g, gp, more):
                    for n in range(2):
                        act.wait_ge(gathered.sem, gathered.at(2 * g + n + 1))
                        act.sem_inc(passed, 1)
                        b0 = g * G + 2 * n
                        for k in range(2):
                            dst = XG[:, :, at(b0 + k), :]
                            src = psX[n][:, k, :].rearrange("p (e c) -> p e c", e=E1)
                            if isinstance(g, Lin):
                                src = src.unsqueeze(2)
                            ins = nc.scalar.activation(dst, src, ACT.Copy)
                        ins.then_inc(stored_x.sem, 1)
                    if more:
                        exponentials(g + 1)
                    if more == 2:
                        front(g + 2)
                groups(nc.scalar, step)

            @block.gpsimd
            def _(pool):
                norm.start(pool)
                norm.root(pool, 0)
                norm.root(pool, 1)

                def step(g, gp, more):
                    if more == 2:
                        norm.root(pool, g + 2)
                groups(nc.gpsimd, step)

            @block.vector
            def _(dve):
                def wide(t):
                    return t[:, :].unsqueeze(1).to_broadcast([128, G, E1])

                def each(t):
                    return t.to_broadcast([128, G, E1])

                def copy_dw(g, gp):
                    for n in range(2):
                        dve.wait_ge(dw_turned.sem, dw_turned.at(2 * g + n + 1))
                        if n == 0:
                            dve.wait_ge(dw_saved[gp].sem, dw_saved[gp].at(16 * (parity_count(g, gp) - 1)))
                        nc.vector.tensor_copy(dwt[:, gp, 2 * n:2 * n + 2, :, :],
                                              psD[n][0:HALF, :, :, :]).then_inc(dw_copied.sem, 1)

                dve.wait_ge(s_w, 16 * 5)
                nc.vector.tensor_copy(before[:, :], beforef[:, :]).then_inc(s_before, 1)
                def route(g):
                    dve.wait_ge(logits.sem, logits.at(g + 1))
                    nc.vector.tensor_tensor(lg[:, :, :], psL[:, :, :], wide(br), ALU.add).then_inc(biased.sem, 1)
                    dve.wait_ge(biased.sem, biased.at(g + 1))
                    dve.sem_inc(passed, 1)
                    for r in range(G):
                        nc.vector.max(out=mx8[:, r, :], in_=lg[:, r, :]).then_inc(own_dve.sem, own_dve.one())
                    dve.wait_ge(own_dve.sem, own_dve.value())
                    if isinstance(g, Lin):
                        dve.sem_inc(passed, 1)
                    for r in range(G):
                        nc.vector.max_index(ix8[:, r, :], mx8[:, r, :], lg[:, r, :]).then_inc(
                            own_dve.sem, own_dve.one())
                    nc.vector.tensor_tensor(dl[:, :, :], lg[:, :, :], each(mx8[:, :, 0:1]),
                                            ALU.subtract).then_inc(shifted.sem, 1)
                    dve.wait_ge(own_dve.sem, own_dve.value())
                    nc.vector.tensor_copy(ixf[:, :, :], ix8[:, :, 0:2]).then_inc(own_dve.sem, own_dve.one())
                    dve.wait_ge(own_dve.sem, own_dve.value())
                    nc.vector.tensor_tensor(oh0[:, :, :], wide(iota8), each(ixf[:, :, 0:1]), ALU.is_equal).then_inc(
                        own_dve.sem, own_dve.one())
                    nc.vector.tensor_tensor(oh1[:, :, :], wide(iota8), each(ixf[:, :, 1:2]), ALU.is_equal).then_inc(
                        own_dve.sem, own_dve.one())
                    dve.wait_ge(own_dve.sem, own_dve.value())
                    nc.vector.tensor_tensor(oh[:, :, :], oh0[:, :, :], oh1[:, :, :], ALU.add).then_inc(
                        own_dve.sem, own_dve.one())
                    dve.wait_ge(own_dve.sem, own_dve.value())
                    nc.vector.tensor_copy(ohb[:, :, :], oh[:, :, :]).then_inc(chosen.sem, 1)

                def place(g, gp):
                    dve.wait_ge(exped.sem, exped.at(g + 1))
                    nc.vector.tensor_reduce(sm[:, :], ex[:, :, :], AX.X, ALU.add).then_inc(own_dve.sem, own_dve.one())
                    dve.wait_ge(own_dve.sem, own_dve.value())
                    nc.vector.reciprocal(rs[:, :], sm[:, :]).then_inc(own_dve.sem, own_dve.one())
                    dve.wait_ge(own_dve.sem, own_dve.value())
                    nc.vector.tensor_tensor(gw[:, :, :], ex[:, :, :], each(rs[:, :].unsqueeze(2)), ALU.mult).then_inc(
                        own_dve.sem, own_dve.one())
                    dve.wait_ge(own_dve.sem, own_dve.value())
                    nc.vector.tensor_tensor(gw[:, :, :], gw[:, :, :], oh[:, :, :], ALU.mult).then_inc(
                        own_dve.sem, own_dve.one())
                    dve.wait_ge(own_dve.sem, own_dve.value())
                    dve.wait_ge(counted.sem, counted.at(g + 1))
                    nc.vector.scalar_tensor_tensor(out=qp[:, :, :], in0=psN[:, :, :], scalar=1.0,
                                                        in1=oh[:, :, :], op0=ALU.add, op1=ALU.mult).then_inc(
                                                            own_dve.sem, own_dve.one())
                    dve.wait_ge(own_dve.sem, own_dve.value())
                    dve.wait_ge(gathered.sem, gathered.at(2 * g - 2))
                    slots = iota20[:, :].unsqueeze(1).to_broadcast([128, G * E1, CAP])
                    nc.vector.tensor_tensor(D[:, gp, :, :, :].rearrange("p a e c -> p (a e) c"), slots,
                                            qp[:, :, :].rearrange("p a e -> p (a e)").unsqueeze(2)
                                            .to_broadcast([128, G * E1, CAP]), ALU.is_equal).then_inc(d_ready.sem, 1)
                    dve.wait_ge(d_ready.sem, d_ready.at(g + 1))
                    dve.wait_ge(dw_turned.sem, dw_turned.at(2 * g - 2))
                    nc.vector.tensor_tensor(Dw[:, gp, :, :, :].rearrange("p a e c -> p (a e) c"),
                                            D[:, gp, :, :, :].rearrange("p a e c -> p (a e) c"),
                                            gw[:, :, :].rearrange("p a e -> p (a e)").unsqueeze(2)
                                            .to_broadcast([128, G * E1, CAP]), ALU.mult).then_inc(dw_ready.sem, 1)

                dw_copied.credit(nc.vector)
                norm.take_stats(dve, 0)
                norm.apply(dve, 0, hn[:, 0, :, :])
                route(0)
                norm.take_stats(dve, 1)
                norm.apply(dve, 1, hn[:, 1, :, :])
                place(0, 0)

                def step(g, gp, more):
                    if more == 2:
                        norm.take_stats(dve, g + 2)
                    if more:
                        route(g + 1)
                    if more == 2:
                        dve.wait_ge(gathered.sem, gathered.at(2 * g + 2))
                        norm.apply(dve, g + 2, hn[:, gp, :, :])
                    if more:
                        place(g + 1, 1 - gp)
                    copy_dw(g, gp)
                groups(nc.vector, step, own_dve, 2 * (G + G + 4 + 4 + 1 + G))

        with ExitStack() as inner:
            ctx2, sb, ps, sem, signal = scope(nc, "rb_")
            inner.enter_context(ctx2)
            N2 = B // 2 * CAP
            w1, w2 = sb("w1", [128, 2, HID]), sb("w2", [128, 2, NJ, 128])
            b1, b2 = sb("b1", [128, E1 * NJ]), sb("b2", [128, E1])
            hid = sb("hid", [128, 2, NJ, N2])
            psF = [ps(f"psF{n}", [128, 512]) for n in range(NJ)]
            psY = [ps(f"psY{n}", [128, 512]) for n in range(2)]
            s_b = sem("biases")
            w_ready = [signal(f"w_ready{n}") for n in range(2)]
            first_done, relu_done = signal("first", 4), signal("relu", 4)
            second_done, y_taken = signal("second", 2), signal("y_taken", 2)
            block = inner.enter_context(nc.Block())

            @block.sync
            def _(sp):
                sp.dma_start(b1[:, :], io["b1T"]).then_inc(s_b, 16)
                sp.dma_start(b2[:, :], io["b2T"]).then_inc(s_b, 16)

                def load(e, gp):
                    a1, a2 = io["w1"][at(e)], io["w2"][at(e)]
                    if isinstance(e, Lin):
                        a1, a2 = a1.squeeze(0), a2.squeeze(0)
                    sp.dma_start(w1[:, gp, :], a1).then_inc(w_ready[gp].sem, 16)
                    sp.dma_start(w2[:, gp, :, :], a2.rearrange("(j p) c -> p j c", p=128)).then_inc(w_ready[gp].sem, 16)

                load(0, 0)

                def step(e, gp, more):
                    sp.wait_ge(second_done.sem, second_done.at(2 * e))
                    sp.sem_inc(passed, 1)
                    if more:
                        load(e + 1, 1 - gp)
                groups(nc.sync, step, pairs=E1 // 2)

            @block.tensor
            def _(pe):
                for s in (first_done, second_done):
                    s.credit(nc.tensor)

                def step(e, gp, more):
                    pe.wait_ge(w_ready[gp].sem, w_ready[gp].at(32 * parity_count(e, gp)))
                    for q in range(2):
                        n = 2 * e + q
                        for j in range(NJ):
                            pe.wait_ge(relu_done.sem, relu_done.at(NJ * n + j - 3))
                            rhs = XG[:, at(e), q * B // 2:(q + 1) * B // 2, :]
                            rhs = rhs.rearrange("p a b c -> p (a b c)") if isinstance(e, Lin) \
                                else rhs.rearrange("p b c -> p (b c)")
                            nc.tensor.matmul(psF[j][:, 0:N2], w1[:, gp, j * 128:(j + 1) * 128], rhs,
                                             start=True, stop=True).then_inc(first_done.sem, 1)
                        pe.wait_ge(y_taken.sem, y_taken.at(n - 1))
                        for j in range(NJ):
                            pe.wait_ge(relu_done.sem, relu_done.at(NJ * n + j + 1))
                            ins = nc.tensor.matmul(psY[q][:, 0:N2], w2[:, gp, j, :], hid[:, q, j, :],
                                                   start=(j == 0), stop=(j == NJ - 1))
                        ins.then_inc(second_done.sem, 1)
                groups(nc.tensor, step, pairs=E1 // 2)

            @block.scalar
            def _(act):
                act.wait_ge(s_b, 32)
                relu_done.credit(nc.scalar)

                def step(e, gp, more):
                    for q in range(2):
                        n = 2 * e + q
                        for j in range(NJ):
                            act.wait_ge(first_done.sem, first_done.at(NJ * n + j + 1))
                            if j == 0:
                                act.wait_ge(second_done.sem, second_done.at(n - 1))
                            act.sem_inc(passed, 1)
                            nc.scalar.activation(hid[:, q, j, :], psF[j][:, 0:N2], ACT.Relu,
                                                 bias=b1[:, at1(NJ * e + j)]).then_inc(relu_done.sem, 1)
                groups(nc.scalar, step, pairs=E1 // 2)

            @block.vector
            def _(dve):
                dve.wait_ge(s_b, 32)
                y_taken.credit(nc.vector)

                def step(e, gp, more):
                    for q in range(2):
                        n = 2 * e + q
                        dve.wait_ge(second_done.sem, second_done.at(n + 1))
                        dst = XG[:, at(e), q * B // 2:(q + 1) * B // 2, :]
                        dst = dst.rearrange("p a b c -> p (a b c)") if isinstance(e, Lin) \
                            else dst.rearrange("p b c -> p (b c)")
                        nc.vector.tensor_scalar(dst, psY[q][:, 0:N2], b2[:, at1(e)], None,
                                                ALU.add).then_inc(y_taken.sem, 1)
                groups(nc.vector, step, pairs=E1 // 2)

        with ExitStack() as inner:
            ctx2, sb, ps, sem, signal = scope(nc, "rc_")
            inner.enter_context(ctx2)
            dwt = sb("dwt", [HALF, 2, G, 2, 128])
            ys = sb("ys", [128, 2, G, E1, CAP])
            yv = sb("yv", [HALF, 2, G, 2, 128])
            psV = [ps(f"psV{n}", [128, 2, 2, 128]) for n in range(4)]
            psO = [ps(f"psO{n}", [128, G, 128]) for n in range(2)]
            loaded = [signal(f"loaded{n}") for n in range(2)]
            staged = signal("staged")
            turned, copied = signal("turned", 4), signal("copied", 4)
            mixed, added = signal("mixed", 2), signal("added", 2)
            block = inner.enter_context(nc.Block())

            @block.sync
            def _(sp):
                def load(g, gp):
                    src = io["dwt"][at(g)]
                    sp.dma_start(dwt[:, gp, :, :, :].rearrange("p a b c -> p (a b c)"),
                                 src.squeeze(0) if isinstance(g, Lin) else src).then_inc(loaded[gp].sem, 16)
                load(0, 0)

                def step(g, gp, more):
                    sp.wait_ge(mixed.sem, mixed.at(g))
                    sp.sem_inc(passed, 1)
                    if more:
                        load(g + 1, 1 - gp)
                groups(nc.sync, step)

            @block.gpsimd
            def _(pool):
                def step(g, gp, more):
                    pool.wait_ge(turned.sem, turned.at(2 * g - 2))
                    pool.sem_inc(passed, 1)
                    src = XG[:, :, span(g, G), :].rearrange("p e b c -> p b e c")
                    nc.gpsimd.tensor_copy(ys[:, gp, :, :, :], src).then_inc(staged.sem, 1)
                groups(nc.gpsimd, step)

            @block.tensor
            def _(pe):
                def front(g, gp):
                    pe.wait_ge(staged.sem, staged.at(g + 1))
                    for n in range(2):
                        pe.wait_ge(copied.sem, copied.at(2 * g + n - 3))
                        for k in range(2):
                            for f in range(2):
                                ins = nc.tensor.transpose(
                                    psV[2 * gp + n][0:HALF, k, f, :],
                                    ys[:, gp, 2 * n + k, 4 * f:4 * f + 4, :].rearrange("p e c -> p (e c)"), ident[:, :])
                        ins.then_inc(turned.sem, 1)

                for s in (turned, mixed):
                    s.credit(nc.tensor)
                front(0, 0)

                def step(g, gp, more):
                    if more:
                        front(g + 1, 1 - gp)
                    pe.wait_ge(copied.sem, copied.at(2 * g + 2))
                    pe.wait_ge(loaded[gp].sem, loaded[gp].at(16 * parity_count(g, gp)))
                    pe.wait_ge(added.sem, added.at(g - 1))
                    for r in range(G):
                        for f in range(2):
                            ins = nc.tensor.matmul(psO[gp][:, r, :], dwt[:, gp, r, f, :], yv[:, gp, r, f, :],
                                                   start=(f == 0), stop=(f == 1), skip_group_check=True)
                    ins.then_inc(mixed.sem, 1)
                groups(nc.tensor, step)

            @block.scalar
            def _(act):
                copied.credit(nc.scalar)

                def step(g, gp, more):
                    act.wait_ge(mixed.sem, mixed.at(g - 1))
                    for n in range(2):
                        act.wait_ge(turned.sem, turned.at(2 * g + n + 1))
                        nc.scalar.activation(yv[:, gp, 2 * n:2 * n + 2, :, :], psV[2 * gp + n][0:HALF, :, :, :],
                                             ACT.Copy).then_inc(copied.sem, 1)
                groups(nc.scalar, step)

            @block.vector
            def _(dve):
                added.credit(nc.vector)

                def step(g, gp, more):
                    dve.wait_ge(mixed.sem, mixed.at(g + 1))
                    nc.vector.tensor_tensor(X[:, span(g, G), :], X[:, span(g, G), :], psO[gp][:, :, :],
                                            ALU.add).then_inc(added.sem, 1)
                groups(nc.vector, step)


def at1(n):
    return bass.ds(n.value(), 1) if isinstance(n, Lin) else slice(n, n + 1)


def sequence_attention(nc, X, io, consts):
    ident, passed = consts["ident"], consts["passed"]
    PL = 4
    BLK = 4
    SC = C ** -0.5
    with ExitStack() as outer:
        ctx0, sb, ps, sem, signal = scope(nc, "s_")
        outer.enter_context(ctx0)
        HT = sb("HT", [128, B, T])
        GTt = sb("GTt", [128, B, T])

        with ExitStack() as inner:
            ctx1, sb, ps, sem, signal = scope(nc, "sa_")
            inner.enter_context(ctx1)
            wq, wk, gm = sb("wq", [128, 128]), sb("wk", [128, 128]), sb("gm", [128, 128])
            hn, hT = sb("hn", [128, 2, G, 128]), sb("hT", [128, 2, GT])
            psH = [ps(f"psH{n}", [128, GT]) for n in range(2)]
            psG = [ps(f"psG{n}", [128, GT]) for n in range(2)]
            psW = ps("psW", [128, 128])
            own_dve = Tally(sem("own_dve"))
            norm = RowNorm(nc, X, sb, signal, own_dve, passed)
            s_w, s_gm = sem("loads"), sem("gm")
            turned, hT_ready = signal("turned", 1), signal("hT_ready", 2)
            projected, kept = signal("projected", 2), signal("kept", 2)
            block = inner.enter_context(nc.Block())

            @block.sync
            def _(sp):
                sp.dma_start(wq[:, :], io["s_wq"]).then_inc(s_w, 16)
                sp.dma_start(wk[:, :], io["s_wk"]).then_inc(s_w, 16)

            @block.gpsimd
            def _(pool):
                norm.start(pool)
                norm.root(pool, 0, 0)
                norm.root(pool, 1, 1)

                def step(g, gp, more):
                    if more == 2:
                        norm.root(pool, g + 2, gp)
                    pool.wait_ge(hT_ready.sem, hT_ready.at(g + 1))
                    pool.sem_inc(passed, 1)
                    src = hT[:, gp, :].rearrange("p (b t) -> p b t", b=G)
                    nc.gpsimd.tensor_copy(HT[:, span(g, G), :], src).then_inc(kept.sem, 1)
                kept.credit(nc.gpsimd)
                groups(nc.gpsimd, step)

            @block.vector
            def _(dve):
                norm.take_stats(dve, 0, 0)
                norm.take_stats(dve, 1, 1)
                norm.apply(dve, 0, hn[:, 0, :, :], 0)
                dve.wait_ge(s_gm, 1)
                nc.vector.tensor_copy(gm[:, :], psW[:, :]).then_inc(s_gm, 1)

                def step(g, gp, more):
                    if more == 2:
                        norm.take_stats(dve, g + 2, gp)
                    if more:
                        dve.wait_ge(turned.sem, turned.at(g))
                        norm.apply(dve, g + 1, hn[:, 1 - gp, :, :], 1 - gp)
                groups(nc.vector, step, own_dve, 2 * G)

            @block.tensor
            def _(pe):
                pe.wait_ge(s_w, 32)
                nc.tensor.matmul(psW[:, :], wq[:, :], wk[:, :], start=True, stop=True).then_inc(s_gm, 1)
                pe.wait_ge(s_gm, 2)
                for s in (turned, projected):
                    s.credit(nc.tensor)

                def front(g, gp):
                    pe.wait_ge(norm.done.sem, norm.done.at(g + 1))
                    pe.wait_ge(hT_ready.sem, hT_ready.at(g - 1))
                    for r in range(G):
                        ins = nc.tensor.transpose(psH[gp][:, r * 128:(r + 1) * 128], hn[:, gp, r, :], ident[:, :])
                    ins.then_inc(turned.sem, 1)
                front(0, 0)

                def step(g, gp, more):
                    if more:
                        front(g + 1, 1 - gp)
                    pe.wait_ge(hT_ready.sem, hT_ready.at(g + 1))
                    nc.tensor.matmul(psG[gp][:, :], gm[:, :], hT[:, gp, :], start=True,
                                     stop=True).then_inc(projected.sem, 1)
                groups(nc.tensor, step)

            @block.scalar
            def _(act):
                def front(g, gp):
                    act.wait_ge(turned.sem, turned.at(g + 1))
                    act.wait_ge(projected.sem, projected.at(g - 1))
                    act.wait_ge(kept.sem, kept.at(g - 1))
                    nc.scalar.activation(hT[:, gp, :], psH[gp][:, :], ACT.Copy).then_inc(hT_ready.sem, 1)

                def keep(g, gp):
                    act.wait_ge(projected.sem, projected.at(g + 1))
                    act.sem_inc(passed, 1)
                    src = psG[gp][:, :].rearrange("p (b t) -> p b t", b=G)
                    nc.scalar.activation(GTt[:, span(g, G), :], src, ACT.Copy)
                hT_ready.credit(nc.scalar)
                front(0, 0)

                def step(g, gp, more):
                    keep(g, gp)
                    if more:
                        front(g + 1, 1 - gp)
                groups(nc.scalar, step)

        with ExitStack() as inner:
            ctx1, sb, ps, sem, signal = scope(nc, "sb_")
            inner.enter_context(ctx1)
            mask = sb("mask", [128, 128])
            hs, hv = sb("hs", [128, 2, BLK, 128]), sb("hv", [128, 2, BLK, 129])
            th, ex, em = sb("th", [128, BLK, 128]), sb("ex", [128, BLK, 128]), sb("em", [128, 2, BLK, 128])
            rd, on = sb("rd", [128, BLK]), sb("on", [128, 2, BLK, 128])
            psV, psS = ps("psV", [128, BLK, 128]), ps("psS", [128, BLK, 128])
            psO = [[ps(f"psO{m}{n}", [128, 2, 256]) for n in range(2)] for m in range(2)]
            psT = ps("psT", [128, BLK, 128])
            own_dve = Tally(sem("own_dve"))
            s_w, s_one = sem("loads"), sem("ones")
            staged, turned, hv_ready = signal("staged"), signal("turned", 2), signal("hv_ready", 1)
            scored, tanh_done, exp_done = signal("scored", 2), signal("tanh", 1), signal("exp", 1)
            masked, weighed, normed = signal("masked", 1), signal("weighed", 3), signal("normed", 1)
            back, back_done = signal("back", 2), signal("back_done", 1)
            block = inner.enter_context(nc.Block())

            def places(t, g):
                w = BLK * PL
                return t[:, :, span(g, w)].rearrange("p b (k q) -> p k b q", q=PL)

            @block.sync
            def _(sp):
                sp.dma_start(mask[:, :], io["same_place"]).then_inc(s_w, 16)

            @block.gpsimd
            def _(pool):
                pool.wait_ge(s_w, 16)
                def step(g, gp, more):
                    pool.wait_ge(scored.sem, scored.at(g - 1))
                    pool.sem_inc(passed, 1)
                    nc.gpsimd.tensor_copy(hs[:, gp, :, :].rearrange("p k (b q) -> p k b q", q=PL),
                                          places(HT, g)).then_inc(staged.sem, 1)
                groups(nc.gpsimd, step)

            @block.tensor
            def _(pe):
                for s in (turned, scored, weighed, back):
                    s.credit(nc.tensor)

                def front(g, gp):
                    pe.wait_ge(staged.sem, staged.at(g + 1))
                    pe.wait_ge(hv_ready.sem, hv_ready.at(g))
                    for k in range(BLK):
                        ins = nc.tensor.transpose(psV[:, k, :], hs[:, gp, k, :], ident[:, :])
                    ins.then_inc(turned.sem, 1)
                    pe.wait_ge(tanh_done.sem, tanh_done.at(g))
                    for k in range(BLK):
                        gt = GTt[:, :, span_at(g, BLK * PL, k * PL, PL)]
                        ins = nc.tensor.matmul(psS[:, k, :].rearrange("p (b q) -> p b q", q=PL), hs[:, gp, k, :], gt,
                                               start=True, stop=True, skip_group_check=True)
                    ins.then_inc(scored.sem, 1)

                def weigh(g, gp):
                    pe.wait_ge(masked.sem, masked.at(g + 1))
                    pe.wait_ge(hv_ready.sem, hv_ready.at(g + 1))
                    pe.wait_ge(normed.sem, normed.at(g - 1))
                    for k in range(BLK):
                        ins = nc.tensor.matmul(psO[gp][k // 2][:, k % 2, 0:129], em[:, gp, k, :], hv[:, gp, k, :],
                                               start=True, stop=True, skip_group_check=True)
                    ins.then_inc(weighed.sem, 1)

                front(0, 0)
                front(1, 1)
                pe.wait_ge(s_one, 1)
                weigh(0, 0)

                def step(g, gp, more):
                    if more == 2:
                        front(g + 2, gp)
                    if more:
                        weigh(g + 1, 1 - gp)
                    pe.wait_ge(normed.sem, normed.at(g + 1))
                    pe.wait_ge(back_done.sem, back_done.at(g))
                    for k in range(BLK):
                        ins = nc.tensor.transpose(psT[:, k, :], on[:, gp, k, :], ident[:, :])
                    ins.then_inc(back.sem, 1)
                groups(nc.tensor, step)

            @block.scalar
            def _(act):
                for s in (hv_ready, tanh_done, exp_done, back_done):
                    s.credit(nc.scalar)

                def front(g, gp):
                    act.wait_ge(turned.sem, turned.at(g + 1))
                    act.wait_ge(weighed.sem, weighed.at(g - 1))
                    nc.scalar.activation(hv[:, gp, :, 0:128], psV[:, :, :], ACT.Copy).then_inc(hv_ready.sem, 1)
                    act.wait_ge(scored.sem, scored.at(g + 1))
                    act.wait_ge(exp_done.sem, exp_done.at(g))
                    nc.scalar.activation(th[:, :, :], psS[:, :, :], ACT.Tanh, scale=SC).then_inc(tanh_done.sem, 1)
                    act.wait_ge(tanh_done.sem, tanh_done.at(g + 1))
                    act.wait_ge(masked.sem, masked.at(g))
                    nc.scalar.activation(ex[:, :, :], th[:, :, :], ACT.Exp).then_inc(exp_done.sem, 1)
                front(0, 0)
                front(1, 1)

                def step(g, gp, more):
                    if more == 2:
                        front(g + 2, gp)
                    act.wait_ge(back.sem, back.at(g + 1))
                    act.sem_inc(passed, 1)
                    nc.scalar.activation(places(HT, g), psT[:, :, :].rearrange("p k (b q) -> p k b q", q=PL),
                                         ACT.Copy).then_inc(back_done.sem, 1)
                groups(nc.scalar, step)

            @block.vector
            def _(dve):
                nc.vector.memset(hv[:, :, :, 128:129], 1.0).then_inc(s_one, 1)
                dve.wait_ge(s_w, 16)
                for s in (masked, normed):
                    s.credit(nc.vector)

                def front(g, gp):
                    dve.wait_ge(exp_done.sem, exp_done.at(g + 1))
                    dve.wait_ge(weighed.sem, weighed.at(g - 1))
                    nc.vector.tensor_tensor(em[:, gp, :, :], ex[:, :, :],
                                            mask[:, :].unsqueeze(1).to_broadcast([128, BLK, 128]),
                                            ALU.mult).then_inc(masked.sem, 1)
                def normalise(g, gp):
                    dve.wait_ge(weighed.sem, weighed.at(g + 1))
                    dve.wait_ge(normed.sem, normed.at(g))
                    for n in range(2):
                        nc.vector.reciprocal(rd[:, 2 * n:2 * n + 2], psO[gp][n][:, :, 128]).then_inc(
                            own_dve.sem, own_dve.one())
                    dve.wait_ge(own_dve.sem, own_dve.value())
                    dve.wait_ge(back.sem, back.at(g - 1))
                    for k in range(BLK):
                        ins = nc.vector.tensor_scalar(on[:, gp, k, :], psO[gp][k // 2][:, k % 2, 0:128],
                                                      rd[:, k:k + 1], None, ALU.mult)
                    ins.then_inc(normed.sem, 1)

                front(0, 0)
                front(1, 1)
                normalise(0, 0)

                def step(g, gp, more):
                    if more == 2:
                        front(g + 2, gp)
                    if more:
                        normalise(g + 1, 1 - gp)
                groups(nc.vector, step, own_dve, 2 * 2)

        with ExitStack() as inner:
            ctx1, sb, ps, sem, signal = scope(nc, "sc_")
            inner.enter_context(ctx1)
            os_ = sb("os", [128, 2, G, 128])
            psB = [ps(f"psB{n}", [128, G, 128]) for n in range(2)]
            staged, turned, added = signal("staged"), signal("turned", 2), signal("added", 2)
            block = inner.enter_context(nc.Block())

            @block.gpsimd
            def _(pool):
                def step(g, gp, more):
                    pool.wait_ge(turned.sem, turned.at(g - 1))
                    pool.sem_inc(passed, 1)
                    nc.gpsimd.tensor_copy(os_[:, gp, :, :], HT[:, span(g, G), :]).then_inc(staged.sem, 1)
                groups(nc.gpsimd, step)

            @block.tensor
            def _(pe):
                turned.credit(nc.tensor)

                def step(g, gp, more):
                    pe.wait_ge(staged.sem, staged.at(g + 1))
                    pe.wait_ge(added.sem, added.at(g - 1))
                    for r in range(G):
                        ins = nc.tensor.transpose(psB[gp][:, r, :], os_[:, gp, r, :], ident[:, :])
                    ins.then_inc(turned.sem, 1)
                groups(nc.tensor, step)

            @block.vector
            def _(dve):
                added.credit(nc.vector)

                def step(g, gp, more):
                    dve.wait_ge(turned.sem, turned.at(g + 1))
                    nc.vector.tensor_tensor(X[:, span(g, G), :], X[:, span(g, G), :], psB[gp][:, :, :],
                                            ALU.add).then_inc(added.sem, 1)
                groups(nc.vector, step)


def span_at(n, width, offset, size):
    return bass.ds((n * width + offset).value(), size) if isinstance(n, Lin) \
        else slice(n * width + offset, n * width + offset + size)


def context_attention(nc, X, io, consts):
    ident, passed = consts["ident"], consts["passed"]
    SC = C ** -0.5
    ctx, sb, ps, sem, signal = scope(nc, "x_")
    with ctx:
        wq, wk, wv, gm = (sb(n, [128, 128]) for n in ("wq", "wk", "wv", "gm"))
        hn, hT, gT = sb("hn", [128, 2, G, 128]), sb("hT", [128, GT]), sb("gT", [128, GT])
        cT = sb("cT", [128, 2, GT])
        vv = sb("vv", [128, 2, G, 128])
        mx, nm, sm, rs = sb("mx", [128, G]), sb("nm", [128, 2, G]), sb("sm", [128, 2, G]), sb("rs", [128, G])
        P, PT = sb("P", [128, G, 128]), sb("PT", [128, G, 128])
        psH, psG, psV = (ps(n, [128, GT]) for n in ("psH", "psG", "psV"))
        psS = [ps(f"psS{n}", [128, GT]) for n in range(2)]
        psP, psO = ps("psP", [128, GT]), ps("psO", [128, GT])
        own_dve = Tally(sem("own_dve"))
        norm = RowNorm(nc, X, sb, signal, own_dve, passed)
        s_w, s_gm = sem("loads"), sem("gm")
        c_ready = [signal(f"ctx{n}") for n in range(2)]
        turned, hT_ready = signal("turned"), signal("hT_ready")
        projected, gT_ready = signal("projected"), signal("gT_ready")
        v_done, v_ready = signal("v_done"), signal("v_ready")
        scored, maxed, exped = signal("scored"), signal("maxed"), signal("exp", 1)
        p_turned, p_copied = signal("p_turned"), signal("p_copied", 1)
        weighed, added = signal("weighed", 1), signal("added", 1)
        block = ctx.enter_context(nc.Block())

        @block.sync
        def _(sp):
            for t, name in ((wq, "x_wq"), (wk, "x_wk"), (wv, "x_wv")):
                sp.dma_start(t[:, :], io[name]).then_inc(s_w, 16)

            def load(g, gp):
                sp.dma_start(cT[:, gp, :], io["ctxT"][:, span(g, GT)]).then_inc(c_ready[gp].sem, 16)
            load(0, 0)
            load(1, 1)

            def step(g, gp, more):
                if more == 2:
                    sp.wait_ge(scored.sem, scored.at(g + 1))
                    sp.wait_ge(v_done.sem, v_done.at(g + 1))
                    sp.sem_inc(passed, 1)
                    load(g + 2, gp)
            groups(nc.sync, step)

        @block.gpsimd
        def _(pool):
            norm.start(pool)
            norm.root(pool, 0)
            norm.root(pool, 1)

            def step(g, gp, more):
                if more == 2:
                    norm.root(pool, g + 2)
            groups(nc.gpsimd, step)

        @block.tensor
        def _(pe):
            def turn(g, gp):
                pe.wait_ge(norm.done.sem, norm.done.at(g + 1))
                pe.wait_ge(hT_ready.sem, hT_ready.at(g))
                for r in range(G):
                    ins = nc.tensor.transpose(psH[:, r * 128:(r + 1) * 128], hn[:, gp, r, :], ident[:, :])
                ins.then_inc(turned.sem, 1)

            def project(g):
                pe.wait_ge(hT_ready.sem, hT_ready.at(g + 1))
                pe.wait_ge(gT_ready.sem, gT_ready.at(g))
                nc.tensor.matmul(psG[:, :], gm[:, :], hT[:, :], start=True, stop=True).then_inc(projected.sem, 1)

            def score(g, gp, nth):
                pe.wait_ge(c_ready[gp].sem, c_ready[gp].at(16 * nth))
                pe.wait_ge(gT_ready.sem, gT_ready.at(g + 1))
                pe.wait_ge(exped.sem, exped.at(g - 1))
                for r in range(G):
                    ins = nc.tensor.matmul(psS[gp][:, r * 128:(r + 1) * 128], gT[:, r * T:(r + 1) * T],
                                           cT[:, gp, r * T:(r + 1) * T], start=True, stop=True, skip_group_check=True)
                ins.then_inc(scored.sem, 1)

            def values(g, gp):
                pe.wait_ge(v_ready.sem, v_ready.at(g))
                for r in range(G):
                    ins = nc.tensor.matmul(psV[:, r * 128:(r + 1) * 128], cT[:, gp, r * T:(r + 1) * T], wv[:, :],
                                           start=True, stop=True, skip_group_check=True)
                ins.then_inc(v_done.sem, 1)

            weighed.credit(nc.tensor)
            pe.wait_ge(s_w, 16 * 3)
            nc.tensor.matmul(psG[:, 0:128], wq[:, :], wk[:, :], start=True, stop=True).then_inc(s_gm, 1)
            turn(0, 0)
            pe.wait_ge(s_gm, 2)
            project(0)
            turn(1, 1)
            score(0, 0, 1)
            values(0, 0)

            def step(g, gp, more):
                if more:
                    project(g + 1)
                pe.wait_ge(exped.sem, exped.at(g + 1))
                pe.wait_ge(p_copied.sem, p_copied.at(g))
                for r in range(G):
                    ins = nc.tensor.transpose(psP[:, r * 128:(r + 1) * 128], P[:, r, :], ident[:, :])
                ins.then_inc(p_turned.sem, 1)
                if more:
                    score(g + 1, 1 - gp, parity_count(g, gp, 1))
                    values(g + 1, 1 - gp)
                if more == 2:
                    turn(g + 2, gp)
                pe.wait_ge(p_copied.sem, p_copied.at(g + 1))
                pe.wait_ge(v_ready.sem, v_ready.at(g + 1))
                pe.wait_ge(added.sem, added.at(g))
                for r in range(G):
                    ins = nc.tensor.matmul(psO[:, r * 128:(r + 1) * 128], PT[:, r, :], vv[:, gp, r, :],
                                           start=True, stop=True, skip_group_check=True)
                ins.then_inc(weighed.sem, 1)
            groups(nc.tensor, step)

        @block.scalar
        def _(act):
            def copy_hT(g):
                act.wait_ge(turned.sem, turned.at(g + 1))
                act.wait_ge(projected.sem, projected.at(g))
                nc.scalar.activation(hT[:, :], psH[:, :], ACT.Copy).then_inc(hT_ready.sem, 1)

            def copy_values(g, gp):
                act.wait_ge(v_done.sem, v_done.at(g + 1))
                act.wait_ge(weighed.sem, weighed.at(g - 1))
                nc.scalar.activation(vv[:, gp, :, :].rearrange("p r c -> p (r c)"), psV[:, :],
                                     ACT.Copy).then_inc(v_ready.sem, 1)

            def exponentials(g, gp):
                act.wait_ge(maxed.sem, maxed.at(g + 1))
                act.wait_ge(p_turned.sem, p_turned.at(g))
                act.wait_ge(added.sem, added.at(g - 1))
                for r in range(G):
                    ins = nc.scalar.activation(P[:, r, :], psS[gp][:, r * 128:(r + 1) * 128], ACT.Exp,
                                               bias=nm[:, gp, r:r + 1], scale=SC, accum_out=sm[:, gp, r:r + 1])
                ins.then_inc(exped.sem, 1)

            for s in (exped, p_copied):
                s.credit(nc.scalar)
            copy_hT(0)
            copy_hT(1)
            exponentials(0, 0)
            copy_values(0, 0)

            def step(g, gp, more):
                act.wait_ge(p_turned.sem, p_turned.at(g + 1))
                act.wait_ge(weighed.sem, weighed.at(g))
                nc.scalar.activation(PT[:, :, :].rearrange("p r c -> p (r c)"), psP[:, :],
                                     ACT.Copy).then_inc(p_copied.sem, 1)
                if more:
                    exponentials(g + 1, 1 - gp)
                    copy_values(g + 1, 1 - gp)
                if more == 2:
                    copy_hT(g + 2)
            groups(nc.scalar, step)

        @block.vector
        def _(dve):
            def copy_gT(g):
                dve.wait_ge(projected.sem, projected.at(g + 1))
                dve.wait_ge(scored.sem, scored.at(g))
                nc.vector.tensor_copy(gT[:, :], psG[:, :]).then_inc(gT_ready.sem, 1)

            def row_max(g, gp):
                dve.wait_ge(scored.sem, scored.at(g + 1))
                nc.vector.tensor_reduce(mx[:, :], psS[gp][:, :].rearrange("p (r k) -> p r k", r=G),
                                        AX.X, ALU.max).then_inc(own_dve.sem, own_dve.one())
                dve.wait_ge(own_dve.sem, own_dve.value())
                dve.wait_ge(exped.sem, exped.at(g - 1))
                nc.vector.tensor_scalar(nm[:, gp, :], mx[:, :], -SC, None, ALU.mult).then_inc(maxed.sem, 1)

            added.credit(nc.vector)
            norm.take_stats(dve, 0)
            norm.apply(dve, 0, hn[:, 0, :, :])
            dve.wait_ge(s_gm, 1)
            nc.vector.tensor_copy(gm[:, :], psG[:, 0:128]).then_inc(s_gm, 1)
            norm.take_stats(dve, 1)
            norm.apply(dve, 1, hn[:, 1, :, :])
            copy_gT(0)
            row_max(0, 0)

            def step(g, gp, more):
                if more:
                    copy_gT(g + 1)
                if more == 2:
                    norm.take_stats(dve, g + 2)
                if more:
                    row_max(g + 1, 1 - gp)
                if more == 2:
                    dve.wait_ge(turned.sem, turned.at(g + 1))
                    norm.apply(dve, g + 2, hn[:, gp, :, :])
                dve.wait_ge(exped.sem, exped.at(g + 1))
                dve.wait_ge(added.sem, added.at(g))
                nc.vector.reciprocal(rs[:, :], sm[:, gp, :]).then_inc(own_dve.sem, own_dve.one())
                dve.wait_ge(own_dve.sem, own_dve.value())
                dve.wait_ge(weighed.sem, weighed.at(g + 1))
                for r in range(G):
                    xb = X[:, at(G * g + r), :]
                    ins = nc.vector.scalar_tensor_tensor(
                        out=xb, in0=psO[:, r * 128:(r + 1) * 128].unsqueeze(1) if isinstance(g, Lin)
                        else psO[:, r * 128:(r + 1) * 128],
                        scalar=rs[:, r:r + 1], in1=xb, op0=ALU.mult, op1=ALU.add)
                ins.then_inc(added.sem, 1)
            groups(nc.vector, step, own_dve, 2 * (G + 2))


def experts_chosen(nc, X, io, consts):
    passed = consts["passed"]
    N, SL = io["cw"].shape[0], io["idx"].shape[0]
    NT, NA = N // 128, SL // 128
    ctx, sb, ps, sem, signal = scope(nc, "e_")
    with ctx:
        w1, w2 = sb("w1", [128, 2, HID]), sb("w2", [128, 2, NJ, 128])
        b1, b2 = sb("b1", [128, E1 * NJ]), sb("b2", [128, E1, 128])
        cw = sb("cw", [128, NT, E1])
        cwr = sb("cwr", [128, NT, E1])
        cwp = sb("cwp", [128, NT, 3, E1], BF16)
        idi, idf = sb("idi", [128, NA, E1], I32), sb("idf", [128, E1, NA])
        idb = sb("idb", [128, E1, SL], I32)
        idc = sb("idc", [128, 2, NA])
        tokid, iotaN = sb("tokid", [128, NT]), sb("iotaN", [128, N])
        hn, hp = sb("hn", [128, NT, 128]), sb("hp", [128, NT, 3, 128], BF16)
        oh, ohT = sb("oh", [128, 2, NT, SL], BF16), sb("ohT", [128, 2, NA, N], BF16)
        xg, h1 = sb("xg", [128, SL]), sb("h1", [128, NJ, SL])
        ws, yw = sb("ws", [128, 2, NA]), sb("yw", [128, NA, 128])
        yp = sb("yp", [128, 3, NA, 128], BF16)
        psX, psW = ps("psX", [128, SL]), ps("psW", [128, NA, 3])
        psF = [ps(f"psF{n}", [128, 2, SL]) for n in range(2)]
        psY = ps("psY", [128, NA, 128])
        psA = [ps(f"psA{n}", [128, G, 128]) for n in range(2)]
        own_dve = Tally(sem("own_dve"))
        norm = RowNorm(nc, X, sb, signal, own_dve, passed)
        s_c = sem("loads")
        split, idc_ready = signal("split"), signal("idc_ready")
        w_ready = [signal(f"w_ready{n}") for n in range(2)]
        oh_ready, ohT_ready = signal("oh_ready"), signal("ohT_ready")
        gathered, xg_ready = signal("gathered"), signal("xg_ready")
        weights, gated = signal("weights"), signal("gated")
        first_done, gelu_done = signal("first"), signal("gelu")
        second_done, weighted = signal("second"), signal("weighted", 1)
        hi_done, rest_done, mid_done, lo_done = (signal(n) for n in ("hi", "rest", "mid", "lo"))
        scattered, added = signal("scattered", 3), signal("added", 2)
        block = ctx.enter_context(nc.Block())

        @block.sync
        def _(sp):
            sp.dma_start(idb[:, :, :].rearrange("p e s -> p (e s)"),
                         io["idxT"].rearrange("e s -> (e s)").partition_broadcast(128)).then_inc(s_c, 16)
            sp.dma_start(tokid[:, :], io["tokid"]).then_inc(s_c, 16)
            sp.dma_start(cw[:, :, :], io["cw"].rearrange("(n p) e -> p n e", p=128)).then_inc(s_c, 16)
            sp.dma_start(idi[:, :, :], io["idx"].rearrange("(a p) e -> p a e", p=128)).then_inc(s_c, 16)
            sp.dma_start(iotaN[:, :], io["iotaN"].partition_broadcast(128)).then_inc(s_c, 16)
            sp.dma_start(b1[:, :], io["eb1T"]).then_inc(s_c, 16)
            sp.dma_start(b2[:, :, :].rearrange("p e c -> p (e c)"),
                         io["eb2"].rearrange("e c -> (e c)").partition_broadcast(128)).then_inc(s_c, 16)

            def load(e, gp):
                a1, a2 = io["ew1"][at(e)], io["ew2"][at(e)]
                if isinstance(e, Lin):
                    a1, a2 = a1.squeeze(0), a2.squeeze(0)
                sp.dma_start(w1[:, gp, :], a1).then_inc(w_ready[gp].sem, 16)
                sp.dma_start(w2[:, gp, :, :], a2.rearrange("(j p) c -> p j c", p=128)).then_inc(w_ready[gp].sem, 16)
            load(0, 0)
            load(1, 1)

            def step(e, gp, more):
                if more == 2:
                    sp.wait_ge(second_done.sem, second_done.at(e + 1))
                    sp.sem_inc(passed, 1)
                    load(e + 2, gp)
            groups(nc.sync, step, pairs=E1 // 2)

        @block.tensor
        def _(pe):
            def gather(e, gp):
                pe.wait_ge(oh_ready.sem, oh_ready.at(e + 1))
                pe.wait_ge(xg_ready.sem, xg_ready.at(e))
                for n in range(NT):
                    for k in range(3):
                        ins = nc.tensor.matmul(psX[:, :], hp[:, n, k, :], oh[:, gp, n, :],
                                               start=(n == 0 and k == 0), stop=(n == NT - 1 and k == 2))
                ins.then_inc(gathered.sem, 1)

            def gate(e, gp):
                pe.wait_ge(gated.sem, gated.at(e))
                for a in range(NA):
                    for n in range(NT):
                        rhs = cwp[:, n, :, at(e)]
                        if isinstance(e, Lin):
                            rhs = rhs.rearrange("p a b -> p (a b)")
                        ins = nc.tensor.matmul(psW[:, a, :], oh[:, gp, n, a * 128:(a + 1) * 128], rhs,
                                               start=(n == 0), stop=(n == NT - 1), skip_group_check=True)
                ins.then_inc(weights.sem, 1)

            def first(e, gp, nth):
                pe.wait_ge(w_ready[gp].sem, w_ready[gp].at(32 * nth))
                pe.wait_ge(xg_ready.sem, xg_ready.at(e + 1))
                for j in range(NJ):
                    pe.wait_ge(gelu_done.sem, gelu_done.at(NJ * (e - 1) + j // 2 * 2 + 2))
                    nc.tensor.matmul(psF[j // 2][:, j % 2, :], w1[:, gp, j * 128:(j + 1) * 128], xg[:, :],
                                     start=True, stop=True, skip_group_check=True).then_inc(first_done.sem, 1)

            def second(e, gp):
                pe.wait_ge(weighted.sem, weighted.at(e))
                pe.wait_ge(gelu_done.sem, gelu_done.at(NJ * (e + 1)))
                for a in range(NA):
                    for j in range(NJ):
                        ins = nc.tensor.matmul(psY[:, a, :], h1[:, j, a * 128:(a + 1) * 128], w2[:, gp, j, :],
                                               start=(j == 0), stop=(j == NJ - 1), skip_group_check=True)
                ins.then_inc(second_done.sem, 1)

            def scatter(e, gp):
                pe.wait_ge(lo_done.sem, lo_done.at(e + 1))
                pe.wait_ge(ohT_ready.sem, ohT_ready.at(e + 1))
                for n in range(NT):
                    if n % G == 0:
                        pe.wait_ge(added.sem, added.at(2 * e + n // G - 1))
                    for a in range(NA):
                        for k in range(3):
                            ins = nc.tensor.matmul(psA[n // G][:, n % G, :], ohT[:, gp, a, n * 128:(n + 1) * 128],
                                                   yp[:, k, a, :], start=(a == 0 and k == 0),
                                                   stop=(a == NA - 1 and k == 2), skip_group_check=True)
                    if n % G == G - 1:
                        ins.then_inc(scattered.sem, 1)

            scattered.credit(nc.tensor)
            pe.wait_ge(split.sem, split.at(2))
            gather(0, 0)
            gate(0, 0)
            first(0, 0, 1)

            def step(e, gp, more):
                second(e, gp)
                if more:
                    gather(e + 1, 1 - gp)
                    gate(e + 1, 1 - gp)
                    first(e + 1, 1 - gp, parity_count(e, gp, 1))
                scatter(e, gp)
            groups(nc.tensor, step, pairs=E1 // 2)

        @block.scalar
        def _(act):
            act.wait_ge(s_c, 16 * 7)

            def copy_x(e):
                act.wait_ge(gathered.sem, gathered.at(e + 1))
                act.wait_ge(first_done.sem, first_done.at(NJ * e))
                nc.scalar.activation(xg[:, :], psX[:, :], ACT.Copy).then_inc(xg_ready.sem, 1)

            def activate(e):
                for j in range(NJ):
                    act.wait_ge(first_done.sem, first_done.at(NJ * e + j // 2 * 2 + 2))
                    if j == 0:
                        act.wait_ge(second_done.sem, second_done.at(e))
                    act.sem_inc(passed, 1)
                    nc.scalar.activation(h1[:, j, :], psF[j // 2][:, j % 2, :], ACT.Gelu_apprx_tanh,
                                         bias=b1[:, at1(NJ * e + j)]).then_inc(gelu_done.sem, 1)
            copy_x(0)
            activate(0)

            def step(e, gp, more):
                if more:
                    copy_x(e + 1)
                    activate(e + 1)
            groups(nc.scalar, step, pairs=E1 // 2)

        @block.gpsimd
        def _(pool):
            norm.start(pool)
            for g in range(2):
                norm.root(pool, g)
            pool.wait_ge(s_c, 16 * 7)
            pool.wait_ge(split.sem, split.at(3))
            pool.sem_inc(passed, 1)

            def step(e, gp, more):
                pool.wait_ge(scattered.sem, scattered.at(2 * e - 2))
                pool.sem_inc(passed, 1)
                nc.gpsimd.tensor_copy(idc[:, gp, :].unsqueeze(1) if isinstance(e, Lin) else idc[:, gp, :],
                                      idf[:, at(e), :]).then_inc(idc_ready.sem, 1)
                pool.wait_ge(idc_ready.sem, idc_ready.at(e + 1))
                pool.sem_inc(passed, 1)
                for a in range(NA):
                    ins = nc.gpsimd.tensor_scalar(ohT[:, gp, a, :], iotaN[:, :], idc[:, gp, a:a + 1], None,
                                                  ALU.is_equal)
                ins.then_inc(ohT_ready.sem, 1)
            groups(nc.gpsimd, step, pairs=E1 // 2)

        @block.vector
        def _(dve):
            for s in (weighted, added):
                s.credit(nc.vector)
            for g in range(2):
                norm.take_stats(dve, g)
                norm.apply(dve, g, hn[:, G * g:G * g + G, :])
            dve.wait_ge(norm.done.sem, norm.done.at(2))
            dve.wait_ge(s_c, 16 * 7)
            for full_, part, last in ((hn, [hp[:, :, k, :] for k in range(3)], split),
                                      (cw, [cwp[:, :, k, :] for k in range(3)], split)):
                nc.vector.tensor_copy(part[0], full_[:, :, :]).then_inc(own_dve.sem, own_dve.one())
                dve.wait_ge(own_dve.sem, own_dve.value())
                nc.vector.tensor_tensor(full_[:, :, :], full_[:, :, :], part[0], ALU.subtract).then_inc(
                    own_dve.sem, own_dve.one())
                dve.wait_ge(own_dve.sem, own_dve.value())
                nc.vector.tensor_copy(part[1], full_[:, :, :]).then_inc(own_dve.sem, own_dve.one())
                dve.wait_ge(own_dve.sem, own_dve.value())
                nc.vector.tensor_tensor(part[2], full_[:, :, :], part[1], ALU.subtract).then_inc(last.sem, 1)
            nc.vector.tensor_copy(idf[:, :, :].rearrange("p e a -> p a e"), idi[:, :, :]).then_inc(split.sem, 1)

            def mark_slots(e, gp):
                dve.wait_ge(weights.sem, weights.at(e - 1))
                for n in range(NT):
                    src = idb[:, at(e), :]
                    dst = oh[:, gp, n, :]
                    ins = nc.vector.tensor_scalar(dst.unsqueeze(1) if isinstance(e, Lin) else dst, src,
                                                  tokid[:, n:n + 1], None, ALU.is_equal)
                ins.then_inc(oh_ready.sem, 1)
            def take_gates(e, gp):
                dve.wait_ge(weights.sem, weights.at(e + 1))
                nc.vector.tensor_reduce(ws[:, gp, :], psW[:, :, :], AX.X, ALU.add).then_inc(gated.sem, 1)

            mark_slots(0, 0)
            mark_slots(1, 1)
            take_gates(0, 0)

            def step(e, gp, more):
                dve.wait_ge(second_done.sem, second_done.at(e + 1))
                bias = b2[:, at(e), :]
                bias = bias.to_broadcast([128, NA, 128]) if isinstance(e, Lin) \
                    else bias.unsqueeze(1).to_broadcast([128, NA, 128])
                nc.vector.tensor_tensor(yw[:, :, :], psY[:, :, :], bias, ALU.add).then_inc(own_dve.sem, own_dve.one())
                dve.wait_ge(own_dve.sem, own_dve.value())
                dve.wait_ge(gated.sem, gated.at(e + 1))
                nc.vector.tensor_tensor(yw[:, :, :], yw[:, :, :],
                                        ws[:, gp, :].unsqueeze(2).to_broadcast([128, NA, 128]),
                                        ALU.mult).then_inc(weighted.sem, 1)
                dve.wait_ge(weighted.sem, weighted.at(e + 1))
                dve.wait_ge(scattered.sem, scattered.at(2 * e))
                nc.vector.tensor_copy(yp[:, 0, :, :], yw[:, :, :]).then_inc(own_dve.sem, own_dve.one())
                dve.wait_ge(own_dve.sem, own_dve.value())
                nc.vector.tensor_tensor(yw[:, :, :], yw[:, :, :], yp[:, 0, :, :], ALU.subtract).then_inc(
                    own_dve.sem, own_dve.one())
                dve.wait_ge(own_dve.sem, own_dve.value())
                nc.vector.tensor_copy(yp[:, 1, :, :], yw[:, :, :]).then_inc(own_dve.sem, own_dve.one())
                dve.wait_ge(own_dve.sem, own_dve.value())
                nc.vector.tensor_tensor(yp[:, 2, :, :], yw[:, :, :], yp[:, 1, :, :],
                                        ALU.subtract).then_inc(lo_done.sem, 1)
                if more:
                    take_gates(e + 1, 1 - gp)
                if more == 2:
                    mark_slots(e + 2, gp)
                for n in range(2):
                    dve.wait_ge(scattered.sem, scattered.at(2 * e + n + 1))
                    nc.vector.tensor_tensor(X[:, G * n:G * n + G, :], X[:, G * n:G * n + G, :], psA[n][:, :, :],
                                            ALU.add).then_inc(added.sem, 1)
            groups(nc.vector, step, own_dve, 2 * 4, pairs=E1 // 2)




def more_arrays(a):
    place = np.arange(128) % 4
    idx, cw = a["L1_ffn_top_idx"], a["L1_ffn_combine_weights"]
    return {
        "wr": a["L0_ffn_Wr"], "br": a["L0_ffn_br"],
        "before": np.triu(np.ones((T, T), np.float32), 1),
        "iota8": np.arange(E1, dtype=np.float32), "iota20": np.arange(1, CAP + 1, dtype=np.float32),
        "w1": a["L0_ffn_W1"], "w2": a["L0_ffn_W2"],
        "b1T": a["L0_ffn_b1"].reshape(E1 * NJ, 128).T, "b2T": a["L0_ffn_b2"].T,
        "s_wq": a["L1_attn_Wq"], "s_wk": a["L1_attn_Wk"],
        "same_place": (place[:, None] == place[None, :]).astype(np.float32),
        "x_wq": a["L1_xattn_Wq"], "x_wk": a["L1_xattn_Wk"], "x_wv": a["L1_xattn_Wv"].T,
        "idx": idx, "idxT": idx.T, "cw": cw,
        "tokid": np.arange(cw.shape[0], dtype=np.float32).reshape(-1, 128).T,
        "iotaN": np.arange(cw.shape[0], dtype=np.float32),
        "ew1": a["L1_ffn_W1"], "ew2": a["L1_ffn_W2"],
        "eb1T": a["L1_ffn_b1"].reshape(E1 * NJ, 128).T, "eb2": a["L1_ffn_b2"],
    }


def setup(nc, consts, io):
    with ExitStack() as ctx:
        used = []
        ctx.push(clear(nc, used))
        loaded = ctx.enter_context(nc.semaphore("identities"))
        used.append(loaded.num)
        block = ctx.enter_context(nc.Block())

        @block.sync
        def _(sp):
            sp.dma_start(consts["ident"][:, :], io["ident"]).then_inc(loaded, 16)

        @block.vector
        def _(dve):
            dve.wait_ge(loaded, 16)
            nc.vector.tensor_copy(consts["identb"][:, :], consts["ident"][:, :])


def store(nc, X, out):
    with ExitStack() as ctx:
        stored = ctx.enter_context(nc.semaphore("stored"))
        block = ctx.enter_context(nc.Block())

        @block.sync
        def _(sp):
            sp.dma_start(out.rearrange("b t c -> t b c"), X[:, :, :]).then_inc(stored, 16)
            sp.wait_ge(stored, 16)


def build(nc, io, out):
    with ExitStack() as ctx:
        X_before = ctx.enter_context(nc.sbuf_tensor("X", [128, B + 1, C], F32))
        X = X_before[:, 1:B + 1, :]
        consts = {"ident": ctx.enter_context(nc.sbuf_tensor("ident", [128, 128], F32)),
                  "identb": ctx.enter_context(nc.sbuf_tensor("identb", [128, 128], BF16)),
                  "passed": ctx.enter_context(nc.semaphore("passed"))}
        setup(nc, consts, io)
        head_attention(nc, "self", X_before, io, consts, True)
        if STAGES >= 2:
            head_attention(nc, "cross", X_before, io, consts, False)
        if STAGES >= 3:
            experts_routed(nc, X, io, consts)
        if STAGES >= 4:
            sequence_attention(nc, X, io, consts)
        if STAGES >= 5:
            context_attention(nc, X, io, consts)
        if STAGES >= 6:
            experts_chosen(nc, X, io, consts)
        store(nc, X, out)


STAGES = 6


def kernel(**inputs):
    import concourse.bacc as bacc
    from concourse.bass_utils import run_bass_kernel_spmd as run

    a = {k: np.asarray(v) for k, v in inputs.items()}

    def heads_inner(w):
        return w.reshape(w.shape[:-1] + (H, DH)).swapaxes(-1, -2).reshape(w.shape)

    idx = np.arange(T, dtype=np.float32)
    eps = float(np.finfo(np.float32).eps)
    scale = (1.0 / (np.float32(10000.0) ** (np.arange(0, DH, 2, dtype=np.float32) / DH) + eps)).astype(np.float32)
    ang = idx[:, None] * scale[None, :]
    pos = np.stack([np.sin(ang), np.cos(ang)], axis=-1).reshape(T, DH).astype(np.float32)
    posT = np.tile(np.repeat(pos.T, H, axis=0), (1, G))
    causal = np.triu(np.full((T, T), CAUSAL_BIG, np.float32), 1)
    arrays = {
        "x": a["x"],
        "ident": np.eye(128, dtype=np.float32),
        "pos": posT,
        "causal": causal,
        "a_wq": heads_inner(a["L0_attn_Wq"]), "a_wk": heads_inner(a["L0_attn_Wk"]),
        "a_wv": a["L0_attn_Wv"], "a_wo": a["L0_attn_Wo"],
        "ctxT": a["ctx_1024"].transpose(2, 0, 1).reshape(C, B * T),
        "mask": a["mask_BxS2_ik0"], "maskT": a["mask_BxS2_ik0"].T,
        "c_wq": heads_inner(a["L0_xattn_Wq"].T), "c_wk": heads_inner(a["L0_xattn_Wk"].T), "c_wv": a["L0_xattn_Wv"].T,
        "bqk": np.stack([heads_inner(a["L0_xattn_bq"]), heads_inner(a["L0_xattn_bk"])], axis=1),
        "bv": a["L0_xattn_bv"],
    }
    arrays.update(more_arrays(a))
    nc = bacc.Bacc("TRN2", target_bir_lowering=False, num_devices=1)
    io = {}
    for name in list(arrays):
        arrays[name] = np.ascontiguousarray(arrays[name])
        io[name] = nc.dram_tensor(name + "_dram", arrays[name].shape, mybir.dt.from_np(arrays[name].dtype),
                                  kind="ExternalInput").ap()
    io["spill"] = nc.dram_tensor("spill_dram", [2, 2, 3, 128, GT], BF16, kind="Internal").ap()
    io["dwt"] = nc.dram_tensor("dwt_dram", [NG, E1 // 2 * CAP, G * 2 * 128], F32, kind="Internal").ap()
    out = nc.dram_tensor("out_dram", [B, T, C], F32, kind="ExternalOutput").ap()
    build(nc, io, out)
    r = run(nc, [{k + "_dram": v for k, v in arrays.items()}], core_ids=[0])
    return r.results[0]["out_dram"]
```
